# Optimizing a Trainium2 kernel written in Bass

```python
import numpy as np
import jax
import jax.numpy as jnp

def _softmax(x, axis=-1):
    return jax.nn.softmax(x, axis=axis)

def _gelu(x):
    return jax.nn.gelu(x, approximate=True)

def _silu(x):
    return jax.nn.silu(x)

def _sigmoid(x):
    return jax.nn.sigmoid(x)

def _layernorm(x, axis=-1, eps=1e-05):
    m = jnp.mean(x, axis=axis, keepdims=True)
    v = jnp.var(x, axis=axis, keepdims=True)
    return (x - m) / jnp.sqrt(v + eps)

def _scatter_add(tgt, idx, src, axis=0):
    return tgt.at[idx].add(src)

def _segment_sum(src, seg, n):
    return jax.ops.segment_sum(src, seg, n)
kernel_name = 'mk_xattn_ffn_d1_seqx_r8_01d8c2'

def setup_inputs(seed: int=0):
    np.random.seed(seed)
    _w = jnp.asarray

    def _rec_inputs():
        import jax
        import jax.numpy as jnp
        _rk = jax.random.key(seed)
        x = 0.0002417 + 0.9998 * jax.random.normal(jax.random.fold_in(_rk, 1), (1, 1024, 128), jnp.float32)
        _lenS = 1024 - jax.random.randint(jax.random.fold_in(_rk, 7), (1,), 0, max(1, 1024 // 4) + 1, jnp.int32)
        _lenS2 = 6404 - jax.random.randint(jax.random.fold_in(_rk, 8), (1,), 0, max(1, 6404 // 4) + 1, jnp.int32)
        _ctx_1024P = jax.random.normal(jax.random.fold_in(_rk, 11), (1, 16, 128), jnp.float32)
        _ctx_1024c = jax.random.dirichlet(jax.random.fold_in(_rk, 511), 0.3 * jnp.ones((16,), jnp.float32), (1, 6404))
        _ctx_1024t = jnp.einsum('bsk,bkd->bsd', _ctx_1024c, _ctx_1024P)
        _ctx_1024t = _ctx_1024t * jax.lax.rsqrt(jnp.mean(jnp.square(_ctx_1024t)) + 1e-12) * 0.953939
        ctx_1024 = 7.22013e-05 + 1.00017 * (_ctx_1024t + 0.3 * jax.random.normal(jax.random.fold_in(_rk, 611), (1, 6404, 128), jnp.float32))
        return (x, ctx_1024)
    x, ctx_1024 = _rec_inputs()

    def _L0_xattn_setup():
        import jax, jax.numpy as jnp
        import numpy as np
        D_MODEL = 128
        B, S = (4, 256)
        key = jax.random.key(seed)
        ks = jax.random.split(key, 10)
        s = 1.0 / np.sqrt(D_MODEL)
        return {'k': jax.random.normal(ks[0], (B, S, D_MODEL), jnp.float32), 'v': jax.random.normal(ks[1], (B, S, D_MODEL), jnp.float32), 'q': jax.random.normal(ks[2], (B, S, D_MODEL), jnp.float32), 'Wk': jax.random.normal(ks[3], (D_MODEL, D_MODEL), jnp.float32) * s, 'Wv': jax.random.normal(ks[4], (D_MODEL, D_MODEL), jnp.float32) * s, 'bv': jnp.zeros((D_MODEL,), jnp.float32), 'Wq': jax.random.normal(ks[5], (D_MODEL, D_MODEL), jnp.float32) * s, 'bq': jnp.zeros((D_MODEL,), jnp.float32), 'Wo': jax.random.normal(ks[6], (D_MODEL, D_MODEL), jnp.float32) * s, 'bo': jnp.zeros((D_MODEL,), jnp.float32)}
    _L0_xattn_all = _L0_xattn_setup()
    _L0_xattn_in = {k: v for k, v in _L0_xattn_all.items() if k in ('Wk', 'Wv', 'bv', 'Wq', 'bq', 'Wo', 'bo')}
    del _L0_xattn_all

    def _L0_ffn_setup():
        import jax, jax.numpy as jnp
        import numpy as np
        DIM = 128
        DEPTH = 2
        HEADS = 8
        DIM_HEAD = 64
        WINDOW = 64
        INNER = HEADS * DIM_HEAD
        HID = int(DIM * 4 * 2 / 3)
        B, N = (2, 1024)
        QK_SCALE = 8.0

        def shift_token(t):
            t1, t2 = jnp.split(t, 2, axis=-1)
            t2 = jnp.pad(t2, ((0, 0), (1, 0), (0, 0)))[:, :-1]
            return jnp.concatenate([t1, t2], axis=-1)

        def l2norm(t):
            return t / jnp.clip(jnp.linalg.norm(t, axis=-1, keepdims=True), 1e-12)

        def rotate_half(x):
            x1, x2 = jnp.split(x, 2, axis=-1)
            return jnp.concatenate([-x2, x1], axis=-1)

        def rotary_xpos(q, k):
            n = q.shape[-2]
            half_idx = jnp.arange(0, DIM_HEAD, 2, dtype=jnp.float32)
            inv_freq = 1.0 / 10000.0 ** (half_idx / DIM_HEAD)
            t = jnp.arange(n, dtype=jnp.float32)
            freqs = t[:, None] * inv_freq[None, :]
            freqs = jnp.concatenate([freqs, freqs], axis=-1)
            base = (half_idx + 0.4 * DIM_HEAD) / (1.4 * DIM_HEAD)
            power = (t - n // 2) / float(WINDOW // 2)
            scale = base[None, :] ** power[:, None]
            scale = jnp.concatenate([scale, scale], axis=-1)
            cos, sin = (jnp.cos(freqs), jnp.sin(freqs))
            q = q * cos * scale + rotate_half(q) * sin * scale
            k = k * cos / scale + rotate_half(k) * sin / scale
            return (q, k)

        def local_attention(q, k, v):
            b, h, n, d = q.shape
            w = n // WINDOW
            bq = q.reshape(b, h, w, WINDOW, d) * QK_SCALE
            bk = k.reshape(b, h, w, WINDOW, d)
            bv = v.reshape(b, h, w, WINDOW, d)

            def look_around(t):
                p = jnp.pad(t, ((0, 0), (0, 0), (1, 0), (0, 0), (0, 0)))
                return jnp.concatenate([p[:, :, :w], p[:, :, 1:]], axis=3)
            bk, bv = (look_around(bk), look_around(bv))
            bt = jnp.arange(n).reshape(w, WINDOW)
            btp = jnp.pad(bt, ((1, 0), (0, 0)), constant_values=-1)
            btk = jnp.concatenate([btp[:w], btp[1:]], axis=1)
            sim = jnp.einsum('bhwid,bhwjd->bhwij', bq, bk)
            i = bt[:, :, None]
            j = btk[:, None, :]
            mask = (i < j) | (i > j + WINDOW) | (j == -1)
            sim = jnp.where(mask, -jnp.finfo(sim.dtype).max, sim)
            attn = jax.nn.softmax(sim, axis=-1)
            out = jnp.einsum('bhwij,bhwjd->bhwid', attn, bv)
            return out.reshape(b, h, n, d)

        def _layer(x, wqkv, qs, ksc, wo, lg, lb, w1, b1, w2, b2):
            b, n, _ = x.shape
            h = shift_token(x)
            qkv = h @ wqkv
            q, k, v = jnp.split(qkv, 3, axis=-1)
            to_heads = lambda t: t.reshape(b, n, HEADS, DIM_HEAD).transpose(0, 2, 1, 3)
            q, k, v = (to_heads(q), to_heads(k), to_heads(v))
            q = l2norm(q) * qs
            k = l2norm(k) * ksc
            q, k = rotary_xpos(q, k)
            o = local_attention(q, k, v)
            o = o.transpose(0, 2, 1, 3).reshape(b, n, INNER)
            x = x + o @ wo
            h = shift_token(x)
            mu = h.mean(-1, keepdims=True)
            var = h.var(-1, keepdims=True)
            h = (h - mu) / jnp.sqrt(var + 1e-05) * lg + lb
            h = h @ w1 + b1
            a, g = jnp.split(h, 2, axis=-1)
            h = a * jax.nn.gelu(g, approximate=False)
            x = x + h @ w2 + b2
            return x
        key = jax.random.key(seed)
        ks = jax.random.split(key, 6)
        return {'x': jax.random.normal(ks[0], (B, N, DIM), jnp.float32), 'wqkv': jax.random.normal(ks[1], (DEPTH, DIM, 3 * INNER), jnp.float32) * 0.02, 'q_scale': jnp.ones((DEPTH, DIM_HEAD), jnp.float32), 'k_scale': jnp.ones((DEPTH, DIM_HEAD), jnp.float32), 'wo': jax.random.normal(ks[2], (DEPTH, INNER, DIM), jnp.float32) * 0.02, 'ln_g': jnp.ones((DEPTH, DIM), jnp.float32), 'ln_b': jnp.zeros((DEPTH, DIM), jnp.float32), 'w1': jax.random.normal(ks[3], (DEPTH, DIM, 2 * HID), jnp.float32) * 0.02, 'b1': jnp.zeros((DEPTH, 2 * HID), jnp.float32), 'w2': jax.random.normal(ks[4], (DEPTH, HID, DIM), jnp.float32) * 0.02, 'b2': jnp.zeros((DEPTH, DIM), jnp.float32)}
    _L0_ffn_all = _L0_ffn_setup()
    _L0_ffn_in = {k: v for k, v in _L0_ffn_all.items() if k in ('wqkv', 'q_scale', 'k_scale', 'wo', 'ln_g', 'ln_b', 'w1', 'b1', 'w2', 'b2')}
    del _L0_ffn_all
    return {'x': x, 'ctx_1024': ctx_1024, 'L0_xattn_Wk': _L0_xattn_in['Wk'], 'L0_xattn_Wv': _L0_xattn_in['Wv'], 'L0_xattn_bv': _L0_xattn_in['bv'], 'L0_xattn_Wq': _L0_xattn_in['Wq'], 'L0_xattn_bq': _L0_xattn_in['bq'], 'L0_xattn_Wo': _L0_xattn_in['Wo'], 'L0_xattn_bo': _L0_xattn_in['bo'], 'L0_ffn_wqkv': _L0_ffn_in['wqkv'], 'L0_ffn_q_scale': _L0_ffn_in['q_scale'], 'L0_ffn_k_scale': _L0_ffn_in['k_scale'], 'L0_ffn_wo': _L0_ffn_in['wo'], 'L0_ffn_ln_g': _L0_ffn_in['ln_g'], 'L0_ffn_ln_b': _L0_ffn_in['ln_b'], 'L0_ffn_w1': _L0_ffn_in['w1'], 'L0_ffn_b1': _L0_ffn_in['b1'], 'L0_ffn_w2': _L0_ffn_in['w2'], 'L0_ffn_b2': _L0_ffn_in['b2']}

def reference(x, ctx_1024, L0_xattn_Wk, L0_xattn_Wv, L0_xattn_bv, L0_xattn_Wq, L0_xattn_bq, L0_xattn_Wo, L0_xattn_bo, L0_ffn_wqkv, L0_ffn_q_scale, L0_ffn_k_scale, L0_ffn_wo, L0_ffn_ln_g, L0_ffn_ln_b, L0_ffn_w1, L0_ffn_b1, L0_ffn_w2, L0_ffn_b2):
    import jax
    import jax.numpy as jnp

    def _L0_xattn_ref(k, v, q, Wk, Wv, bv, Wq, bq, Wo, bo):
        import jax, jax.numpy as jnp
        import numpy as np
        D_MODEL = 128
        B, S = (4, 256)
        kp = jnp.einsum('bsd,ed->bse', k, Wk)
        vp = jnp.einsum('bsd,ed->bse', v, Wv) + bv
        qp = jnp.einsum('bsd,ed->bse', q, Wq) + bq
        scale = 1.0 / jnp.sqrt(jnp.float32(kp.shape[-1]))
        scores = jnp.einsum('bqd,bkd->bqk', qp, kp) * scale
        probs = jax.nn.softmax(scores, axis=-1)
        ctx = jnp.einsum('bqk,bkd->bqd', probs, vp)
        return jnp.einsum('bqd,ed->bqe', ctx, Wo) + bo

    def _L0_ffn_ref(x, wqkv, q_scale, k_scale, wo, ln_g, ln_b, w1, b1, w2, b2):
        import jax, jax.numpy as jnp
        import numpy as np
        DIM = 128
        DEPTH = 2
        HEADS = 8
        DIM_HEAD = 64
        WINDOW = 64
        INNER = HEADS * DIM_HEAD
        HID = int(DIM * 4 * 2 / 3)
        B, N = (2, 1024)
        QK_SCALE = 8.0

        def shift_token(t):
            t1, t2 = jnp.split(t, 2, axis=-1)
            t2 = jnp.pad(t2, ((0, 0), (1, 0), (0, 0)))[:, :-1]
            return jnp.concatenate([t1, t2], axis=-1)

        def l2norm(t):
            return t / jnp.clip(jnp.linalg.norm(t, axis=-1, keepdims=True), 1e-12)

        def rotate_half(x):
            x1, x2 = jnp.split(x, 2, axis=-1)
            return jnp.concatenate([-x2, x1], axis=-1)

        def rotary_xpos(q, k):
            n = q.shape[-2]
            half_idx = jnp.arange(0, DIM_HEAD, 2, dtype=jnp.float32)
            inv_freq = 1.0 / 10000.0 ** (half_idx / DIM_HEAD)
            t = jnp.arange(n, dtype=jnp.float32)
            freqs = t[:, None] * inv_freq[None, :]
            freqs = jnp.concatenate([freqs, freqs], axis=-1)
            base = (half_idx + 0.4 * DIM_HEAD) / (1.4 * DIM_HEAD)
            power = (t - n // 2) / float(WINDOW // 2)
            scale = base[None, :] ** power[:, None]
            scale = jnp.concatenate([scale, scale], axis=-1)
            cos, sin = (jnp.cos(freqs), jnp.sin(freqs))
            q = q * cos * scale + rotate_half(q) * sin * scale
            k = k * cos / scale + rotate_half(k) * sin / scale
            return (q, k)

        def local_attention(q, k, v):
            b, h, n, d = q.shape
            w = n // WINDOW
            bq = q.reshape(b, h, w, WINDOW, d) * QK_SCALE
            bk = k.reshape(b, h, w, WINDOW, d)
            bv = v.reshape(b, h, w, WINDOW, d)

            def look_around(t):
                p = jnp.pad(t, ((0, 0), (0, 0), (1, 0), (0, 0), (0, 0)))
                return jnp.concatenate([p[:, :, :w], p[:, :, 1:]], axis=3)
            bk, bv = (look_around(bk), look_around(bv))
            bt = jnp.arange(n).reshape(w, WINDOW)
            btp = jnp.pad(bt, ((1, 0), (0, 0)), constant_values=-1)
            btk = jnp.concatenate([btp[:w], btp[1:]], axis=1)
            sim = jnp.einsum('bhwid,bhwjd->bhwij', bq, bk)
            i = bt[:, :, None]
            j = btk[:, None, :]
            mask = (i < j) | (i > j + WINDOW) | (j == -1)
            sim = jnp.where(mask, -jnp.finfo(sim.dtype).max, sim)
            attn = jax.nn.softmax(sim, axis=-1)
            out = jnp.einsum('bhwij,bhwjd->bhwid', attn, bv)
            return out.reshape(b, h, n, d)

        def _layer(x, wqkv, qs, ksc, wo, lg, lb, w1, b1, w2, b2):
            b, n, _ = x.shape
            h = shift_token(x)
            qkv = h @ wqkv
            q, k, v = jnp.split(qkv, 3, axis=-1)
            to_heads = lambda t: t.reshape(b, n, HEADS, DIM_HEAD).transpose(0, 2, 1, 3)
            q, k, v = (to_heads(q), to_heads(k), to_heads(v))
            q = l2norm(q) * qs
            k = l2norm(k) * ksc
            q, k = rotary_xpos(q, k)
            o = local_attention(q, k, v)
            o = o.transpose(0, 2, 1, 3).reshape(b, n, INNER)
            x = x + o @ wo
            h = shift_token(x)
            mu = h.mean(-1, keepdims=True)
            var = h.var(-1, keepdims=True)
            h = (h - mu) / jnp.sqrt(var + 1e-05) * lg + lb
            h = h @ w1 + b1
            a, g = jnp.split(h, 2, axis=-1)
            h = a * jax.nn.gelu(g, approximate=False)
            x = x + h @ w2 + b2
            return x
        for l in range(DEPTH):
            x = _layer(x, wqkv[l], q_scale[l], k_scale[l], wo[l], ln_g[l], ln_b[l], w1[l], b1[l], w2[l], b2[l])
        return x
    x = x + _L0_xattn_ref(ctx_1024, ctx_1024, _layernorm(x, axis=-1), L0_xattn_Wk, L0_xattn_Wv, L0_xattn_bv, L0_xattn_Wq, L0_xattn_bq, L0_xattn_Wo, L0_xattn_bo)
    x = x + _L0_ffn_ref(_layernorm(x, axis=-1), L0_ffn_wqkv, L0_ffn_q_scale, L0_ffn_k_scale, L0_ffn_wo, L0_ffn_ln_g, L0_ffn_ln_b, L0_ffn_w1, L0_ffn_b1, L0_ffn_w2, L0_ffn_b2)
    return x

_drawn_inputs = setup_inputs


def setup_inputs(seed=0):
    import zlib

    import numpy as np

    out = dict(_drawn_inputs(seed))
    spreads = {'L0_xattn_bv': (0.0, 0.1),
     'L0_xattn_bq': (0.0, 0.343),
     'L0_xattn_bo': (0.0, 0.1),
     'L0_ffn_q_scale': (1.0, 0.6),
     'L0_ffn_k_scale': (1.0, 0.6),
     'L0_ffn_ln_g': (1.0, 0.6),
     'L0_ffn_ln_b': (0.0, 0.8),
     'L0_ffn_b1': (0.0, 0.8),
     'L0_ffn_b2': (0.0, 0.788)}
    factors = {'L0_ffn_w1': 6.893, 'L0_ffn_w2': 6.76}
    for name, (base, spread) in spreads.items():
        noise = np.random.default_rng([zlib.crc32(name.encode()), seed]).standard_normal(out[name].shape)
        drawn = base * np.exp(spread * noise) if base else spread * noise
        out[name] = jnp.asarray(drawn.astype(out[name].dtype))
    for name, factor in factors.items():
        out[name] = (out[name] * factor).astype(out[name].dtype)
    return out
```

```python
from contextlib import ExitStack

import numpy as np

import concourse.bass as bass
from concourse import mybir

ALU = mybir.AluOpType
ACT = mybir.ActivationFunctionType
AX_X = mybir.AxisListType.X
F32 = mybir.dt.float32
F32R = mybir.dt.float32r

P = 128
MASKED = -1e30


class Shapes:

    def __init__(self, x, ctx, w1):
        _, self.n, self.d = x.shape
        _, self.keys, _ = ctx.shape
        self.tiles = self.n // P
        self.ktiles = self.keys // P
        self.tail = self.keys - self.ktiles * P
        self.hid = w1.shape[2] // 2


def shape_constants(n, heads_dim, window):
    half = np.arange(0, heads_dim, 2, dtype=np.float32)
    inv_freq = (1.0 / 10000.0 ** (half / np.float32(heads_dim))).astype(np.float32)
    t = np.arange(n, dtype=np.float32)
    freqs = t[:, None] * inv_freq[None, :]
    freqs = np.concatenate([freqs, freqs], axis=-1)
    base = ((half + np.float32(0.4 * heads_dim)) / np.float32(1.4 * heads_dim)).astype(np.float32)
    power = ((t - n // 2) / np.float32(window // 2)).astype(np.float32)
    scale = base[None, :] ** power[:, None]
    scale = np.concatenate([scale, scale], axis=-1)
    cos, sin = np.cos(freqs), np.sin(freqs)
    sign = np.where(np.arange(heads_dim) < heads_dim // 2, -1.0, 1.0).astype(np.float32)
    rot = np.stack([np.stack([cos * scale, cos / scale], 1),
                    np.stack([sin * scale * sign, sin / scale * sign], 1)], 1)
    rot = rot.reshape(n // P, P, 2 * 2 * heads_dim).transpose(1, 0, 2)
    i = np.arange(P)[:, None]
    j = np.arange(-window, P)[None, :]
    ok = (j <= i) & (i <= j + window) & (j // window >= i // window - 1)
    mask = np.stack([np.where(ok & (j >= 0), 0.0, MASKED), np.where(ok, 0.0, MASKED)], 1)
    ident = np.eye(P)
    down = np.eye(P, k=1)
    edge = np.zeros((P, P))
    edge[P - 1, 0] = 1.0
    mats = np.stack([ident, down, edge], 1)
    return (np.ascontiguousarray(rot, np.float32), np.ascontiguousarray(mask, np.float32),
            np.ascontiguousarray(mats, np.float32))


def xattn_ffn_kernel(nc, x, ctx_1024, Wk, Wv, bv, Wq, bq, Wo, bo,
                     wqkv, q_scale, k_scale, wo, ln_g, ln_b, w1, b1, w2, b2,
                     rot_tab, mask_tab, mats, out):
    sh = Shapes(x, ctx_1024, w1)
    D = sh.d
    NT, KT, TAIL, NKEYS = sh.tiles, sh.ktiles, sh.tail, sh.keys
    DEPTH = wqkv.shape[0]
    INNER = wqkv.shape[2] // 3
    HD = q_scale.shape[1]
    H = INNER // HD
    HID = sh.hid
    WIN = HD
    SCALE = float(1.0 / np.sqrt(np.float32(D)))
    QK_SCALE = 8.0
    EPS = 1e-5

    PAIRS = NT // 2
    HALVES = 2
    UNITS = PAIRS * HALVES
    HT_ = KT // HALVES
    half0 = [h * HT_ * P for h in range(HALVES)]
    hkeys = [HT_ * P, HT_ * P + TAIL]
    CH = 4
    CB = HT_ * P // (2 * CH)
    chunks = [[(c * 2 * CB, CB, CB + (TAIL if h == HALVES - 1 and c == CH - 1 else 0)) for c in range(CH)]
              for h in range(HALVES)]
    G = 2
    NG = (HT_ + G) // G
    SC_STEP = {g: g for g in range(2 * CH)}

    def group(h, g):
        tiles = [(i * P, P, h * HT_ + i) for i in range(HT_)]
        if h == HALVES - 1:
            tiles.append((HT_ * P, TAIL, KT))
        return tiles[G * g:G * g + G]

    ring = []
    for u in range(UNITS):
        for g in range(NG):
            ring.append(("T", u, g))
            if u and g == 3:
                ring.append(("C", u - 1, 0))
            if u and g == 6:
                ring.append(("O", u - 1, 0))
    ring += [("C", UNITS - 1, 0), ("O", UNITS - 1, 0)]
    at = {e: i for i, e in enumerate(ring)}
    exp_steps = {4: (0, 0), 6: (0, 1), 7: (0, 2), 8: (0, 3), 9: (1, 0), 11: (1, 1)}
    exp_late = {1: (1, 2), 3: (1, 3)}
    exps = [(0, j, c) for (j, c) in exp_steps.values()]
    for u in range(UNITS):
        for g in range(NG):
            if g in exp_late:
                exps.append((u, *exp_late[g]))
            if g in exp_steps and u + 1 < UNITS:
                exps.append((u + 1, *exp_steps[g]))
    exp_at = {e: i for i, e in enumerate(exps)}
    RING = 4

    N_UNITS = DEPTH * NT
    GT = 4
    NBLK = (HID + P - 1) // P
    blk = [(b * P, min(P, HID - b * P)) for b in range(NBLK)]

    with ExitStack() as ctx:
        def sem(name):
            return ctx.enter_context(nc.semaphore(name))

        def sb(name, shape, dt=F32, stack=ctx):
            return stack.enter_context(nc.sbuf_tensor(name, shape, dt))

        psum = ctx.enter_context(nc.psum_tensor("psum", [P, 8, 512], F32))

        x_sb = sb("x_sb", [P, NT, D])
        y_sb = [sb(f"y{l}", [P, NT, D]) for l in range(DEPTH)]
        mat = sb("mat", [P, 3, P])
        ident, down, edge = mat[:, 0, :], mat[:, 1, :], mat[:, 2, :]
        stats = sb("stats", [P, NT, 6])
        mv = sb("mv", [P, NT, 2])
        rstd = sb("rstd", [P, NT, 1])
        minus_half = sb("minus_half", [P, 2 * H])

        first = ExitStack()
        with first:
            a = lambda name, shape, dt=F32: sb(name, shape, dt, first)
            keyT = a("keyT", [P, 2, NKEYS], F32R)
            vals = a("vals", [P, 2, KT + 1, D], F32R)
            S = a("S", [P, HALVES, 2, hkeys[-1]])
            turned = a("turned", [P, RING, G, 2, 2 * P], F32R)
            w4 = a("w4", [P, 4, D])
            wT = a("wT", [P, 3, D])
            qT = a("qT", [P, NT * P])
            qpT = a("qpT", [P, NT * P])
            qh = a("qh", [P, 2, NT * P], F32R)
            bqc = a("bqc", [P, 1])
            bvc = a("bvc", [P, 1])
            bvr = a("bvr", [P, P])
            bob = a("bob", [P, D])
            cmax = a("cmax", [P, UNITS, 2, CH])
            nmax = a("nmax", [P, UNITS, 2])
            zpart = a("zpart", [P, UNITS, 2, CH])
            accb = a("accb", [P, 2 * P])
            uT = a("uT", [P, 2 * P])
            cT = a("cT", [P, 2 * P])
            oh = a("oh", [P, HALVES, 2, D])
            mmin = a("mmin", [P, 2])
            al = a("al", [P, HALVES, 2])
            zs = a("zs", [P, HALVES, 2])
            zt = a("zt", [P, 2])
            raw = S[:, :, :, :].rearrange("p h j k -> p (h j k)")[:, 0:KT * D].rearrange("p (t d) -> p t d", d=D)
            rawt = a("rawt", [P, D])

        second = ExitStack()
        ctx.enter_context(second)
        f = lambda name, shape, dt=F32: sb(name, shape, dt, second)
        wqkv_sb = f("wqkv_sb", [P, DEPTH, 3 * INNER])
        wo_sb = f("wo_sb", [P, DEPTH, INNER // P, D])
        w1_sb = f("w1_sb", [P, DEPTH, 2 * HID])
        w2_sb = f("w2_sb", [P, DEPTH, NBLK, D])
        b1c = f("b1c", [P, DEPTH, 2, NBLK])
        b2r = f("b2r", [1, DEPTH, D])
        lnc = f("lnc", [P, 2, DEPTH])
        sc_b = f("sc_b", [P, 2, DEPTH, HD])
        ones_row = f("ones_row", [1, P])
        rot = f("rot", [P, NT, 2, 2, HD])
        rotl = f("rotl", [P, DEPTH, NT, 2, 2, HD])
        mask = f("mask", [P, 2, WIN + P])
        mask_r = f("mask_r", [P, 2, WIN + P], F32R)
        ident_r = f("ident_r", [P, P], F32R)
        hT = [f(f"hT{l}", [P, WIN + NT * P + 4]) for l in range(DEPTH)]
        qk = f("qk", [P, 2, H, HD])
        sq = f("sq", [P, 2 * H, HD])
        ra = f("ra", [P, 2, H, HD])
        rb = f("rb", [P, 2, H, HD])
        ss = f("ss", [P, 2 * H])
        rinv = f("rinv", [P, 2, 2 * H])
        r8 = f("r8", [P, 3, H])
        kn = f("kn", [P, H, HD])
        qTh = f("qTh", [P, 2, H // 2, P])
        kTh = f("kTh", [P, H // 2, WIN + NT * P])
        v_sb = f("v_sb", [P, 3, INNER])
        v_prev = f("v_prev", [WIN, 3, INNER])
        mx = f("mx", [P, H])
        nb = f("nb", [P, 2, H])
        z = f("z", [P, 2, H])
        rz = f("rz", [P, H])
        prob = f("prob", [P, 2, H // 2, WIN + P])
        ptA = f("ptA", [P, H // 2, P])
        ptB = f("ptB", [WIN, H // 2, WIN])
        o_sb = f("o_sb", [P, H, HD])
        oT = f("oT", [P, INNER // P, P])
        y1 = [f(f"yatt{l}", [P, NT, D]) for l in range(DEPTH)]
        h2 = f("h2", [P, GT, D])
        hn = f("hn", [P, GT, D])
        fstats = f("fstats", [P, GT, 6])
        fmv = f("fmv", [P, GT, 2])
        fve = f("fve", [P, GT])
        frs = f("frs", [P, GT])
        h2T = f("h2T", [P, GT * P])
        gl = f("gl", [P, NBLK, GT * P])
        mid = f("mid", [P, NBLK, GT * P])

        ld_x, ld_w, ld_t, ld_m, ld_b = (sem(s) for s in ("ld_x", "ld_w", "ld_t", "ld_m", "ld_b"))
        LOADS = 5
        ld_c = [sem(f"ld_c{i}") for i in range(LOADS)]
        stored = sem("stored")
        ld_f, ld_g = sem("ld_f"), sem("ld_g")
        half_set = sem("half_set")
        dve_link, act_link, pool_link = sem("dve_link"), sem("act_link"), sem("pool_link")
        var_ready, rstd_ready, xn_ready = sem("var_ready"), sem("rstd_ready"), sem("xn_ready")
        pre_pe, pre_act = sem("pre_pe"), sem("pre_act")
        pre_dve = sem("pre_dve")
        ct_ready, ct_high, ct_low = sem("ct_ready"), sem("ct_high"), sem("ct_low")
        vh_ready, vl_ready = sem("vh_ready"), sem("vl_ready")
        scores_ready, scores_moved = sem("scores_ready"), sem("scores_moved")
        max_ready, prob_ready = sem("max_ready"), sem("prob_ready")
        ring_ready, high_ready, ring_done = sem("ring_ready"), sem("high_ready"), sem("ring_done")
        pv_done, accb_ready, acc_read = sem("pv_done"), sem("accb_ready"), sem("acc_read")
        alpha_in, alpha_ready = sem("alpha_in"), sem("alpha_ready")
        y0_ready = sem("y0_ready")
        x_out = sem("x_out")
        cross_pe, cross_act = sem("cross_pe"), sem("cross_act")
        setup_f = sem("setup_f")
        f_yT, f_hTa, f_hTb, f_qkv, f_qk_moved, f_v_moved = (
            sem(s) for s in ("f_yT", "f_hTa", "f_hTb", "f_qkv", "f_qk_moved", "f_v_moved"))
        f_vp = [sem(f"f_vp{i}") for i in range(3)]
        f_sq, f_ss, f_rinv, f_rab, f_rsum, f_kn, f_r8 = (
            sem(s) for s in ("f_sq", "f_ss", "f_rinv", "f_rab", "f_rsum", "f_kn", "f_r8"))
        f_turn, f_turned = sem("f_turn"), sem("f_turned")
        a_s, a_nb, a_p, a_t, a_tA, a_tB, a_o, a_on, a_oT, a_oTm, a_wo, a_y1 = (
            sem(s) for s in ("a_s", "a_nb", "a_p", "a_t", "a_tA", "a_tB", "a_o", "a_on", "a_oT", "a_oTm",
                             "a_wo", "a_y1"))
        m_sh, m_h2, m_var, m_rs, m_hn, m_hT, m_h2T, m_w1, m_gelu, m_mid, m_w2, m_y = (
            sem(s) for s in ("m_sh", "m_h2", "m_var", "m_rs", "m_hn", "m_hT", "m_h2T", "m_w1", "m_gelu",
                             "m_mid", "m_w2", "m_y"))
        block = ctx.enter_context(nc.Block())

        x_tok = x.rearrange("a (t p) d -> p (a t) d", p=P)
        out_tok = out.rearrange("a (t p) d -> p (a t) d", p=P)
        ctx_whole = ctx_1024[0, 0:KT * P, :].rearrange("(p t) d -> p t d", p=P)
        piece = KT // LOADS

        FFN_LOADS = 3 + DEPTH * (3 * NBLK + 2) + 1
        G_LOADS = 2 + 2 * DEPTH

        @block.sync
        def _(sp):
            sp.dma_start(x_sb[:, :, :], x_tok).then_inc(ld_x, 16)
            sp.dma_start(mat[:, :, :], mats).then_inc(ld_m, 16)
            for i, w in enumerate((Wq, Wk, Wv, Wo)):
                sp.dma_start(w4[:, i, :], w).then_inc(ld_w, 16)
            sp.dma_start(bqc[:, :], bq.rearrange("(p a) -> p a", a=1)).then_inc(ld_b, 16)
            sp.dma_start(bvc[:, :], bv.rearrange("(p a) -> p a", a=1)).then_inc(ld_b, 16)
            sp.dma_start(bob[:, :], bo.rearrange("(a d) -> a d", a=1).broadcast_to([P, D])).then_inc(ld_b, 16)
            for i in range(LOADS):
                sp.dma_start(raw[:, i * piece:(i + 1) * piece, :],
                             ctx_whole[:, i * piece:(i + 1) * piece, :]).then_inc(ld_c[i], 16)
            sp.dma_start(rawt[0:TAIL, :], ctx_1024[0, KT * P:NKEYS, :]).then_inc(ld_t, 16)

            sp.wait_ge(cross_pe, 1)
            sp.wait_ge(y0_ready, 1)
            sp.wait_ge(cross_act, 1)
            sp.dma_start(wqkv_sb[:, :, :], wqkv.rearrange("l p n -> p l n")).then_inc(ld_f, 16)
            sp.dma_start(rot[:, :, :, :, :], rot_tab.rearrange("p t (c k d) -> p t c k d", c=2, k=2)).then_inc(ld_g, 16)
            for i, s in enumerate((q_scale, k_scale)):
                for l in range(DEPTH):
                    sp.dma_start(sc_b[:, i, l, :], s[l:l + 1, :].broadcast_to([P, HD])).then_inc(ld_g, 16)
            sp.dma_start(mask[:, :, :], mask_tab).then_inc(ld_g, 16)
            sp.dma_start(wo_sb[:, :, :, :], wo.rearrange("l (c p) n -> p l c n", p=P)).then_inc(ld_f, 16)
            sp.dma_start(w1_sb[:, :, :], w1.rearrange("l p n -> p l n")).then_inc(ld_f, 16)
            n_f = 3
            for l in range(DEPTH):
                for b, (c0, w) in enumerate(blk):
                    sp.dma_start(w2_sb[0:w, l, b, :], w2[l, c0:c0 + w, :]).then_inc(ld_f, 16)
                    for k in range(2):
                        sp.dma_start(b1c[0:w, l, k, b:b + 1],
                                     b1[l, k * HID + c0:k * HID + c0 + w].rearrange("(p a) -> p a", a=1)).then_inc(ld_f, 16)
                        n_f += 1
                    n_f += 1
                sp.dma_start(lnc[:, 0, l:l + 1], ln_g[l, :].rearrange("(p a) -> p a", a=1)).then_inc(ld_f, 16)
                sp.dma_start(lnc[:, 1, l:l + 1], ln_b[l, :].rearrange("(p a) -> p a", a=1)).then_inc(ld_f, 16)
                n_f += 2
            sp.dma_start(b2r[:, :, :], b2.rearrange("(a l) d -> a l d", a=1)).then_inc(ld_f, 16)
            assert n_f + 1 == FFN_LOADS

            for n in range(N_UNITS):
                sp.wait_ge(f_v_moved, n + 1)
                if n >= 3:
                    sp.wait_ge(a_o, 2 * (n - 1))
                sp.dma_start(v_prev[:, n % 3, :], v_sb[WIN:2 * WIN, n % 3, :]).then_inc(f_vp[n % 3], 16)
            for g in range(NT // GT):
                sp.wait_ge(x_out, g + 1)
                sp.dma_start(out_tok[:, g * GT:(g + 1) * GT, :], x_sb[:, g * GT:(g + 1) * GT, :]).then_inc(stored, 16)
            sp.wait_ge(stored, 16 * (NT // GT))


        def three(pe, o, lh, ll, rh, rl):
            pe.matmul(o, lh, rh, start=True, stop=False)
            pe.matmul(o, lh, rl, start=False, stop=False)
            return pe.matmul(o, ll, rh, start=False, stop=True)

        def cross_tensor(pe):
            pe.wait_ge(ld_w, 64)
            pe.wait_ge(ld_m, 16)
            for i, k in enumerate((0, 2, 3)):
                m = pe.transpose(psum[:, 0, i * P:(i + 1) * P], w4[:, k, :], ident)
            m.then_inc(pre_pe, 1)
            pe.wait_ge(xn_ready, 1)
            for t in range(NT):
                m = pe.transpose(psum[:, 1 + t // 4, (t % 4) * P:(t % 4 + 1) * P], y_sb[0][:, t, :], ident)
            m.then_inc(pre_pe, 1)
            pe.wait_ge(pre_act, 2)
            for b in range(NT // 4):
                m = pe.matmul(psum[:, 3 + b, :], wT[:, 0, :], qT[:, b * 512:(b + 1) * 512], start=True, stop=True)
            m.then_inc(pre_pe, 1)
            pe.wait_ge(pre_act, 3)
            for b in range(NT // 4):
                m = pe.matmul(psum[:, 5 + b, :], w4[:, 1, :], qpT[:, b * 512:(b + 1) * 512], start=True, stop=True)
            m.then_inc(pre_pe, 1)
            pe.wait_ge(pre_dve, 1)
            m = pe.matmul(psum[:, 7, 0:P], bvr[:, :], wT[:, 2, :], start=True, stop=True)
            m.then_inc(pre_pe, 1)
            for i in range((KT + 1 + 3) // 4):
                if i == 0:
                    pe.wait_ge(pre_act, 2)
                if i >= 2:
                    pe.wait_ge(ct_low, i - 1)
                for t in range(4 * i, min(4 * i + 4, KT + 1)):
                    if t < KT:
                        pe.wait_ge(ld_c[t // piece], 16)
                        m = pe.transpose(psum[:, 1 + i % 2, (t % 4) * P:(t % 4 + 1) * P], raw[:, t, :], ident)
                    else:
                        pe.wait_ge(ld_t, 16)
                        m = pe.transpose(psum[:, 1 + i % 2, (t % 4) * P:(t % 4) * P + TAIL], rawt[0:TAIL, :],
                                         ident[0:TAIL, 0:TAIL])
                m.then_inc(ct_ready, 1)
            n_ct = (KT + 1 + 3) // 4

            def scores(u, j, c):
                p, h = divmod(u, HALVES)
                k = (u * 2 + j) * CH + c
                c0, *widths = chunks[h][c]
                if k >= 2:
                    pe.wait_ge(scores_moved, k - 1)
                rows = slice((2 * p + j) * P, (2 * p + j + 1) * P)
                for b, w in enumerate(widths):
                    cols = slice(half0[h] + c0 + b * CB, half0[h] + c0 + b * CB + w)
                    m = three(pe, psum[:, 2 * (k % 2) + b, 0:w], qh[:, 0, rows], qh[:, 1, rows],
                              keyT[:, 0, cols], keyT[:, 1, cols])
                m.then_inc(scores_ready, 1)

            def enter(e):
                i = at[e]
                if i >= 2:
                    pe.wait_ge(ring_done, i - 1)
                return psum[:, 4 + i % 2, :]

            def turn(u, g):
                h = u % HALVES
                last = group(h, g)[-1]
                c = min((last[0] + last[1] - 1) // (2 * CB), CH - 1)
                pe.wait_ge(prob_ready, max(exp_at[u, 0, c], exp_at[u, 1, c]) + 1)
                b = enter(("T", u, g))
                for s, (c0, rows, _) in enumerate(group(h, g)):
                    for j in range(2):
                        m = pe.transpose(b[0:rows, s * 256 + j * P:s * 256 + (j + 1) * P],
                                         S[:, h, j, c0:c0 + rows], ident)
                m.then_inc(ring_ready, 1)

            def weigh(u, g):
                h = u % HALVES
                if g == 0 and u:
                    pe.wait_ge(acc_read, u)
                i = at["T", u, g]
                pe.wait_ge(ring_done, i + 1)
                slot = (u * NG + g) % RING
                for s, (c0, rows, t) in enumerate(group(h, g)):
                    start, stop = g == 0 and s == 0, g == NG - 1 and s == len(group(h, g)) - 1
                    pe.matmul(psum[:, 6, :], vals[0:rows, 0, t, :],
                              turned[0:rows, slot, s, :, :].rearrange("p a b -> p (a b)"), start=start, stop=stop)
                    m = pe.matmul(psum[:, 7, 0:256], vals[0:rows, 1, t, :], turned[0:rows, slot, s, 0, :],
                                  start=start, stop=stop)
                m.then_inc(pv_done, 1)

            def through(u, part):
                b = enter((part, u, 0))
                if part == "C":
                    pe.wait_ge(acc_read, u + 1)
                    m = pe.matmul(b[:, 0:256], wT[:, 1, :], uT[:, :], start=True, stop=True)
                else:
                    pe.wait_ge(ring_done, at["C", u, 0] + 1)
                    for j in range(2):
                        m = pe.matmul(b[:, j * P:(j + 1) * P], cT[:, j * P:(j + 1) * P], wT[:, 2, :],
                                      start=True, stop=True)
                m.then_inc(ring_ready, 1)

            pe.wait_ge(ct_low, n_ct)
            pe.wait_ge(pre_dve, 3)
            for j in range(2):
                for c in range(CH):
                    scores(0, j, c)
            pe.wait_ge(vl_ready, 2)
            for u in range(UNITS):
                for g in range(NG):
                    turn(u, g)
                    if u and g == 3:
                        through(u - 1, "C")
                    if u and g == 6:
                        through(u - 1, "O")
                    if g in SC_STEP and u + 1 < UNITS:
                        scores(u + 1, *divmod(SC_STEP[g], CH))
                    if g >= 2:
                        weigh(u, g - 2)
                weigh(u, NG - 2)
                weigh(u, NG - 1)
            through(UNITS - 1, "C")
            through(UNITS - 1, "O")
            pe.wait_ge(ring_done, len(ring))
            pe.matmul(psum[:, 0, 0:8], ident, ident[:, 0:8], start=True, stop=True).then_inc(cross_pe, 1)

        def place(n):
            return divmod(n, NT)

        def moved_b(i):
            return sum(k // 2 % NT > 0 for k in range(i + 1))

        def turn_y(pe, n):
            l, t = place(n)
            if l == 0:
                pe.wait_ge(y0_ready, 1)
            else:
                pe.wait_ge(m_y, (l - 1) * (NT // GT) + t // GT + 1)
            if n:
                pe.wait_ge(f_turned, 2 * n)
            pe.transpose(psum[:, 0, 0:P], y_sb[l][:, t, :], ident).then_inc(f_yT, 1)

        def project(pe, n):
            l, t = place(n)
            if n == 0:
                pe.wait_ge(ld_f, 16 * FFN_LOADS)
                pe.wait_ge(setup_f, 2)
            pe.wait_ge(f_hTa, n + 1)
            pe.wait_ge(f_hTb, n + 1)
            if n:
                pe.wait_ge(f_v_moved, n)
            h = hT[l][:, WIN + t * P:WIN + (t + 1) * P]
            for i in range(3):
                m = pe.matmul(psum[:, i, 0:INNER], h, wqkv_sb[:, l, i * INNER:(i + 1) * INNER], start=True, stop=True)
            m.then_inc(f_qkv, 1)

        def turn_qk(pe, n):
            pe.wait_ge(f_qk_moved, n + 1)
            pe.wait_ge(f_rsum, n + 1)
            for a_ in range(H // 2):
                m = pe.transpose(psum[:, 0, a_ * P:(a_ + 1) * P],
                                 ra[:, 0, 2 * a_:2 * a_ + 2, :].rearrange("p h d -> p (h d)"), ident)
            m.then_inc(f_turn, 1)
            pe.wait_ge(f_kn, n + 1)
            for a_ in range(H // 2):
                m = pe.transpose(psum[:, 1, a_ * P:(a_ + 1) * P],
                                 kn[:, 2 * a_:2 * a_ + 2, :].rearrange("p h d -> p (h d)"), ident)
            m.then_inc(f_turn, 1)

        def att_scores(pe, n, hg):
            l, t = place(n)
            pe.wait_ge(f_turned, 2 * (n + 1))
            i = 2 * n + hg
            if i:
                pe.wait_ge(a_p, i)
            for b in range(2):
                rows = slice(b * HD, (b + 1) * HD)
                pe.matmul(psum[:, 3 + b, 0:2 * (WIN + P)].rearrange("p (h k) -> p h k", h=2), ident_r[:, :],
                          mask_r[:, min(t, 1), :].unsqueeze(1).broadcast_to([P, 2, WIN + P]), start=True, stop=False)
                for e in range(2):
                    pr = 2 * hg + e
                    m = pe.matmul(psum[:, 3 + b, e * (WIN + P):(e + 1) * (WIN + P)], qTh[rows, n % 2, pr, :],
                                  kTh[rows, pr, t * P:t * P + WIN + P], start=False, stop=(e == 1))
            m.then_inc(a_s, 1)

        def att_turn(pe, n, hg):
            l, t = place(n)
            i = 2 * n + hg
            pe.wait_ge(a_p, i + 1)
            if i:
                pe.wait_ge(a_tA, i)
                if i > 2:
                    pe.wait_ge(a_tB, moved_b(i - 1))
            if n and hg == 0:
                pe.wait_ge(a_oTm, n)
                pe.wait_ge(a_y1, n)
            elif n >= 1:
                pe.wait_ge(a_oTm, n)
                pe.wait_ge(a_y1, n)
            for e in range(H // 2):
                pe.transpose(psum[:, 5, e * P:(e + 1) * P], prob[:, hg, e, WIN:WIN + P], ident)
            if t:
                for e in range(H // 2):
                    m = pe.transpose(psum[0:WIN, 6, e * WIN:(e + 1) * WIN], prob[0:WIN, hg, e, 0:WIN],
                                     ident[0:WIN, 0:WIN])
                m.then_inc(a_t, 1)
            else:
                pe.transpose(psum[:, 5, (H // 2 - 1) * P:(H // 2) * P], prob[:, hg, H // 2 - 1, WIN:WIN + P],
                             ident).then_inc(a_t, 1)

        def att_weigh(pe, n, hg):
            l, t = place(n)
            i = 2 * n + hg
            pe.wait_ge(a_tA, i + 1)
            if t:
                pe.wait_ge(a_tB, moved_b(i))
            pe.wait_ge(f_v_moved, n + 1)
            if hg == 0 and n:
                pe.wait_ge(a_on, n)
            if t:
                pe.wait_ge(f_vp[(n - 1) % 3], 16 * ((n - 1) // 3 + 1))
            for e in range(H // 2):
                hd = hg * (H // 2) + e
                o = psum[:, 7, hd * HD:(hd + 1) * HD]
                m = pe.matmul(o, ptA[:, e, :], v_sb[:, n % 3, hd * HD:(hd + 1) * HD], start=True, stop=not t,
                              skip_group_check=True)
                if t:
                    m = pe.matmul(psum[0:WIN, 7, hd * HD:(hd + 1) * HD], ptB[:, e, :],
                                  v_prev[:, (n - 1) % 3, hd * HD:(hd + 1) * HD], start=False, stop=True,
                                  skip_group_check=True)
            m.then_inc(a_o, 1)

        def turn_o(pe, n):
            pe.wait_ge(a_on, n + 1)
            pe.wait_ge(a_tA, 2 * n + 2)
            for a_ in range(INNER // P):
                m = pe.transpose(psum[:, 5, a_ * P:(a_ + 1) * P],
                                 o_sb[:, 2 * a_:2 * a_ + 2, :].rearrange("p h d -> p (h d)"), ident)
            m.then_inc(a_oT, 1)

        def out_proj(pe, n):
            l, t = place(n)
            pe.wait_ge(a_oTm, n + 1)
            if n:
                pe.wait_ge(a_tB, moved_b(2 * n + 1))
            for a_ in range(INNER // P):
                m = pe.matmul(psum[:, 6, 0:D], oT[:, a_, :], wo_sb[:, l, a_, :], start=(a_ == 0),
                              stop=(a_ == INNER // P - 1))
            m.then_inc(a_wo, 1)

        def feed(pe, l, g):
            k = l * (NT // GT) + g
            n0 = l * NT + g * GT
            pe.wait_ge(a_y1, n0 + GT)
            for s in range(GT):
                t = g * GT + s
                o = psum[:, 5, s * HD:(s + 1) * HD]
                m = pe.matmul(o, down, y1[l][:, t, HD:D], start=True, stop=(t == 0), skip_group_check=True)
                if t:
                    m = pe.matmul(o, edge, y1[l][:, t - 1, HD:D], start=False, stop=True, skip_group_check=True)
            m.then_inc(m_sh, 1)
            pe.wait_ge(m_hn, k + 1)
            for s in range(GT):
                m = pe.transpose(psum[:, 5, s * P:(s + 1) * P], hn[:, s, :], ident)
            m.then_inc(m_hT, 1)
            pe.wait_ge(m_h2T, k + 1)
            pe.wait_ge(a_p, 2 * n0 + 2 * GT)
            order = [(kind, b) for b in range(NBLK) for kind in (1, 0)]
            for i, (kind, b) in enumerate(order):
                if i >= 3:
                    pk, pb = order[i - 3]
                    pe.wait_ge(m_gelu if pk else m_mid, k * NBLK + pb + 1)
                c0, w = blk[b]
                pe.matmul(psum[0:w, (3, 4, 6)[i % 3], :], w1_sb[:, l, kind * HID + c0:kind * HID + c0 + w],
                          h2T[:, :], start=True, stop=True).then_inc(m_w1, 1)
            pe.wait_ge(m_mid, (k + 1) * NBLK)
            for s in range(GT):
                o = psum[:, 5, s * D:(s + 1) * D]
                for b, (c0, w) in enumerate(blk):
                    pe.matmul(o, mid[0:w, b, s * P:(s + 1) * P], w2_sb[0:w, l, b, :], start=(b == 0), stop=False,
                              skip_group_check=True)
                m = pe.matmul(o, ones_row[:, :], b2r[:, l, :], start=False, stop=True, skip_group_check=True)
            m.then_inc(m_w2, 1)
            pe.wait_ge(m_y, k + 1)

        @block.tensor
        def _(pe):
            cross_tensor(pe)
            turn_y(pe, 0)
            project(pe, 0)
            turn_qk(pe, 0)
            for n in range(N_UNITS + 1):
                more = n + 1 < N_UNITS
                if n < N_UNITS:
                    att_scores(pe, n, 0)
                if more:
                    turn_y(pe, n + 1)
                if n:
                    att_turn(pe, n - 1, 1)
                    att_weigh(pe, n - 1, 1)
                if n < N_UNITS:
                    att_scores(pe, n, 1)
                if more:
                    project(pe, n + 1)
                if n:
                    turn_o(pe, n - 1)
                    out_proj(pe, n - 1)
                if n < N_UNITS:
                    att_turn(pe, n, 0)
                    att_weigh(pe, n, 0)
                if more:
                    turn_qk(pe, n + 1)
                if n and n % GT == 0:
                    feed(pe, *divmod(n // GT - 1, NT // GT))

        @block.scalar
        def _(act):
            act.wait_ge(pre_pe, 1)
            act.copy(wT[:, :, :], psum[:, 0, 0:3 * P].rearrange("p (a b) -> p a b", a=3)).then_inc(pre_act, 1)
            act.wait_ge(pre_pe, 2)
            act.copy(qT[:, :], psum[:, 1:3, :]).then_inc(pre_act, 1)
            act.wait_ge(pre_pe, 3)
            act.wait_ge(ld_b, 48)
            act.activation(qpT[:, :], psum[:, 3:5, :], ACT.Identity, bias=bqc[:, 0:1]).then_inc(pre_act, 1)
            act.wait_ge(pre_pe, 4)
            act.copy(qh[:, 0, :], psum[:, 5:7, :]).then_inc(pre_act, 1)
            n_ct = (KT + 1 + 3) // 4
            for i in range(n_ct):
                c0, w = 512 * i, min(512, NKEYS - 512 * i)
                act.wait_ge(ct_ready, i + 1)
                act.copy(keyT[:, 0, c0:c0 + w], psum[:, 1 + i % 2, 0:w]).then_inc(ct_high, 1)

            def high(u, g):
                act.wait_ge(ring_ready, at["T", u, g] + 1)
                k = u * NG + g
                if k >= RING:
                    act.wait_ge(pv_done, k - RING + 1)
                tiles = group(u % HALVES, g)
                rows = tiles[0][1]
                if all(r == P for _, r, _ in tiles):
                    w = len(tiles)
                    act.copy(turned[:, k % RING, 0:w, 0, :],
                             psum[:, 4 + at["T", u, g] % 2, 0:256 * w].rearrange("p (a b) -> p a b", b=256))\
                       .then_inc(high_ready, 1)
                else:
                    for s, (_, r, _) in enumerate(tiles):
                        m = act.copy(turned[0:r, k % RING, s, 0, :],
                                     psum[0:r, 4 + at["T", u, g] % 2, 256 * s:256 * (s + 1)])
                    m.then_inc(high_ready, 1)

            def expo(u, j, c):
                h = u % HALVES
                act.wait_ge(max_ready, 2 * u + j + 1)
                c0, w0, w1_ = chunks[h][c]
                s = S[:, h, j, c0:c0 + w0 + w1_]
                act.activation(s, s, ACT.Exp, bias=nmax[:, u, j:j + 1],
                               accum_out=zpart[:, u, j, c:c + 1]).then_inc(prob_ready, 1)

            def acc_b(u):
                act.wait_ge(pv_done, (u + 1) * NG)
                if u:
                    act.wait_ge(acc_read, u)
                act.copy(accb[:, :], psum[:, 7, 0:256]).then_inc(accb_ready, 1)

            def alphas(p):
                act.wait_ge(alpha_in, p + 1)
                act.activation(al[:, :, :], al[:, :, :], ACT.Exp).then_inc(alpha_ready, 1)

            for j, c in exp_steps.values():
                expo(0, j, c)
            for u in range(UNITS):
                for g in range(NG):
                    high(u, g)
                    if g in exp_late:
                        expo(u, *exp_late[g])
                    if g in exp_steps and u + 1 < UNITS:
                        expo(u + 1, *exp_steps[g])
                    if g == 7 and u and u % HALVES == 0:
                        alphas(u // HALVES - 1)
                acc_b(u)
            alphas(PAIRS - 1)
            act.wait_ge(alpha_ready, PAIRS)
            act.copy(accb[:, 0:1], accb[:, 1:2]).then_inc(cross_act, 1)

            def h_turn(n):
                l, t = place(n)
                act.wait_ge(f_yT, n + 1)
                if n == 0:
                    act.wait_ge(setup_f, 1)
                c = WIN + t * P
                act.copy(hT[l][0:HD, c:c + P], psum[0:HD, 0, 0:P]).then_inc(f_hTa, 1)

            def qkv_move(n):
                act.wait_ge(f_qkv, n + 1)
                if n:
                    act.wait_ge(f_rab, n)
                act.copy(qk[:, :, :, :], psum[:, 0:2, :].rearrange("p k (h d) -> p k h d", h=H)).then_inc(f_qk_moved, 1)
                if n:
                    act.wait_ge(f_ss, n)
                act.wait_ge(f_qk_moved, n + 1)
                act.activation(sq[:, :, :], qk[:, :, :, :].rearrange("p k h d -> p (k h) d"), ACT.Square).then_inc(f_sq, 1)
                if n >= 3:
                    act.wait_ge(a_o, 2 * (n - 2))
                    act.wait_ge(f_vp[n % 3], 16 * (n // 3))
                act.copy(v_sb[:, n % 3, :], psum[:, 2, :]).then_inc(f_v_moved, 1)

            def qk_turned(n):
                l, t = place(n)
                act.wait_ge(f_turn, 2 * n + 1)
                if n >= 2:
                    act.wait_ge(a_s, 2 * (n - 1))
                act.copy(qTh[:, n % 2, :, :], psum[:, 0, :].rearrange("p (a t) -> p a t", t=P)).then_inc(f_turned, 1)
                act.wait_ge(f_turn, 2 * n + 2)
                if n >= NT:
                    act.wait_ge(a_s, 2 * (n - NT + 2) if n - NT + 1 < NT else 2 * NT)
                c = WIN + t * P
                act.copy(kTh[:, :, c:c + P], psum[:, 1, :].rearrange("p (a t) -> p a t", t=P)).then_inc(f_turned, 1)

            def probs(n, hg):
                i = 2 * n + hg
                act.wait_ge(a_nb, i + 1)
                if i >= 2:
                    act.wait_ge(a_t, i - 1)
                for e in range(H // 2):
                    hd = hg * (H // 2) + e
                    m = act.activation(prob[:, hg, e, :],
                                       psum[:, 3 + e % 2, (e // 2) * (WIN + P):(e // 2 + 1) * (WIN + P)],
                                       ACT.Exp, bias=nb[:, n % 2, hd:hd + 1], scale=r8[:, n % 3, hd:hd + 1],
                                       accum_out=z[:, n % 2, hd:hd + 1])
                m.then_inc(a_p, 1)

            def turned_a(n, hg):
                i = 2 * n + hg
                act.wait_ge(a_t, i + 1)
                if i:
                    act.wait_ge(a_o, i)
                act.copy(ptA[:, :, :], psum[:, 5, :].rearrange("p (a t) -> p a t", t=P)).then_inc(a_tA, 1)

            def o_turned(n):
                act.wait_ge(a_oT, n + 1)
                if n:
                    act.wait_ge(a_wo, n)
                act.copy(oT[:, :, :], psum[:, 5, :].rearrange("p (a t) -> p a t", t=P)).then_inc(a_oTm, 1)

            def feed_act(l, g):
                k = l * (NT // GT) + g
                act.wait_ge(m_sh, k + 1)
                act.copy(h2[:, :, HD:D], psum[:, 5, 0:GT * HD].rearrange("p (s d) -> p s d", d=HD)).then_inc(m_h2, 1)
                act.wait_ge(m_hT, k + 1)
                act.activation(h2T[:, :], psum[:, 5, :], ACT.Identity, bias=lnc[:, 1, l:l + 1],
                               scale=lnc[:, 0, l:l + 1]).then_inc(m_h2T, 1)
                for b, (c0, w) in enumerate(blk):
                    act.wait_ge(m_w1, 2 * NBLK * k + 2 * b + 1)
                    if k:
                        act.wait_ge(m_mid, k * NBLK)
                    act.activation(gl[0:w, b, :], psum[0:w, (3, 4, 6)[2 * b % 3], :], ACT.Gelu,
                                   bias=b1c[0:w, l, 1, b:b + 1]).then_inc(m_gelu, 1)

            h_turn(0)
            qkv_move(0)
            qk_turned(0)
            for n in range(N_UNITS + 1):
                more = n + 1 < N_UNITS
                if more:
                    h_turn(n + 1)
                if n < N_UNITS:
                    probs(n, 0)
                if n:
                    turned_a(n - 1, 1)
                if n < N_UNITS:
                    probs(n, 1)
                if more:
                    qkv_move(n + 1)
                if n:
                    o_turned(n - 1)
                if n < N_UNITS:
                    turned_a(n, 0)
                if more:
                    qk_turned(n + 1)
                if n and n % GT == 0:
                    feed_act(*divmod(n // GT - 1, NT // GT))

        @block.gpsimd
        def _(pool):
            pool.memset(minus_half[:, :], -0.5).then_inc(half_set, 1)
            pool.wait_ge(half_set, 1)
            for i in range(2):
                pool.wait_ge(var_ready, i + 1)
                pool.tensor_tensor(rstd[:, :, 0], rstd[:, :, 0], minus_half[:, 0:NT], ALU.pow).then_inc(rstd_ready, 1)

            def rotate(n):
                pool.wait_ge(f_ss, n + 1)
                if n >= 2:
                    pool.wait_ge(f_kn, n - 1)
                    pool.wait_ge(f_r8, n - 1)
                pool.tensor_tensor(rinv[:, n % 2, :], ss[:, :], minus_half[:, :], ALU.pow).then_inc(f_rinv, 1)
                pool.wait_ge(f_rab, n + 1)
                pool.tensor_tensor(ra[:, :, :, :], ra[:, :, :, :], rb[:, :, :, :], ALU.add).then_inc(f_rsum, 1)

            def feed_pool(k):
                pool.wait_ge(m_var, k + 1)
                pool.tensor_tensor(frs[:, :], fve[:, :], minus_half[:, 0:GT], ALU.pow).then_inc(m_rs, 1)

            rotate(0)
            for n in range(N_UNITS + 1):
                if n + 1 < N_UNITS:
                    rotate(n + 1)
                if n and n % GT == 0:
                    feed_pool(n // GT - 1)

        @block.vector
        def _(dve):
            links = [0]

            def link(ins):
                links[0] += 1
                ins.then_inc(dve_link, 1)
                dve.wait_ge(dve_link, links[0])

            def norm_x(i, dst):
                for t in range(NT):
                    m = dve.bn_stats(stats[:, t, :], x_sb[:, t, :])
                link(m)
                for t in range(NT):
                    m = dve.bn_aggr(mv[:, t, :], stats[:, t, :])
                link(m)
                dve.tensor_scalar(rstd[:, :, :], mv[:, :, 1:2], EPS, None, ALU.add).then_inc(var_ready, 1)
                dve.wait_ge(rstd_ready, i + 1)
                for t in range(NT):
                    m = dve.tensor_scalar(dst[:, t, :], x_sb[:, t, :], mv[:, t, 0:1], rstd[:, t, 0:1],
                                          ALU.subtract, ALU.mult)
                return m

            dve.wait_ge(ld_x, 16)
            norm_x(0, y_sb[0]).then_inc(xn_ready, 1)
            dve.wait_ge(ld_b, 48)
            dve.tensor_copy(bvr[:, :], bvc[:, 0:1].broadcast_to([P, P])).then_inc(pre_dve, 1)
            dve.wait_ge(pre_act, 4)
            dve.tensor_tensor(qh[:, 1, :], psum[:, 5:7, :], qh[:, 0, :].bitcast(F32), ALU.subtract).then_inc(pre_dve, 1)
            dve.wait_ge(pre_pe, 5)
            link(dve.tensor_tensor(bob[:, :], psum[:, 7, 0:P], bob[:, :], ALU.add))
            dve.wait_ge(xn_ready, 1)
            for t in range(NT):
                m = dve.tensor_tensor(x_sb[:, t, :], x_sb[:, t, :], bob[:, :], ALU.add)
            m.then_inc(pre_dve, 1)
            n_ct = (KT + 1 + 3) // 4
            for i in range(n_ct):
                c0, w = 512 * i, min(512, NKEYS - 512 * i)
                dve.wait_ge(ct_high, i + 1)
                dve.tensor_tensor(keyT[:, 1, c0:c0 + w], psum[:, 1 + i % 2, 0:w], keyT[:, 0, c0:c0 + w].bitcast(F32),
                                  ALU.subtract).then_inc(ct_low, 1)
            for s in ld_c:
                dve.wait_ge(s, 16)
            dve.wait_ge(ld_t, 16)
            dve.tensor_copy(vals[:, 0, 0:KT, :], raw).then_inc(vh_ready, 1)
            dve.tensor_copy(vals[0:TAIL, 0, KT, :], rawt[0:TAIL, :]).then_inc(vh_ready, 1)
            dve.wait_ge(vh_ready, 2)
            dve.tensor_tensor(vals[:, 1, 0:KT, :], raw, vals[:, 0, 0:KT, :].bitcast(F32), ALU.subtract).then_inc(vl_ready, 1)
            dve.tensor_tensor(vals[0:TAIL, 1, KT, :], rawt[0:TAIL, :], vals[0:TAIL, 0, KT, :].bitcast(F32),
                              ALU.subtract).then_inc(vl_ready, 1)
            dve.wait_ge(vl_ready, 2)

            def move_scores(u, j, c):
                h = u % HALVES
                k = (u * 2 + j) * CH + c
                c0, w0, w1_ = chunks[h][c]
                dve.wait_ge(scores_ready, k + 1)
                if u >= HALVES:
                    dve.wait_ge(ring_done, at["T", u - HALVES, NG - 1] + 1)
                if w0 == w1_:
                    dve.tensor_scalar(S[:, h, j, c0:c0 + 2 * w0].rearrange("p (a b) -> p a b", a=2),
                                      psum[:, 2 * (k % 2):2 * (k % 2) + 2, 0:w0], SCALE, None, ALU.mult, ALU.max,
                                      accum_out=cmax[:, u, j, c:c + 1]).then_inc(scores_moved, 1)
                    dve.wait_ge(scores_moved, k + 1)
                else:
                    link(dve.tensor_scalar(S[:, h, j, c0:c0 + w0], psum[:, 2 * (k % 2), 0:w0], SCALE, None, ALU.mult,
                                           ALU.max, accum_out=cmax[:, u, j, c:c + 1]))
                    dve.tensor_scalar(S[:, h, j, c0 + w0:c0 + w0 + w1_], psum[:, 2 * (k % 2) + 1, 0:w1_], SCALE,
                                      cmax[:, u, j, c:c + 1], ALU.mult, ALU.max,
                                      accum_out=cmax[:, u, j, c:c + 1]).then_inc(scores_moved, 1)
                    dve.wait_ge(scores_moved, k + 1)
                if c == CH - 1:
                    link(dve.tensor_reduce(nmax[:, u, j:j + 1], cmax[:, u, j, :], AX_X, ALU.max))
                    dve.tensor_scalar(nmax[:, u, j:j + 1], nmax[:, u, j:j + 1], -1.0, None, ALU.mult).then_inc(max_ready, 1)

            def low(u, g):
                i = at["T", u, g]
                k = u * NG + g
                dve.wait_ge(high_ready, k + 1)
                tiles = group(u % HALVES, g)
                if all(r == P for _, r, _ in tiles):
                    w = len(tiles)
                    dve.tensor_tensor(turned[:, k % RING, 0:w, 1, :],
                                      psum[:, 4 + i % 2, 0:256 * w].rearrange("p (a b) -> p a b", b=256),
                                      turned[:, k % RING, 0:w, 0, :].bitcast(F32), ALU.subtract).then_inc(ring_done, 1)
                else:
                    for s, (_, r, _) in enumerate(tiles):
                        m = dve.tensor_tensor(turned[0:r, k % RING, s, 1, :], psum[0:r, 4 + i % 2, 256 * s:256 * (s + 1)],
                                              turned[0:r, k % RING, s, 0, :].bitcast(F32), ALU.subtract)
                    m.then_inc(ring_done, 1)

            def acc_a(u):
                dve.wait_ge(accb_ready, u + 1)
                if u:
                    dve.wait_ge(ring_ready, at["C", u - 1, 0] + 1)
                link(dve.tensor_tensor(uT[:, :], psum[:, 6, 0:256], accb[:, :], ALU.add))
                dve.tensor_tensor(uT[:, :], psum[:, 6, 256:512], uT[:, :], ALU.add).then_inc(acc_read, 1)

            def c_out(u):
                dve.wait_ge(ring_ready, at["C", u, 0] + 1)
                dve.tensor_copy(cT[:, :], psum[:, 4 + at["C", u, 0] % 2, 0:256]).then_inc(ring_done, 1)

            def o_out(u):
                dve.wait_ge(ring_ready, at["O", u, 0] + 1)
                dve.tensor_copy(oh[:, u % HALVES, :, :],
                                psum[:, 4 + at["O", u, 0] % 2, 0:256].rearrange("p (j d) -> p j d", d=D)).then_inc(ring_done, 1)

            def merge_in(p):
                u0, u1 = HALVES * p, HALVES * p + 1
                if p:
                    dve.wait_ge(alpha_ready, p)
                link(dve.tensor_tensor(mmin[:, :], nmax[:, u0, :], nmax[:, u1, :], ALU.min))
                for h, u in ((0, u0), (1, u1)):
                    m = dve.tensor_tensor(al[:, h, :], mmin[:, :], nmax[:, u, :], ALU.subtract)
                m.then_inc(alpha_in, 1)

            def merge(p):
                u0, u1 = HALVES * p, HALVES * p + 1
                dve.wait_ge(alpha_ready, p + 1)
                for h, u in ((0, u0), (1, u1)):
                    dve.wait_ge(prob_ready, exp_at[u, 1, CH - 1] + 1)
                    m = dve.tensor_reduce(zs[:, h, :], zpart[:, u, :, :], AX_X, ALU.add)
                link(m)
                link(dve.tensor_tensor(zs[:, :, :], zs[:, :, :], al[:, :, :], ALU.mult))
                link(dve.tensor_tensor(zt[:, :], zs[:, 0, :], zs[:, 1, :], ALU.add))
                link(dve.reciprocal(zt[:, :], zt[:, :]))
                for j in range(2):
                    m = dve.tensor_scalar(al[:, :, j], al[:, :, j], zt[:, j:j + 1], None, ALU.mult)
                link(m)
                dve.wait_ge(ring_done, at["O", u1, 0] + 1)
                for j in range(2):
                    m = dve.scalar_tensor_tensor(x_sb[:, 2 * p + j, :], oh[:, 0, j, :], al[:, 0, j:j + 1],
                                                 x_sb[:, 2 * p + j, :], ALU.mult, ALU.add)
                link(m)
                for j in range(2):
                    m = dve.scalar_tensor_tensor(x_sb[:, 2 * p + j, :], oh[:, 1, j, :], al[:, 1, j:j + 1],
                                                 x_sb[:, 2 * p + j, :], ALU.mult, ALU.add)
                link(m)

            for j in range(2):
                for c in range(CH):
                    move_scores(0, j, c)
            for u in range(UNITS):
                for g in range(NG):
                    low(u, g)
                    if u and g == 3:
                        c_out(u - 1)
                    if u and g == 6:
                        o_out(u - 1)
                        if u % HALVES == 0:
                            merge_in(u // HALVES - 1)
                    if g == 8 and u and u % HALVES == 0:
                        merge(u // HALVES - 1)
                    if g in SC_STEP and u + 1 < UNITS:
                        move_scores(u + 1, *divmod(SC_STEP[g], CH))
                acc_a(u)
            c_out(UNITS - 1)
            o_out(UNITS - 1)
            merge_in(PAIRS - 1)
            merge(PAIRS - 1)
            norm_x(1, y_sb[0]).then_inc(y0_ready, 1)

            dve.wait_ge(y0_ready, 1)
            dve.wait_ge(cross_pe, 1)
            dve.wait_ge(cross_act, 1)
            for l in range(DEPTH):
                m = dve.memset(hT[l][:, 0:WIN + 1], 0.0)
            link(dve.memset(kTh[:, :, 0:WIN], 0.0))
            dve.memset(ones_row[:, :], 1.0).then_inc(setup_f, 1)
            dve.tensor_copy(ident_r[:, :], ident)
            dve.wait_ge(ld_g, 16 * G_LOADS)
            link(dve.tensor_copy(mask_r[:, :, :], mask[:, :, :]))
            hh = HD // 2
            for l in range(DEPTH):
                for k in range(2):
                    dve.tensor_tensor(rotl[:, l, :, 0, k, :], rot[:, :, 0, k, :],
                                      sc_b[:, k, l, :].unsqueeze(1).broadcast_to([P, NT, HD]), ALU.mult)
                    for e in range(2):
                        m = dve.tensor_tensor(rotl[:, l, :, 1, k, e * hh:(e + 1) * hh],
                                              rot[:, :, 1, k, e * hh:(e + 1) * hh],
                                              sc_b[:, k, l, (1 - e) * hh:(2 - e) * hh].unsqueeze(1).broadcast_to([P, NT, hh]),
                                              ALU.mult)
            m.then_inc(setup_f, 1)
            dve.wait_ge(setup_f, 2)

            def h_turn(n):
                l, t = place(n)
                dve.wait_ge(f_yT, n + 1)
                c = WIN + 1 + t * P
                dve.tensor_copy(hT[l][HD:D, c:c + P], psum[HD:D, 0, 0:P]).then_inc(f_hTb, 1)

            def rotate(n):
                l, t = place(n)
                dve.wait_ge(f_qk_moved, n + 1)
                if n:
                    dve.wait_ge(f_turn, 2 * n - 1)
                for k in range(2):
                    dve.tensor_tensor(ra[:, k, :, :], qk[:, k, :, :],
                                      rotl[:, l, t, 0, k, :].unsqueeze(1).broadcast_to([P, H, HD]), ALU.mult)
                    for e in range(2):
                        m = dve.tensor_tensor(rb[:, k, :, e * hh:(e + 1) * hh], qk[:, k, :, (1 - e) * hh:(2 - e) * hh],
                                              rotl[:, l, t, 1, k, e * hh:(e + 1) * hh].unsqueeze(1).broadcast_to([P, H, hh]),
                                              ALU.mult)
                m.then_inc(f_rab, 1)
                dve.wait_ge(f_sq, n + 1)
                if n:
                    dve.wait_ge(f_rinv, n)
                link(dve.tensor_reduce(ss[:, :], sq[:, :, :], AX_X, ALU.add))
                dve.tensor_scalar(ss[:, :], ss[:, :], 1e-24, None, ALU.max).then_inc(f_ss, 1)

            def key_norm(n):
                dve.wait_ge(f_rinv, n + 1)
                if n >= 3:
                    dve.wait_ge(a_p, 2 * (n - 2))
                dve.tensor_scalar(r8[:, n % 3, :], rinv[:, n % 2, 0:H], QK_SCALE, None, ALU.mult).then_inc(f_r8, 1)
                dve.wait_ge(f_rsum, n + 1)
                if n:
                    dve.wait_ge(f_turn, 2 * n)
                dve.tensor_tensor(kn[:, :, :], ra[:, 1, :, :],
                                  rinv[:, n % 2, H:2 * H].unsqueeze(2).broadcast_to([P, H, HD]), ALU.mult).then_inc(f_kn, 1)

            def maxima(n, hg):
                i = 2 * n + hg
                dve.wait_ge(a_s, i + 1)
                q = H // 2
                if i >= 4:
                    dve.wait_ge(a_p, i - 3)
                link(dve.tensor_reduce(mx[:, hg * q:(hg + 1) * q].rearrange("p (e b) -> p b e", b=2),
                                       psum[:, 3:5, 0:2 * (WIN + P)].rearrange("p a (h k) -> p a h k", h=2), AX_X, ALU.max))
                dve.wait_ge(f_r8, n + 1)
                dve.scalar_tensor_tensor(nb[:, n % 2, hg * q:(hg + 1) * q], mx[:, hg * q:(hg + 1) * q], -1.0,
                                         r8[:, n % 3, hg * q:(hg + 1) * q], ALU.mult, ALU.mult).then_inc(a_nb, 1)

            def turned_b(n, hg):
                i = 2 * n + hg
                l, t = place(n)
                if t:
                    dve.wait_ge(a_t, i + 1)
                    dve.wait_ge(a_o, i)
                    dve.tensor_copy(ptB[:, :, :], psum[0:WIN, 6, 0:H // 2 * WIN].rearrange("p (a t) -> p a t", t=WIN))\
                       .then_inc(a_tB, 1)

            def o_norm(n):
                dve.wait_ge(a_p, 2 * n + 2)
                link(dve.reciprocal(rz[:, :], z[:, n % 2, :]))
                dve.wait_ge(a_o, 2 * n + 2)
                if n:
                    dve.wait_ge(a_oT, n)
                dve.tensor_tensor(o_sb[:, :, :], psum[:, 7, :].rearrange("p (h d) -> p h d", h=H),
                                  rz[:, :].unsqueeze(2).broadcast_to([P, H, HD]), ALU.mult).then_inc(a_on, 1)

            def add_att(n):
                l, t = place(n)
                dve.wait_ge(a_wo, n + 1)
                dve.tensor_tensor(y1[l][:, t, :], psum[:, 6, 0:D], y_sb[l][:, t, :], ALU.add).then_inc(a_y1, 1)

            def feed_dve(l, g):
                k = l * (NT // GT) + g
                ts = slice(g * GT, (g + 1) * GT)
                dve.wait_ge(a_y1, l * NT + (g + 1) * GT)
                link(dve.tensor_copy(h2[:, :, 0:HD], y1[l][:, ts, 0:HD]))
                dve.wait_ge(m_h2, k + 1)
                for s in range(GT):
                    m = dve.bn_stats(fstats[:, s, :], h2[:, s, :])
                link(m)
                for s in range(GT):
                    m = dve.bn_aggr(fmv[:, s, :], fstats[:, s, :])
                link(m)
                dve.tensor_scalar(fve[:, :], fmv[:, :, 1], EPS, None, ALU.add).then_inc(m_var, 1)
                dve.wait_ge(m_rs, k + 1)
                for s in range(GT):
                    m = dve.tensor_scalar(hn[:, s, :], h2[:, s, :], fmv[:, s, 0:1], frs[:, s:s + 1],
                                          ALU.subtract, ALU.mult)
                m.then_inc(m_hn, 1)
                for b, (c0, w) in enumerate(blk):
                    dve.wait_ge(m_gelu, k * NBLK + b + 1)
                    dve.wait_ge(m_w1, 2 * NBLK * k + 2 * b + 2)
                    dve.scalar_tensor_tensor(mid[0:w, b, :], psum[0:w, (3, 4, 6)[(2 * b + 1) % 3], :],
                                             b1c[0:w, l, 0, b:b + 1], gl[0:w, b, :], ALU.add, ALU.mult).then_inc(m_mid, 1)
                dve.wait_ge(m_w2, k + 1)
                if l + 1 < DEPTH:
                    dve.tensor_tensor(y_sb[l + 1][:, ts, :], psum[:, 5, :].rearrange("p (s d) -> p s d", d=D),
                                      y1[l][:, ts, :], ALU.add).then_inc(m_y, 1)
                    dve.wait_ge(m_y, k + 1)
                else:
                    dve.tensor_tensor(hn[:, :, :], psum[:, 5, :].rearrange("p (s d) -> p s d", d=D),
                                      y1[l][:, ts, :], ALU.add).then_inc(m_y, 1)
                    dve.wait_ge(m_y, k + 1)
                    dve.tensor_tensor(x_sb[:, ts, :], x_sb[:, ts, :], hn[:, :, :], ALU.add).then_inc(x_out, 1)

            h_turn(0)
            rotate(0)
            key_norm(0)
            for n in range(N_UNITS + 1):
                more = n + 1 < N_UNITS
                if n < N_UNITS:
                    maxima(n, 0)
                if more:
                    h_turn(n + 1)
                if n:
                    turned_b(n - 1, 1)
                    o_norm(n - 1)
                if n < N_UNITS:
                    maxima(n, 1)
                if n:
                    add_att(n - 1)
                if n < N_UNITS:
                    turned_b(n, 0)
                if more:
                    rotate(n + 1)
                    key_norm(n + 1)
                if n and n % GT == 0:
                    feed_dve(*divmod(n // GT - 1, NT // GT))


_INS = ['x', 'ctx_1024', 'L0_xattn_Wk', 'L0_xattn_Wv', 'L0_xattn_bv', 'L0_xattn_Wq', 'L0_xattn_bq', 'L0_xattn_Wo',
        'L0_xattn_bo', 'L0_ffn_wqkv', 'L0_ffn_q_scale', 'L0_ffn_k_scale', 'L0_ffn_wo', 'L0_ffn_ln_g', 'L0_ffn_ln_b',
        'L0_ffn_w1', 'L0_ffn_b1', 'L0_ffn_w2', 'L0_ffn_b2']
_OUTS = [((1, 1024, 128), 'float32')]


def kernel(**inputs):
    import numpy as _np
    import concourse.bacc as _bacc
    from concourse import mybir as _mybir
    from concourse.bass_utils import run_bass_kernel_spmd as _run

    nc = _bacc.Bacc("TRN2", target_bir_lowering=False, num_devices=1)
    arrays, args = {}, []
    given = {name: _np.ascontiguousarray(inputs[name]) for name in _INS}
    rot, mask, mats = shape_constants(1024, 64, 64)
    given.update(rot_tab=rot, mask_tab=mask, mats=mats)
    for name, a in given.items():
        arrays[f"in_{name}_dram"] = a
        args.append(nc.dram_tensor(f"in_{name}_dram", a.shape, _mybir.dt.from_np(a.dtype), kind="ExternalInput").ap())
    for i, (shape, dtype) in enumerate(_OUTS):
        dt = _mybir.dt.from_np(_np.dtype(dtype))
        args.append(nc.dram_tensor(f"out_{i}_dram", shape, dt, kind="ExternalOutput").ap())
    xattn_ffn_kernel(nc, *args)
    r = _run(nc, [arrays], core_ids=[0])
    got = tuple(r.results[0][f"out_{i}_dram"] for i in range(len(_OUTS)))
    return got[0]
```

```python
from contextlib import ExitStack

import numpy as np

import concourse.bass as bass
from concourse import mybir

ALU = mybir.AluOpType
ACT = mybir.ActivationFunctionType
AX_X = mybir.AxisListType.X
F32 = mybir.dt.float32
F32R = mybir.dt.float32r

P = 128
MASKED = -1e30


class Shapes:

    def __init__(self, x, ctx, w1):
        _, self.n, self.d = x.shape
        _, self.keys, _ = ctx.shape
        self.tiles = self.n // P
        self.ktiles = self.keys // P
        self.tail = self.keys - self.ktiles * P
        self.hid = w1.shape[2] // 2


def shape_constants(n, heads_dim, window):
    half = np.arange(0, heads_dim, 2, dtype=np.float32)
    inv_freq = (1.0 / 10000.0 ** (half / np.float32(heads_dim))).astype(np.float32)
    t = np.arange(n, dtype=np.float32)
    freqs = t[:, None] * inv_freq[None, :]
    freqs = np.concatenate([freqs, freqs], axis=-1)
    base = ((half + np.float32(0.4 * heads_dim)) / np.float32(1.4 * heads_dim)).astype(np.float32)
    power = ((t - n // 2) / np.float32(window // 2)).astype(np.float32)
    scale = base[None, :] ** power[:, None]
    scale = np.concatenate([scale, scale], axis=-1)
    cos, sin = np.cos(freqs), np.sin(freqs)
    sign = np.where(np.arange(heads_dim) < heads_dim // 2, -1.0, 1.0).astype(np.float32)
    rot = np.stack([np.stack([cos * scale, cos / scale], 1),
                    np.stack([sin * scale * sign, sin / scale * sign], 1)], 1)
    rot = rot.reshape(n // P, P, 2 * 2 * heads_dim).transpose(1, 0, 2)
    i = np.arange(P)[:, None]
    j = np.arange(-window, P)[None, :]
    ok = (j <= i) & (i <= j + window) & (j // window >= i // window - 1)
    mask = np.stack([np.where(ok & (j >= 0), 0.0, MASKED), np.where(ok, 0.0, MASKED)], 1)
    ident = np.eye(P)
    down = np.eye(P, k=1)
    edge = np.zeros((P, P))
    edge[P - 1, 0] = 1.0
    mats = np.stack([ident, down, edge], 1)
    return (np.ascontiguousarray(rot, np.float32), np.ascontiguousarray(mask, np.float32),
            np.ascontiguousarray(mats, np.float32))


def xattn_ffn_kernel(nc, x, ctx_1024, Wk, Wv, bv, Wq, bq, Wo, bo,
                     wqkv, q_scale, k_scale, wo, ln_g, ln_b, w1, b1, w2, b2,
                     rot_tab, mask_tab, mats, out):
    sh = Shapes(x, ctx_1024, w1)
    D = sh.d
    NT, KT, TAIL, NKEYS = sh.tiles, sh.ktiles, sh.tail, sh.keys
    DEPTH = wqkv.shape[0]
    INNER = wqkv.shape[2] // 3
    HD = q_scale.shape[1]
    H = INNER // HD
    HID = sh.hid
    WIN = HD
    SCALE = float(1.0 / np.sqrt(np.float32(D)))
    QK_SCALE = 8.0
    EPS = 1e-5

    PAIRS = NT // 2
    HALVES = 2
    UNITS = PAIRS * HALVES
    HT_ = KT // HALVES
    half0 = [h * HT_ * P for h in range(HALVES)]
    hkeys = [HT_ * P, HT_ * P + TAIL]
    CH = 4
    CB = HT_ * P // (2 * CH)
    chunks = [[(c * 2 * CB, CB, CB + (TAIL if h == HALVES - 1 and c == CH - 1 else 0)) for c in range(CH)]
              for h in range(HALVES)]
    G = 2
    NG = (HT_ + G) // G
    SC_STEP = {g: g for g in range(2 * CH)}

    def group(h, g):
        tiles = [(i * P, P, h * HT_ + i) for i in range(HT_)]
        if h == HALVES - 1:
            tiles.append((HT_ * P, TAIL, KT))
        return tiles[G * g:G * g + G]

    ring = []
    for u in range(UNITS):
        for g in range(NG):
            ring.append(("T", u, g))
            if u and g == 3:
                ring.append(("C", u - 1, 0))
            if u and g == 6:
                ring.append(("O", u - 1, 0))
    ring += [("C", UNITS - 1, 0), ("O", UNITS - 1, 0)]
    at = {e: i for i, e in enumerate(ring)}
    exp_steps = {4: (0, 0), 6: (0, 1), 7: (0, 2), 8: (0, 3), 9: (1, 0), 11: (1, 1)}
    exp_late = {1: (1, 2), 3: (1, 3)}
    exps = [(0, j, c) for (j, c) in exp_steps.values()]
    for u in range(UNITS):
        for g in range(NG):
            if g in exp_late:
                exps.append((u, *exp_late[g]))
            if g in exp_steps and u + 1 < UNITS:
                exps.append((u + 1, *exp_steps[g]))
    exp_at = {e: i for i, e in enumerate(exps)}
    RING = 4

    N_UNITS = DEPTH * NT
    GT = 4
    NG_F = NT // GT
    NBLK = (HID + P - 1) // P
    VS = 4
    blk = [(b * P, min(P, HID - b * P)) for b in range(NBLK)]

    with ExitStack() as ctx:
        def sem(name):
            return ctx.enter_context(nc.semaphore(name))

        def sb(name, shape, dt=F32, stack=ctx):
            return stack.enter_context(nc.sbuf_tensor(name, shape, dt))

        psum = ctx.enter_context(nc.psum_tensor("psum", [P, 8, 512], F32))

        x_sb = sb("x_sb", [P, NT, D])
        y_sb = [sb(f"y{l}", [P, NT, D]) for l in range(DEPTH)]
        mat = sb("mat", [P, 3, P])
        ident, down, edge = mat[:, 0, :], mat[:, 1, :], mat[:, 2, :]
        stats = sb("stats", [P, NT, 6])
        mv = sb("mv", [P, NT, 2])
        rstd = sb("rstd", [P, NT, 1])
        minus_half = sb("minus_half", [P, 2 * H])

        first = ExitStack()
        with first:
            a = lambda name, shape, dt=F32: sb(name, shape, dt, first)
            keyT = a("keyT", [P, 2, NKEYS], F32R)
            vals = a("vals", [P, 2, KT + 1, D], F32R)
            S = a("S", [P, HALVES, 2, hkeys[-1]])
            turned = a("turned", [P, RING, G, 2, 2 * P], F32R)
            w4 = a("w4", [P, 4, D])
            wT = a("wT", [P, 3, D])
            qT = a("qT", [P, NT * P])
            qpT = a("qpT", [P, NT * P])
            qh = a("qh", [P, 2, NT * P], F32R)
            bqc = a("bqc", [P, 1])
            bvc = a("bvc", [P, 1])
            bvr = a("bvr", [P, P])
            bob = a("bob", [P, D])
            cmax = a("cmax", [P, UNITS, 2, CH])
            nmax = a("nmax", [P, UNITS, 2])
            zpart = a("zpart", [P, UNITS, 2, CH])
            accb = a("accb", [P, 2 * P])
            uT = a("uT", [P, 2 * P])
            cT = a("cT", [P, 2 * P])
            oh = a("oh", [P, HALVES, 2, D])
            mmin = a("mmin", [P, 2])
            al = a("al", [P, HALVES, 2])
            zs = a("zs", [P, HALVES, 2])
            zt = a("zt", [P, 2])
            raw = S[:, :, :, :].rearrange("p h j k -> p (h j k)")[:, 0:KT * D].rearrange("p (t d) -> p t d", d=D)
            rawt = a("rawt", [P, D])

        second = ExitStack()
        ctx.enter_context(second)
        f = lambda name, shape, dt=F32: sb(name, shape, dt, second)
        wqkv_sb = f("wqkv_sb", [P, DEPTH, 3 * INNER])
        wo_sb = f("wo_sb", [P, DEPTH, INNER // P, D])
        w1_sb = f("w1_sb", [P, DEPTH, 2 * HID])
        w2_sb = f("w2_sb", [P, DEPTH, NBLK, D])
        b1c = f("b1c", [P, DEPTH, 2, NBLK])
        b2r = f("b2r", [1, DEPTH, D])
        lnc = f("lnc", [P, 2, DEPTH])
        sc_b = f("sc_b", [P, 2, DEPTH, HD])
        ones_row = f("ones_row", [1, P])
        rot = f("rot", [P, NT, 2, 2, HD])
        rotl = f("rotl", [P, DEPTH, NT, 2, 2, HD])
        mask = f("mask", [P, 2, WIN + P])
        mask_r = f("mask_r", [P, 2, WIN + P], F32R)
        ident_r = f("ident_r", [P, P], F32R)
        hT = [f(f"hT{l}", [P, WIN + NT * P + 4]) for l in range(DEPTH)]
        qk = f("qk", [P, 2, H, HD])
        sq = f("sq", [P, 2 * H, HD])
        ra = f("ra", [P, 2, 2, H, HD])
        rb = f("rb", [P, 2, H, HD])
        ss = f("ss", [P, 2 * H])
        rinv = f("rinv", [P, 2, 2 * H])
        r8 = f("r8", [P, 3, H])
        kn = f("kn", [P, H, HD])
        qTh = f("qTh", [P, 2, H // 2, P])
        kTh = f("kTh", [P, H // 2, WIN + NT * P])
        v_sb = f("v_sb", [P, VS, INNER])
        v_prev = f("v_prev", [WIN, VS, INNER])
        mx = f("mx", [P, H])
        nb = f("nb", [P, 2, H])
        z = f("z", [P, 2, H])
        rz = f("rz", [P, H])
        prob = f("prob", [P, 2, H // 2, WIN + P])
        ptA = f("ptA", [P, 2, H // 2, P])
        ptB = f("ptB", [WIN, 2, H // 2, WIN])
        o_sb = f("o_sb", [P, H, HD])
        oT = f("oT", [P, INNER // P, P])
        y1 = [f(f"yatt{l}", [P, NT, D]) for l in range(DEPTH)]
        h2 = f("h2", [P, GT, D])
        hn = f("hn", [P, GT, D])
        fstats = f("fstats", [P, GT, 6])
        fmv = f("fmv", [P, GT, 2])
        fve = f("fve", [P, GT])
        frs = f("frs", [P, GT])
        last = f("last", [P, GT, D])
        h2T = f("h2T", [P, GT * P])
        gl = f("gl", [P, NBLK, GT * P])
        mid = f("mid", [P, NBLK, GT * P])

        ld_x, ld_w, ld_t, ld_m, ld_b = (sem(s) for s in ("ld_x", "ld_w", "ld_t", "ld_m", "ld_b"))
        LOADS = 5
        ld_c = [sem(f"ld_c{i}") for i in range(LOADS)]
        stored = sem("stored")
        ld_f, ld_g = sem("ld_f"), sem("ld_g")
        half_set = sem("half_set")
        dve_link, act_link, pool_link = sem("dve_link"), sem("act_link"), sem("pool_link")
        var_ready, rstd_ready, xn_ready = sem("var_ready"), sem("rstd_ready"), sem("xn_ready")
        pre_pe, pre_act = sem("pre_pe"), sem("pre_act")
        pre_dve = sem("pre_dve")
        ct_ready, ct_high, ct_low = sem("ct_ready"), sem("ct_high"), sem("ct_low")
        vh_ready, vl_ready = sem("vh_ready"), sem("vl_ready")
        scores_ready, scores_moved = sem("scores_ready"), sem("scores_moved")
        max_ready, prob_ready = sem("max_ready"), sem("prob_ready")
        ring_ready, high_ready, ring_done = sem("ring_ready"), sem("high_ready"), sem("ring_done")
        pv_done, accb_ready, acc_read = sem("pv_done"), sem("accb_ready"), sem("acc_read")
        alpha_in, alpha_ready = sem("alpha_in"), sem("alpha_ready")
        y0_ready = sem("y0_ready")
        x_out = sem("x_out")
        cross_pe, cross_act = sem("cross_pe"), sem("cross_act")
        setup_f = sem("setup_f")
        f_yT, f_hT, f_q, f_k, f_v, f_q_moved, f_k_moved, f_v_moved = (
            sem(s) for s in ("f_yT", "f_hT", "f_q", "f_k", "f_v", "f_q_moved", "f_k_moved", "f_v_moved"))
        f_vp = [sem(f"f_vp{i}") for i in range(VS)]
        f_sq, f_ss, f_rinv, f_rab, f_rsum, f_kn, f_r8 = (
            sem(s) for s in ("f_sq", "f_ss", "f_rinv", "f_rab", "f_rsum", "f_kn", "f_r8"))
        f_qT, f_kT, f_qT_moved, f_kT_moved = (sem(s) for s in ("f_qT", "f_kT", "f_qT_moved", "f_kT_moved"))
        a_s, a_nb, a_p, a_t, a_tb, a_tA, a_tB, a_o, a_on, a_oT, a_oTm, a_wo, a_y1 = (
            sem(s) for s in ("a_s", "a_nb", "a_p", "a_t", "a_tb", "a_tA", "a_tB", "a_o", "a_on", "a_oT", "a_oTm",
                             "a_wo", "a_y1"))
        m_left = sem("m_left")
        m_sh, m_h2, m_var, m_rs, m_hn, m_hT, m_h2T, m_w1, m_gelu, m_mid, m_w2, m_y = (
            sem(s) for s in ("m_sh", "m_h2", "m_var", "m_rs", "m_hn", "m_hT", "m_h2T", "m_w1", "m_gelu",
                             "m_mid", "m_w2", "m_y"))
        block = ctx.enter_context(nc.Block())

        x_tok = x.rearrange("a (t p) d -> p (a t) d", p=P)
        out_tok = out.rearrange("a (t p) d -> p (a t) d", p=P)
        ctx_whole = ctx_1024[0, 0:KT * P, :].rearrange("(p t) d -> p t d", p=P)
        piece = KT // LOADS

        FFN_LOADS = 3 + DEPTH * (3 * NBLK + 2) + 1
        G_LOADS = 2 + 2 * DEPTH

        @block.sync
        def _(sp):
            sp.dma_start(x_sb[:, :, :], x_tok).then_inc(ld_x, 16)
            sp.dma_start(mat[:, :, :], mats).then_inc(ld_m, 16)
            for i, w in enumerate((Wq, Wk, Wv, Wo)):
                sp.dma_start(w4[:, i, :], w).then_inc(ld_w, 16)
            sp.dma_start(bqc[:, :], bq.rearrange("(p a) -> p a", a=1)).then_inc(ld_b, 16)
            sp.dma_start(bvc[:, :], bv.rearrange("(p a) -> p a", a=1)).then_inc(ld_b, 16)
            sp.dma_start(bob[:, :], bo.rearrange("(a d) -> a d", a=1).broadcast_to([P, D])).then_inc(ld_b, 16)
            for i in range(LOADS):
                sp.dma_start(raw[:, i * piece:(i + 1) * piece, :],
                             ctx_whole[:, i * piece:(i + 1) * piece, :]).then_inc(ld_c[i], 16)
            sp.dma_start(rawt[0:TAIL, :], ctx_1024[0, KT * P:NKEYS, :]).then_inc(ld_t, 16)

            sp.wait_ge(cross_pe, 1)
            sp.wait_ge(y0_ready, 1)
            sp.wait_ge(cross_act, 1)
            sp.dma_start(wqkv_sb[:, :, :], wqkv.rearrange("l p n -> p l n")).then_inc(ld_f, 16)
            sp.dma_start(rot[:, :, :, :, :], rot_tab.rearrange("p t (c k d) -> p t c k d", c=2, k=2)).then_inc(ld_g, 16)
            for i, s in enumerate((q_scale, k_scale)):
                for l in range(DEPTH):
                    sp.dma_start(sc_b[:, i, l, :], s[l:l + 1, :].broadcast_to([P, HD])).then_inc(ld_g, 16)
            sp.dma_start(mask[:, :, :], mask_tab).then_inc(ld_g, 16)
            sp.dma_start(wo_sb[:, :, :, :], wo.rearrange("l (c p) n -> p l c n", p=P)).then_inc(ld_f, 16)
            sp.dma_start(w1_sb[:, :, :], w1.rearrange("l p n -> p l n")).then_inc(ld_f, 16)
            n_f = 3
            for l in range(DEPTH):
                for b, (c0, w) in enumerate(blk):
                    sp.dma_start(w2_sb[0:w, l, b, :], w2[l, c0:c0 + w, :]).then_inc(ld_f, 16)
                    for k in range(2):
                        sp.dma_start(b1c[0:w, l, k, b:b + 1],
                                     b1[l, k * HID + c0:k * HID + c0 + w].rearrange("(p a) -> p a", a=1)).then_inc(ld_f, 16)
                        n_f += 1
                    n_f += 1
                sp.dma_start(lnc[:, 0, l:l + 1], ln_g[l, :].rearrange("(p a) -> p a", a=1)).then_inc(ld_f, 16)
                sp.dma_start(lnc[:, 1, l:l + 1], ln_b[l, :].rearrange("(p a) -> p a", a=1)).then_inc(ld_f, 16)
                n_f += 2
            sp.dma_start(b2r[:, :, :], b2.rearrange("(a l) d -> a l d", a=1)).then_inc(ld_f, 16)
            assert n_f + 1 == FFN_LOADS

            for n in range(N_UNITS):
                sp.wait_ge(f_v_moved, n + 1)
                if n >= VS:
                    sp.wait_ge(a_o, 2 * (n - VS + 2))
                sp.dma_start(v_prev[:, n % VS, :], v_sb[WIN:2 * WIN, n % VS, :]).then_inc(f_vp[n % VS], 16)
            for g in range(NT // GT):
                sp.wait_ge(x_out, g + 1)
                sp.dma_start(out_tok[:, g * GT:(g + 1) * GT, :], x_sb[:, g * GT:(g + 1) * GT, :]).then_inc(stored, 16)
            sp.wait_ge(stored, 16 * (NT // GT))


        def three(pe, o, lh, ll, rh, rl):
            pe.matmul(o, lh, rh, start=True, stop=False)
            pe.matmul(o, lh, rl, start=False, stop=False)
            return pe.matmul(o, ll, rh, start=False, stop=True)

        def cross_tensor(pe):
            pe.wait_ge(ld_w, 64)
            pe.wait_ge(ld_m, 16)
            for i, k in enumerate((0, 2, 3)):
                m = pe.transpose(psum[:, 0, i * P:(i + 1) * P], w4[:, k, :], ident)
            m.then_inc(pre_pe, 1)
            pe.wait_ge(xn_ready, 1)
            for t in range(NT):
                m = pe.transpose(psum[:, 1 + t // 4, (t % 4) * P:(t % 4 + 1) * P], y_sb[0][:, t, :], ident)
            m.then_inc(pre_pe, 1)
            pe.wait_ge(pre_act, 2)
            for b in range(NT // 4):
                m = pe.matmul(psum[:, 3 + b, :], wT[:, 0, :], qT[:, b * 512:(b + 1) * 512], start=True, stop=True)
            m.then_inc(pre_pe, 1)
            pe.wait_ge(pre_act, 3)
            for b in range(NT // 4):
                m = pe.matmul(psum[:, 5 + b, :], w4[:, 1, :], qpT[:, b * 512:(b + 1) * 512], start=True, stop=True)
            m.then_inc(pre_pe, 1)
            pe.wait_ge(pre_dve, 1)
            m = pe.matmul(psum[:, 7, 0:P], bvr[:, :], wT[:, 2, :], start=True, stop=True)
            m.then_inc(pre_pe, 1)
            for i in range((KT + 1 + 3) // 4):
                if i == 0:
                    pe.wait_ge(pre_act, 2)
                if i >= 2:
                    pe.wait_ge(ct_low, i - 1)
                for t in range(4 * i, min(4 * i + 4, KT + 1)):
                    if t < KT:
                        pe.wait_ge(ld_c[t // piece], 16)
                        m = pe.transpose(psum[:, 1 + i % 2, (t % 4) * P:(t % 4 + 1) * P], raw[:, t, :], ident)
                    else:
                        pe.wait_ge(ld_t, 16)
                        m = pe.transpose(psum[:, 1 + i % 2, (t % 4) * P:(t % 4) * P + TAIL], rawt[0:TAIL, :],
                                         ident[0:TAIL, 0:TAIL])
                m.then_inc(ct_ready, 1)
            n_ct = (KT + 1 + 3) // 4

            def scores(u, j, c):
                p, h = divmod(u, HALVES)
                k = (u * 2 + j) * CH + c
                c0, *widths = chunks[h][c]
                if k >= 2:
                    pe.wait_ge(scores_moved, k - 1)
                rows = slice((2 * p + j) * P, (2 * p + j + 1) * P)
                for b, w in enumerate(widths):
                    cols = slice(half0[h] + c0 + b * CB, half0[h] + c0 + b * CB + w)
                    m = three(pe, psum[:, 2 * (k % 2) + b, 0:w], qh[:, 0, rows], qh[:, 1, rows],
                              keyT[:, 0, cols], keyT[:, 1, cols])
                m.then_inc(scores_ready, 1)

            def enter(e):
                i = at[e]
                if i >= 2:
                    pe.wait_ge(ring_done, i - 1)
                return psum[:, 4 + i % 2, :]

            def turn(u, g):
                h = u % HALVES
                last = group(h, g)[-1]
                c = min((last[0] + last[1] - 1) // (2 * CB), CH - 1)
                pe.wait_ge(prob_ready, max(exp_at[u, 0, c], exp_at[u, 1, c]) + 1)
                b = enter(("T", u, g))
                for s, (c0, rows, _) in enumerate(group(h, g)):
                    for j in range(2):
                        m = pe.transpose(b[0:rows, s * 256 + j * P:s * 256 + (j + 1) * P],
                                         S[:, h, j, c0:c0 + rows], ident)
                m.then_inc(ring_ready, 1)

            def weigh(u, g):
                h = u % HALVES
                if g == 0 and u:
                    pe.wait_ge(acc_read, u)
                i = at["T", u, g]
                pe.wait_ge(ring_done, i + 1)
                slot = (u * NG + g) % RING
                for s, (c0, rows, t) in enumerate(group(h, g)):
                    start, stop = g == 0 and s == 0, g == NG - 1 and s == len(group(h, g)) - 1
                    pe.matmul(psum[:, 6, :], vals[0:rows, 0, t, :],
                              turned[0:rows, slot, s, :, :].rearrange("p a b -> p (a b)"), start=start, stop=stop)
                    m = pe.matmul(psum[:, 7, 0:256], vals[0:rows, 1, t, :], turned[0:rows, slot, s, 0, :],
                                  start=start, stop=stop)
                m.then_inc(pv_done, 1)

            def through(u, part):
                b = enter((part, u, 0))
                if part == "C":
                    pe.wait_ge(acc_read, u + 1)
                    m = pe.matmul(b[:, 0:256], wT[:, 1, :], uT[:, :], start=True, stop=True)
                else:
                    pe.wait_ge(ring_done, at["C", u, 0] + 1)
                    for j in range(2):
                        m = pe.matmul(b[:, j * P:(j + 1) * P], cT[:, j * P:(j + 1) * P], wT[:, 2, :],
                                      start=True, stop=True)
                m.then_inc(ring_ready, 1)

            pe.wait_ge(ct_low, n_ct)
            pe.wait_ge(pre_dve, 3)
            for j in range(2):
                for c in range(CH):
                    scores(0, j, c)
            pe.wait_ge(vl_ready, 2)
            for u in range(UNITS):
                for g in range(NG):
                    turn(u, g)
                    if u and g == 3:
                        through(u - 1, "C")
                    if u and g == 6:
                        through(u - 1, "O")
                    if g in SC_STEP and u + 1 < UNITS:
                        scores(u + 1, *divmod(SC_STEP[g], CH))
                    if g >= 2:
                        weigh(u, g - 2)
                weigh(u, NG - 2)
                weigh(u, NG - 1)
            through(UNITS - 1, "C")
            through(UNITS - 1, "O")
            pe.wait_ge(ring_done, len(ring))
            pe.matmul(psum[:, 0, 0:8], ident, ident[:, 0:8], start=True, stop=True).then_inc(cross_pe, 1)

        def place(n):
            return divmod(n, NT)

        def is_unit(n):
            return 0 <= n < N_UNITS

        def group_from(n, lag):
            m = n - lag
            return m // GT - 1 if m > 0 and m % GT == 0 and m // GT - 1 < DEPTH * NG_F else None

        LAST_STEP = N_UNITS + 3
        front = []
        for n in range(-2, LAST_STEP):
            if group_from(n, 2) is not None:
                front.append(("w2", group_from(n, 2)))
            if is_unit(n + 2):
                front += [(kind, n + 2) for kind in ("yT", "q", "k", "v")]
            if is_unit(n + 1):
                front += [(kind, n + 1) for kind in ("qT", "kT")]
            if group_from(n, 1) is not None:
                front.append(("hn", group_from(n, 1)))
            if group_from(n, 0) is not None:
                front.append(("shift", group_from(n, 0)))
        fat = {e: i for i, e in enumerate(front)}
        taken = {"yT": f_hT, "q": f_q_moved, "k": f_k_moved, "v": f_v_moved, "qT": f_qT_moved, "kT": f_kT_moved,
                 "w2": m_y, "hn": m_h2T, "shift": m_h2}

        def front_bank(kind, n):
            return fat[kind, n] % 2

        def enter_front(pe, kind, n):
            i = fat[kind, n]
            if i >= 2:
                before, m = front[i - 2]
                pe.wait_ge(taken[before], m + 1)
            return psum[:, i % 2, :]

        def turn_y(pe, n):
            l, t = place(n)
            if l == 0:
                pe.wait_ge(y0_ready, 1)
            else:
                pe.wait_ge(m_y, (l - 1) * NG_F + t // GT + 1)
            b = enter_front(pe, "yT", n)
            pe.transpose(b[:, 0:P], y_sb[l][:, t, :], ident).then_inc(f_yT, 1)

        def project(pe, n):
            l, t = place(n)
            if n == 0:
                pe.wait_ge(ld_f, 16 * FFN_LOADS)
                pe.wait_ge(setup_f, 2)
            pe.wait_ge(f_hT, n + 1)
            h = hT[l][:, WIN + t * P:WIN + (t + 1) * P]
            for i, (kind, made) in enumerate((("q", f_q), ("k", f_k), ("v", f_v))):
                b = enter_front(pe, kind, n)
                pe.matmul(b[:, 0:INNER], h, wqkv_sb[:, l, i * INNER:(i + 1) * INNER], start=True, stop=True)\
                  .then_inc(made, 1)

        def turn_qk(pe, n):
            pe.wait_ge(f_rsum, n + 1)
            b = enter_front(pe, "qT", n)
            for a_ in range(H // 2):
                m = pe.transpose(b[:, a_ * P:(a_ + 1) * P],
                                 ra[:, n % 2, 0, 2 * a_:2 * a_ + 2, :].rearrange("p h d -> p (h d)"), ident)
            m.then_inc(f_qT, 1)
            pe.wait_ge(f_kn, n + 1)
            b = enter_front(pe, "kT", n)
            for a_ in range(H // 2):
                m = pe.transpose(b[:, a_ * P:(a_ + 1) * P],
                                 kn[:, 2 * a_:2 * a_ + 2, :].rearrange("p h d -> p (h d)"), ident)
            m.then_inc(f_kT, 1)

        def moved_b(i):
            return sum(k // 2 % NT > 0 for k in range(i + 1))

        def att_scores(pe, n, hg):
            l, t = place(n)
            pe.wait_ge(f_qT_moved, n + 1)
            pe.wait_ge(f_kT_moved, n + 1)
            if n:
                pe.wait_ge(a_tA, 2 * (n - 1) + hg + 1)
                if moved_b(2 * (n - 1) + hg):
                    pe.wait_ge(a_tB, moved_b(2 * (n - 1) + hg))
            for b in range(2):
                rows = slice(b * HD, (b + 1) * HD)
                sc = psum[:, 2 + 2 * hg + b, :]
                pe.matmul(sc[:, 0:2 * (WIN + P)].rearrange("p (h k) -> p h k", h=2), ident_r[:, :],
                          mask_r[:, min(t, 1), :].unsqueeze(1).broadcast_to([P, 2, WIN + P]), start=True, stop=False)
                for e in range(2):
                    pr = 2 * hg + e
                    m = pe.matmul(sc[:, e * (WIN + P):(e + 1) * (WIN + P)], qTh[rows, n % 2, pr, :],
                                  kTh[rows, pr, t * P:t * P + WIN + P], start=False, stop=(e == 1))
            m.then_inc(a_s, 1)

        def att_turn(pe, n, hg):
            l, t = place(n)
            pe.wait_ge(a_p, 2 * n + hg + 1)
            for e in range(H // 2):
                m = pe.transpose(psum[:, 2 + 2 * hg, e * P:(e + 1) * P], prob[:, hg, e, WIN:WIN + P], ident)
            m.then_inc(a_t, 1)
            if t:
                for e in range(H // 2):
                    m = pe.transpose(psum[0:WIN, 3 + 2 * hg, e * WIN:(e + 1) * WIN], prob[0:WIN, hg, e, 0:WIN],
                                     ident[0:WIN, 0:WIN])
                m.then_inc(a_tb, 1)

        def att_weigh(pe, n, hg):
            l, t = place(n)
            i = 2 * n + hg
            pe.wait_ge(a_tA, i + 1)
            pe.wait_ge(f_v_moved, n + 1)
            if t:
                pe.wait_ge(a_tB, moved_b(i))
                pe.wait_ge(f_vp[(n - 1) % VS], 16 * ((n - 1) // VS + 1))
            if hg == 0 and n:
                pe.wait_ge(a_on, n)
            for e in range(H // 2):
                hd = hg * (H // 2) + e
                m = pe.matmul(psum[:, 7, hd * HD:(hd + 1) * HD], ptA[:, hg, e, :],
                              v_sb[:, n % VS, hd * HD:(hd + 1) * HD], start=True, stop=not t, skip_group_check=True)
                if t:
                    m = pe.matmul(psum[0:WIN, 7, hd * HD:(hd + 1) * HD], ptB[:, hg, e, :],
                                  v_prev[:, (n - 1) % VS, hd * HD:(hd + 1) * HD], start=False, stop=True,
                                  skip_group_check=True)
            m.then_inc(a_o, 1)

        def turn_o(pe, n):
            pe.wait_ge(a_on, n + 1)
            if n:
                pe.wait_ge(a_y1, n)
            for a_ in range(INNER // P):
                m = pe.transpose(psum[:, 6, a_ * P:(a_ + 1) * P],
                                 o_sb[:, 2 * a_:2 * a_ + 2, :].rearrange("p h d -> p (h d)"), ident)
            m.then_inc(a_oT, 1)

        def out_proj(pe, n):
            l, t = place(n)
            pe.wait_ge(a_oTm, n + 1)
            for a_ in range(INNER // P):
                m = pe.matmul(psum[:, 6, 0:D], oT[:, a_, :], wo_sb[:, l, a_, :], start=(a_ == 0),
                              stop=(a_ == INNER // P - 1))
            m.then_inc(a_wo, 1)

        w1_order = [(kind, b) for b in range(NBLK) for kind in (1, 0)]

        def shift(pe, k):
            l, g = divmod(k, NG_F)
            pe.wait_ge(a_y1, (k + 1) * GT)
            bank = enter_front(pe, "shift", k)
            for s in range(GT):
                t = g * GT + s
                o = bank[:, s * HD:(s + 1) * HD]
                m = pe.matmul(o, down, y1[l][:, t, HD:D], start=True, stop=(t == 0), skip_group_check=True)
                if t:
                    m = pe.matmul(o, edge, y1[l][:, t - 1, HD:D], start=False, stop=True, skip_group_check=True)
            m.then_inc(m_sh, 1)

        def turn_hn(pe, k):
            pe.wait_ge(m_hn, k + 1)
            bank = enter_front(pe, "hn", k)
            for s in range(GT):
                m = pe.transpose(bank[:, s * P:(s + 1) * P], hn[:, s, :], ident)
            m.then_inc(m_hT, 1)

        def hidden(pe, k):
            l = k // NG_F
            pe.wait_ge(m_h2T, k + 1)
            done = min((k + 1) * GT + 2, N_UNITS)
            pe.wait_ge(a_on, done)
            pe.wait_ge(a_y1, min(done, (k + 1) * GT + 1))
            for i, (kind, b) in enumerate(w1_order):
                if i >= 2:
                    pe.wait_ge(m_gelu if kind else m_mid, k * NBLK + b)
                c0, w = blk[b]
                pe.matmul(psum[0:w, 6 + i % 2, :], w1_sb[:, l, kind * HID + c0:kind * HID + c0 + w],
                          h2T[:, :], start=True, stop=True).then_inc(m_w1, 1)

        def feed_out(pe, k):
            l = k // NG_F
            pe.wait_ge(m_mid, (k + 1) * NBLK)
            bank = enter_front(pe, "w2", k)
            for s in range(GT):
                o = bank[:, s * D:(s + 1) * D]
                for b, (c0, w) in enumerate(blk):
                    pe.matmul(o, mid[0:w, b, s * P:(s + 1) * P], w2_sb[0:w, l, b, :], start=(b == 0), stop=False,
                              skip_group_check=True)
                m = pe.matmul(o, ones_row[:, :], b2r[:, l, :], start=False, stop=True, skip_group_check=True)
            m.then_inc(m_w2, 1)

        @block.tensor
        def _(pe):
            cross_tensor(pe)
            for n in range(-2, LAST_STEP):
                if group_from(n, 2) is not None:
                    hidden(pe, group_from(n, 2))
                if is_unit(n):
                    att_scores(pe, n, 0)
                if group_from(n, 2) is not None:
                    feed_out(pe, group_from(n, 2))
                if is_unit(n + 2):
                    turn_y(pe, n + 2)
                if is_unit(n):
                    att_scores(pe, n, 1)
                if is_unit(n - 1):
                    turn_o(pe, n - 1)
                if is_unit(n + 2):
                    project(pe, n + 2)
                if is_unit(n):
                    att_turn(pe, n, 0)
                if is_unit(n + 1):
                    turn_qk(pe, n + 1)
                if is_unit(n):
                    att_turn(pe, n, 1)
                if group_from(n, 1) is not None:
                    turn_hn(pe, group_from(n, 1))
                if is_unit(n - 1):
                    out_proj(pe, n - 1)
                if is_unit(n):
                    att_weigh(pe, n, 0)
                    att_weigh(pe, n, 1)
                if group_from(n, 0) is not None:
                    shift(pe, group_from(n, 0))

        @block.scalar
        def _(act):
            act.wait_ge(pre_pe, 1)
            act.copy(wT[:, :, :], psum[:, 0, 0:3 * P].rearrange("p (a b) -> p a b", a=3)).then_inc(pre_act, 1)
            act.wait_ge(pre_pe, 2)
            act.copy(qT[:, :], psum[:, 1:3, :]).then_inc(pre_act, 1)
            act.wait_ge(pre_pe, 3)
            act.wait_ge(ld_b, 48)
            act.activation(qpT[:, :], psum[:, 3:5, :], ACT.Identity, bias=bqc[:, 0:1]).then_inc(pre_act, 1)
            act.wait_ge(pre_pe, 4)
            act.copy(qh[:, 0, :], psum[:, 5:7, :]).then_inc(pre_act, 1)
            n_ct = (KT + 1 + 3) // 4
            for i in range(n_ct):
                c0, w = 512 * i, min(512, NKEYS - 512 * i)
                act.wait_ge(ct_ready, i + 1)
                act.copy(keyT[:, 0, c0:c0 + w], psum[:, 1 + i % 2, 0:w]).then_inc(ct_high, 1)

            def high(u, g):
                act.wait_ge(ring_ready, at["T", u, g] + 1)
                k = u * NG + g
                if k >= RING:
                    act.wait_ge(pv_done, k - RING + 1)
                tiles = group(u % HALVES, g)
                rows = tiles[0][1]
                if all(r == P for _, r, _ in tiles):
                    w = len(tiles)
                    act.copy(turned[:, k % RING, 0:w, 0, :],
                             psum[:, 4 + at["T", u, g] % 2, 0:256 * w].rearrange("p (a b) -> p a b", b=256))\
                       .then_inc(high_ready, 1)
                else:
                    for s, (_, r, _) in enumerate(tiles):
                        m = act.copy(turned[0:r, k % RING, s, 0, :],
                                     psum[0:r, 4 + at["T", u, g] % 2, 256 * s:256 * (s + 1)])
                    m.then_inc(high_ready, 1)

            def expo(u, j, c):
                h = u % HALVES
                act.wait_ge(max_ready, 2 * u + j + 1)
                c0, w0, w1_ = chunks[h][c]
                s = S[:, h, j, c0:c0 + w0 + w1_]
                act.activation(s, s, ACT.Exp, bias=nmax[:, u, j:j + 1],
                               accum_out=zpart[:, u, j, c:c + 1]).then_inc(prob_ready, 1)

            def acc_b(u):
                act.wait_ge(pv_done, (u + 1) * NG)
                if u:
                    act.wait_ge(acc_read, u)
                act.copy(accb[:, :], psum[:, 7, 0:256]).then_inc(accb_ready, 1)

            def alphas(p):
                act.wait_ge(alpha_in, p + 1)
                act.activation(al[:, :, :], al[:, :, :], ACT.Exp).then_inc(alpha_ready, 1)

            for j, c in exp_steps.values():
                expo(0, j, c)
            for u in range(UNITS):
                for g in range(NG):
                    high(u, g)
                    if g in exp_late:
                        expo(u, *exp_late[g])
                    if g in exp_steps and u + 1 < UNITS:
                        expo(u + 1, *exp_steps[g])
                    if g == 7 and u and u % HALVES == 0:
                        alphas(u // HALVES - 1)
                acc_b(u)
            alphas(PAIRS - 1)
            act.wait_ge(alpha_ready, PAIRS)
            act.copy(accb[:, 0:1], accb[:, 1:2]).then_inc(cross_act, 1)

            def key_move(n):
                act.wait_ge(f_k, n + 1)
                if n:
                    act.wait_ge(f_rab, n)
                act.copy(qk[:, 1, :, :], psum[:, front_bank("k", n), :].rearrange("p (h d) -> p h d", h=H))\
                   .then_inc(f_k_moved, 1)

            def squares(n):
                act.wait_ge(f_q_moved, n + 1)
                act.wait_ge(f_k_moved, n + 1)
                if n:
                    act.wait_ge(f_ss, n)
                act.activation(sq[:, :, :], qk[:, :, :, :].rearrange("p k h d -> p (k h) d"), ACT.Square).then_inc(f_sq, 1)

            def qk_turned(n):
                l, t = place(n)
                act.wait_ge(f_qT, n + 1)
                if n >= 2:
                    act.wait_ge(a_s, 2 * (n - 1))
                act.copy(qTh[:, n % 2, :, :], psum[:, front_bank("qT", n), :].rearrange("p (a t) -> p a t", t=P))\
                   .then_inc(f_qT_moved, 1)
                act.wait_ge(f_kT, n + 1)
                if n >= NT:
                    act.wait_ge(a_s, 2 * min(n - NT + 2, NT))
                c = WIN + t * P
                act.copy(kTh[:, :, c:c + P], psum[:, front_bank("kT", n), :].rearrange("p (a t) -> p a t", t=P))\
                   .then_inc(f_kT_moved, 1)

            def probs(n, hg):
                i = 2 * n + hg
                act.wait_ge(a_nb, i + 1)
                if i >= 2:
                    act.wait_ge(a_t, i - 1)
                    if moved_b(i - 2):
                        act.wait_ge(a_tb, moved_b(i - 2))
                if n >= 2 and hg == 0:
                    act.wait_ge(a_on, n - 1)
                for e in range(H // 2):
                    hd = hg * (H // 2) + e
                    m = act.activation(prob[:, hg, e, :],
                                       psum[:, 2 + 2 * hg + e % 2, (e // 2) * (WIN + P):(e // 2 + 1) * (WIN + P)],
                                       ACT.Exp, bias=nb[:, n % 2, hd:hd + 1], scale=r8[:, n % 3, hd:hd + 1],
                                       accum_out=z[:, n % 2, hd:hd + 1])
                m.then_inc(a_p, 1)

            def turned_a(n, hg):
                i = 2 * n + hg
                act.wait_ge(a_t, i + 1)
                if i >= 2:
                    act.wait_ge(a_o, i - 1)
                act.copy(ptA[:, hg, :, :], psum[:, 2 + 2 * hg, :].rearrange("p (a t) -> p a t", t=P)).then_inc(a_tA, 1)

            def o_turned(n):
                act.wait_ge(a_oT, n + 1)
                if n:
                    act.wait_ge(a_wo, n)
                act.copy(oT[:, :, :], psum[:, 6, :].rearrange("p (a t) -> p a t", t=P)).then_inc(a_oTm, 1)

            def shifted(k):
                act.wait_ge(m_sh, k + 1)
                if k:
                    act.wait_ge(m_hn, k)
                act.copy(h2[:, :, HD:D], psum[:, front_bank("shift", k), 0:GT * HD].rearrange("p (s d) -> p s d", d=HD))\
                   .then_inc(m_h2, 1)

            def hn_turned(k):
                l = k // NG_F
                act.wait_ge(m_hT, k + 1)
                if k:
                    act.wait_ge(m_w1, 2 * NBLK * k)
                act.activation(h2T[:, :], psum[:, front_bank("hn", k), :], ACT.Identity, bias=lnc[:, 1, l:l + 1],
                               scale=lnc[:, 0, l:l + 1]).then_inc(m_h2T, 1)

            def gates(k):
                l = k // NG_F
                if k:
                    act.wait_ge(m_mid, k * NBLK)
                for b, (c0, w) in enumerate(blk):
                    act.wait_ge(m_w1, 2 * NBLK * k + 2 * b + 1)
                    act.activation(gl[0:w, b, :], psum[0:w, 6, :], ACT.Gelu,
                                   bias=b1c[0:w, l, 1, b:b + 1]).then_inc(m_gelu, 1)

            for n in range(-2, LAST_STEP):
                if group_from(n, 2) is not None:
                    gates(group_from(n, 2))
                if is_unit(n):
                    probs(n, 0)
                if is_unit(n - 1):
                    o_turned(n - 1)
                if is_unit(n + 2):
                    key_move(n + 2)
                if is_unit(n):
                    probs(n, 1)
                    turned_a(n, 0)
                if is_unit(n + 1):
                    qk_turned(n + 1)
                if is_unit(n):
                    turned_a(n, 1)
                if group_from(n, 1) is not None:
                    hn_turned(group_from(n, 1))
                if is_unit(n + 2):
                    squares(n + 2)
                if group_from(n, 0) is not None:
                    shifted(group_from(n, 0))

        @block.gpsimd
        def _(pool):
            pool.memset(minus_half[:, :], -0.5).then_inc(half_set, 1)
            pool.wait_ge(half_set, 1)
            for i in range(2):
                pool.wait_ge(var_ready, i + 1)
                pool.tensor_tensor(rstd[:, :, 0], rstd[:, :, 0], minus_half[:, 0:NT], ALU.pow).then_inc(rstd_ready, 1)

            def rotate(n):
                pool.wait_ge(f_rab, n + 1)
                pool.tensor_tensor(ra[:, n % 2, :, :, :], ra[:, n % 2, :, :, :], rb[:, :, :, :], ALU.add).then_inc(f_rsum, 1)
                pool.wait_ge(f_ss, n + 1)
                if n >= 2:
                    pool.wait_ge(f_kn, n - 1)
                pool.tensor_tensor(rinv[:, n % 2, :], ss[:, :], minus_half[:, :], ALU.pow).then_inc(f_rinv, 1)

            def left_half(k):
                l, g = divmod(k, NG_F)
                pool.wait_ge(a_y1, (k + 1) * GT)
                if k:
                    pool.wait_ge(m_hn, k)
                pool.tensor_copy(h2[:, :, 0:HD], y1[l][:, g * GT:(g + 1) * GT, 0:HD]).then_inc(m_left, 1)
                pool.wait_ge(m_var, k + 1)
                pool.tensor_tensor(frs[:, :], fve[:, :], minus_half[:, 0:GT], ALU.pow).then_inc(m_rs, 1)

            for n in range(-2, LAST_STEP):
                if is_unit(n + 2):
                    rotate(n + 2)
                if group_from(n, 0) is not None:
                    left_half(group_from(n, 0))

        @block.vector
        def _(dve):
            links = [0]

            def link(ins):
                links[0] += 1
                ins.then_inc(dve_link, 1)
                dve.wait_ge(dve_link, links[0])

            def norm_x(i, dst):
                for t in range(NT):
                    m = dve.bn_stats(stats[:, t, :], x_sb[:, t, :])
                link(m)
                for t in range(NT):
                    m = dve.bn_aggr(mv[:, t, :], stats[:, t, :])
                link(m)
                dve.tensor_scalar(rstd[:, :, :], mv[:, :, 1:2], EPS, None, ALU.add).then_inc(var_ready, 1)
                dve.wait_ge(rstd_ready, i + 1)
                for t in range(NT):
                    m = dve.tensor_scalar(dst[:, t, :], x_sb[:, t, :], mv[:, t, 0:1], rstd[:, t, 0:1],
                                          ALU.subtract, ALU.mult)
                return m

            dve.wait_ge(ld_x, 16)
            norm_x(0, y_sb[0]).then_inc(xn_ready, 1)
            dve.wait_ge(ld_b, 48)
            dve.tensor_copy(bvr[:, :], bvc[:, 0:1].broadcast_to([P, P])).then_inc(pre_dve, 1)
            dve.wait_ge(pre_act, 4)
            dve.tensor_tensor(qh[:, 1, :], psum[:, 5:7, :], qh[:, 0, :].bitcast(F32), ALU.subtract).then_inc(pre_dve, 1)
            dve.wait_ge(pre_pe, 5)
            link(dve.tensor_tensor(bob[:, :], psum[:, 7, 0:P], bob[:, :], ALU.add))
            dve.wait_ge(xn_ready, 1)
            for t in range(NT):
                m = dve.tensor_tensor(x_sb[:, t, :], x_sb[:, t, :], bob[:, :], ALU.add)
            m.then_inc(pre_dve, 1)
            n_ct = (KT + 1 + 3) // 4
            for i in range(n_ct):
                c0, w = 512 * i, min(512, NKEYS - 512 * i)
                dve.wait_ge(ct_high, i + 1)
                dve.tensor_tensor(keyT[:, 1, c0:c0 + w], psum[:, 1 + i % 2, 0:w], keyT[:, 0, c0:c0 + w].bitcast(F32),
                                  ALU.subtract).then_inc(ct_low, 1)
            for s in ld_c:
                dve.wait_ge(s, 16)
            dve.wait_ge(ld_t, 16)
            dve.tensor_copy(vals[:, 0, 0:KT, :], raw).then_inc(vh_ready, 1)
            dve.tensor_copy(vals[0:TAIL, 0, KT, :], rawt[0:TAIL, :]).then_inc(vh_ready, 1)
            dve.wait_ge(vh_ready, 2)
            dve.tensor_tensor(vals[:, 1, 0:KT, :], raw, vals[:, 0, 0:KT, :].bitcast(F32), ALU.subtract).then_inc(vl_ready, 1)
            dve.tensor_tensor(vals[0:TAIL, 1, KT, :], rawt[0:TAIL, :], vals[0:TAIL, 0, KT, :].bitcast(F32),
                              ALU.subtract).then_inc(vl_ready, 1)
            dve.wait_ge(vl_ready, 2)

            def move_scores(u, j, c):
                h = u % HALVES
                k = (u * 2 + j) * CH + c
                c0, w0, w1_ = chunks[h][c]
                dve.wait_ge(scores_ready, k + 1)
                if u >= HALVES:
                    dve.wait_ge(ring_done, at["T", u - HALVES, NG - 1] + 1)
                if w0 == w1_:
                    dve.tensor_scalar(S[:, h, j, c0:c0 + 2 * w0].rearrange("p (a b) -> p a b", a=2),
                                      psum[:, 2 * (k % 2):2 * (k % 2) + 2, 0:w0], SCALE, None, ALU.mult, ALU.max,
                                      accum_out=cmax[:, u, j, c:c + 1]).then_inc(scores_moved, 1)
                    dve.wait_ge(scores_moved, k + 1)
                else:
                    link(dve.tensor_scalar(S[:, h, j, c0:c0 + w0], psum[:, 2 * (k % 2), 0:w0], SCALE, None, ALU.mult,
                                           ALU.max, accum_out=cmax[:, u, j, c:c + 1]))
                    dve.tensor_scalar(S[:, h, j, c0 + w0:c0 + w0 + w1_], psum[:, 2 * (k % 2) + 1, 0:w1_], SCALE,
                                      cmax[:, u, j, c:c + 1], ALU.mult, ALU.max,
                                      accum_out=cmax[:, u, j, c:c + 1]).then_inc(scores_moved, 1)
                    dve.wait_ge(scores_moved, k + 1)
                if c == CH - 1:
                    link(dve.tensor_reduce(nmax[:, u, j:j + 1], cmax[:, u, j, :], AX_X, ALU.max))
                    dve.tensor_scalar(nmax[:, u, j:j + 1], nmax[:, u, j:j + 1], -1.0, None, ALU.mult).then_inc(max_ready, 1)

            def low(u, g):
                i = at["T", u, g]
                k = u * NG + g
                dve.wait_ge(high_ready, k + 1)
                tiles = group(u % HALVES, g)
                if all(r == P for _, r, _ in tiles):
                    w = len(tiles)
                    dve.tensor_tensor(turned[:, k % RING, 0:w, 1, :],
                                      psum[:, 4 + i % 2, 0:256 * w].rearrange("p (a b) -> p a b", b=256),
                                      turned[:, k % RING, 0:w, 0, :].bitcast(F32), ALU.subtract).then_inc(ring_done, 1)
                else:
                    for s, (_, r, _) in enumerate(tiles):
                        m = dve.tensor_tensor(turned[0:r, k % RING, s, 1, :], psum[0:r, 4 + i % 2, 256 * s:256 * (s + 1)],
                                              turned[0:r, k % RING, s, 0, :].bitcast(F32), ALU.subtract)
                    m.then_inc(ring_done, 1)

            def acc_a(u):
                dve.wait_ge(accb_ready, u + 1)
                if u:
                    dve.wait_ge(ring_ready, at["C", u - 1, 0] + 1)
                link(dve.tensor_tensor(uT[:, :], psum[:, 6, 0:256], accb[:, :], ALU.add))
                dve.tensor_tensor(uT[:, :], psum[:, 6, 256:512], uT[:, :], ALU.add).then_inc(acc_read, 1)

            def c_out(u):
                dve.wait_ge(ring_ready, at["C", u, 0] + 1)
                dve.tensor_copy(cT[:, :], psum[:, 4 + at["C", u, 0] % 2, 0:256]).then_inc(ring_done, 1)

            def o_out(u):
                dve.wait_ge(ring_ready, at["O", u, 0] + 1)
                dve.tensor_copy(oh[:, u % HALVES, :, :],
                                psum[:, 4 + at["O", u, 0] % 2, 0:256].rearrange("p (j d) -> p j d", d=D)).then_inc(ring_done, 1)

            def merge_in(p):
                u0, u1 = HALVES * p, HALVES * p + 1
                if p:
                    dve.wait_ge(alpha_ready, p)
                link(dve.tensor_tensor(mmin[:, :], nmax[:, u0, :], nmax[:, u1, :], ALU.min))
                for h, u in ((0, u0), (1, u1)):
                    m = dve.tensor_tensor(al[:, h, :], mmin[:, :], nmax[:, u, :], ALU.subtract)
                m.then_inc(alpha_in, 1)

            def merge(p):
                u0, u1 = HALVES * p, HALVES * p + 1
                dve.wait_ge(alpha_ready, p + 1)
                for h, u in ((0, u0), (1, u1)):
                    dve.wait_ge(prob_ready, exp_at[u, 1, CH - 1] + 1)
                    m = dve.tensor_reduce(zs[:, h, :], zpart[:, u, :, :], AX_X, ALU.add)
                link(m)
                link(dve.tensor_tensor(zs[:, :, :], zs[:, :, :], al[:, :, :], ALU.mult))
                link(dve.tensor_tensor(zt[:, :], zs[:, 0, :], zs[:, 1, :], ALU.add))
                link(dve.reciprocal(zt[:, :], zt[:, :]))
                for j in range(2):
                    m = dve.tensor_scalar(al[:, :, j], al[:, :, j], zt[:, j:j + 1], None, ALU.mult)
                link(m)
                dve.wait_ge(ring_done, at["O", u1, 0] + 1)
                for j in range(2):
                    m = dve.scalar_tensor_tensor(x_sb[:, 2 * p + j, :], oh[:, 0, j, :], al[:, 0, j:j + 1],
                                                 x_sb[:, 2 * p + j, :], ALU.mult, ALU.add)
                link(m)
                for j in range(2):
                    m = dve.scalar_tensor_tensor(x_sb[:, 2 * p + j, :], oh[:, 1, j, :], al[:, 1, j:j + 1],
                                                 x_sb[:, 2 * p + j, :], ALU.mult, ALU.add)
                link(m)

            for j in range(2):
                for c in range(CH):
                    move_scores(0, j, c)
            for u in range(UNITS):
                for g in range(NG):
                    low(u, g)
                    if u and g == 3:
                        c_out(u - 1)
                    if u and g == 6:
                        o_out(u - 1)
                        if u % HALVES == 0:
                            merge_in(u // HALVES - 1)
                    if g == 8 and u and u % HALVES == 0:
                        merge(u // HALVES - 1)
                    if g in SC_STEP and u + 1 < UNITS:
                        move_scores(u + 1, *divmod(SC_STEP[g], CH))
                acc_a(u)
            c_out(UNITS - 1)
            o_out(UNITS - 1)
            merge_in(PAIRS - 1)
            merge(PAIRS - 1)
            norm_x(1, y_sb[0]).then_inc(y0_ready, 1)

            dve.wait_ge(y0_ready, 1)
            dve.wait_ge(cross_pe, 1)
            dve.wait_ge(cross_act, 1)
            for l in range(DEPTH):
                m = dve.memset(hT[l][:, 0:WIN + 1], 0.0)
            link(dve.memset(kTh[:, :, 0:WIN], 0.0))
            dve.memset(ones_row[:, :], 1.0).then_inc(setup_f, 1)
            dve.tensor_copy(ident_r[:, :], ident)
            dve.wait_ge(ld_g, 16 * G_LOADS)
            link(dve.tensor_copy(mask_r[:, :, :], mask[:, :, :]))
            hh = HD // 2
            for l in range(DEPTH):
                for k in range(2):
                    dve.tensor_tensor(rotl[:, l, :, 0, k, :], rot[:, :, 0, k, :],
                                      sc_b[:, k, l, :].unsqueeze(1).broadcast_to([P, NT, HD]), ALU.mult)
                    for e in range(2):
                        m = dve.tensor_tensor(rotl[:, l, :, 1, k, e * hh:(e + 1) * hh],
                                              rot[:, :, 1, k, e * hh:(e + 1) * hh],
                                              sc_b[:, k, l, (1 - e) * hh:(2 - e) * hh].unsqueeze(1).broadcast_to([P, NT, hh]),
                                              ALU.mult)
            m.then_inc(setup_f, 1)
            dve.wait_ge(setup_f, 2)

            def h_turn(n):
                l, t = place(n)
                dve.wait_ge(f_yT, n + 1)
                c = WIN + t * P
                dve.tensor_copy(hT[l][0:HD, c:c + P], psum[0:HD, front_bank("yT", n), 0:P])
                dve.tensor_copy(hT[l][HD:D, c + 1:c + 1 + P], psum[HD:D, front_bank("yT", n), 0:P]).then_inc(f_hT, 1)

            def query_move(n):
                dve.wait_ge(f_q, n + 1)
                if n:
                    dve.wait_ge(f_sq, n)
                dve.tensor_copy(qk[:, 0, :, :], psum[:, front_bank("q", n), :].rearrange("p (h d) -> p h d", h=H))\
                   .then_inc(f_q_moved, 1)

            def value_move(n):
                dve.wait_ge(f_v, n + 1)
                if n >= VS:
                    dve.wait_ge(a_o, 2 * (n - VS + 1))
                    dve.wait_ge(f_vp[n % VS], 16 * (n // VS))
                dve.tensor_copy(v_sb[:, n % VS, :], psum[:, front_bank("v", n), :]).then_inc(f_v_moved, 1)

            def rotate(n):
                l, t = place(n)
                dve.wait_ge(f_q_moved, n + 1)
                dve.wait_ge(f_k_moved, n + 1)
                if n:
                    dve.wait_ge(f_rsum, n)
                if n >= 2:
                    dve.wait_ge(f_qT, n - 1)
                for k in range(2):
                    dve.tensor_tensor(ra[:, n % 2, k, :, :], qk[:, k, :, :],
                                      rotl[:, l, t, 0, k, :].unsqueeze(1).broadcast_to([P, H, HD]), ALU.mult)
                    for e in range(2):
                        m = dve.tensor_tensor(rb[:, k, :, e * hh:(e + 1) * hh], qk[:, k, :, (1 - e) * hh:(2 - e) * hh],
                                              rotl[:, l, t, 1, k, e * hh:(e + 1) * hh].unsqueeze(1).broadcast_to([P, H, hh]),
                                              ALU.mult)
                m.then_inc(f_rab, 1)

            def square_sums(n):
                dve.wait_ge(f_sq, n + 1)
                if n:
                    dve.wait_ge(f_rinv, n)
                link(dve.tensor_reduce(ss[:, :], sq[:, :, :], AX_X, ALU.add))
                dve.tensor_scalar(ss[:, :], ss[:, :], 1e-24, None, ALU.max).then_inc(f_ss, 1)

            def key_norm(n):
                dve.wait_ge(f_rinv, n + 1)
                if n >= 3:
                    dve.wait_ge(a_p, 2 * (n - 2))
                dve.tensor_scalar(r8[:, n % 3, :], rinv[:, n % 2, 0:H], QK_SCALE, None, ALU.mult).then_inc(f_r8, 1)
                dve.wait_ge(f_rsum, n + 1)
                if n:
                    dve.wait_ge(f_kT, n)
                dve.tensor_tensor(kn[:, :, :], ra[:, n % 2, 1, :, :],
                                  rinv[:, n % 2, H:2 * H].unsqueeze(2).broadcast_to([P, H, HD]), ALU.mult).then_inc(f_kn, 1)

            def maxima(n, hg):
                i = 2 * n + hg
                dve.wait_ge(a_s, i + 1)
                q = H // 2
                if i >= 4:
                    dve.wait_ge(a_p, i - 3)
                link(dve.tensor_reduce(mx[:, hg * q:(hg + 1) * q].rearrange("p (e b) -> p b e", b=2),
                                       psum[:, 2 + 2 * hg:4 + 2 * hg, 0:2 * (WIN + P)].rearrange("p a (h k) -> p a h k", h=2),
                                       AX_X, ALU.max))
                dve.wait_ge(f_r8, n + 1)
                dve.scalar_tensor_tensor(nb[:, n % 2, hg * q:(hg + 1) * q], mx[:, hg * q:(hg + 1) * q], -1.0,
                                         r8[:, n % 3, hg * q:(hg + 1) * q], ALU.mult, ALU.mult).then_inc(a_nb, 1)
                dve.wait_ge(a_nb, i + 1)

            def turned_b(n, hg):
                l, t = place(n)
                if t:
                    dve.wait_ge(a_tb, moved_b(2 * n + hg))
                    if n >= 2:
                        dve.wait_ge(a_o, 2 * (n - 1) + hg + 1)
                    dve.tensor_copy(ptB[:, hg, :, :], psum[0:WIN, 3 + 2 * hg, 0:H // 2 * WIN].rearrange("p (a t) -> p a t", t=WIN))\
                       .then_inc(a_tB, 1)

            def o_norm(n):
                dve.wait_ge(a_p, 2 * n + 2)
                link(dve.reciprocal(rz[:, :], z[:, n % 2, :]))
                dve.wait_ge(a_o, 2 * n + 2)
                if n:
                    dve.wait_ge(a_oT, n)
                dve.tensor_tensor(o_sb[:, :, :], psum[:, 7, :].rearrange("p (h d) -> p h d", h=H),
                                  rz[:, :].unsqueeze(2).broadcast_to([P, H, HD]), ALU.mult).then_inc(a_on, 1)
                dve.wait_ge(a_on, n + 1)

            def add_att(n):
                l, t = place(n)
                dve.wait_ge(a_wo, n + 1)
                dve.tensor_tensor(y1[l][:, t, :], psum[:, 6, 0:D], y_sb[l][:, t, :], ALU.add).then_inc(a_y1, 1)

            def group_stats(k):
                dve.wait_ge(m_h2, k + 1)
                dve.wait_ge(m_left, k + 1)
                if k:
                    dve.wait_ge(m_rs, k)
                for s in range(GT):
                    m = dve.bn_stats(fstats[:, s, :], h2[:, s, :])
                link(m)
                for s in range(GT):
                    m = dve.bn_aggr(fmv[:, s, :], fstats[:, s, :])
                link(m)
                dve.tensor_scalar(fve[:, :], fmv[:, :, 1], EPS, None, ALU.add).then_inc(m_var, 1)

            def group_norm(k):
                dve.wait_ge(m_rs, k + 1)
                if k:
                    dve.wait_ge(m_hT, k)
                for s in range(GT):
                    m = dve.tensor_scalar(hn[:, s, :], h2[:, s, :], fmv[:, s, 0:1], frs[:, s:s + 1],
                                          ALU.subtract, ALU.mult)
                m.then_inc(m_hn, 1)
                dve.wait_ge(m_hn, k + 1)

            def gated(k):
                l = k // NG_F
                if k:
                    dve.wait_ge(m_w2, k)
                for b, (c0, w) in enumerate(blk):
                    dve.wait_ge(m_gelu, k * NBLK + b + 1)
                    dve.wait_ge(m_w1, 2 * NBLK * k + 2 * b + 2)
                    dve.scalar_tensor_tensor(mid[0:w, b, :], psum[0:w, 7, :],
                                             b1c[0:w, l, 0, b:b + 1], gl[0:w, b, :], ALU.add, ALU.mult).then_inc(m_mid, 1)

            def add_feed(k):
                l, g = divmod(k, NG_F)
                ts = slice(g * GT, (g + 1) * GT)
                fed = psum[:, front_bank("w2", k), :].rearrange("p (s d) -> p s d", d=D)
                dve.wait_ge(m_w2, k + 1)
                if l + 1 < DEPTH:
                    dve.tensor_tensor(y_sb[l + 1][:, ts, :], fed, y1[l][:, ts, :], ALU.add).then_inc(m_y, 1)
                else:
                    dve.tensor_tensor(last[:, :, :], fed, y1[l][:, ts, :], ALU.add).then_inc(m_y, 1)
                    dve.wait_ge(m_y, k + 1)
                    dve.tensor_tensor(x_sb[:, ts, :], x_sb[:, ts, :], last[:, :, :], ALU.add).then_inc(x_out, 1)
                    dve.wait_ge(x_out, g + 1)

            for n in range(-2, LAST_STEP):
                if group_from(n, 2) is not None:
                    gated(group_from(n, 2))
                if is_unit(n):
                    maxima(n, 0)
                if group_from(n, 2) is not None:
                    add_feed(group_from(n, 2))
                if is_unit(n + 2):
                    h_turn(n + 2)
                if is_unit(n):
                    maxima(n, 1)
                if is_unit(n + 1):
                    key_norm(n + 1)
                if is_unit(n + 2):
                    query_move(n + 2)
                    value_move(n + 2)
                if is_unit(n):
                    turned_b(n, 0)
                if group_from(n, 1) is not None:
                    group_norm(group_from(n, 1))
                if is_unit(n + 2):
                    rotate(n + 2)
                if is_unit(n):
                    turned_b(n, 1)
                if is_unit(n - 1):
                    add_att(n - 1)
                if is_unit(n + 2):
                    square_sums(n + 2)
                if is_unit(n):
                    o_norm(n)
                if group_from(n, 0) is not None:
                    group_stats(group_from(n, 0))


_INS = ['x', 'ctx_1024', 'L0_xattn_Wk', 'L0_xattn_Wv', 'L0_xattn_bv', 'L0_xattn_Wq', 'L0_xattn_bq', 'L0_xattn_Wo',
        'L0_xattn_bo', 'L0_ffn_wqkv', 'L0_ffn_q_scale', 'L0_ffn_k_scale', 'L0_ffn_wo', 'L0_ffn_ln_g', 'L0_ffn_ln_b',
        'L0_ffn_w1', 'L0_ffn_b1', 'L0_ffn_w2', 'L0_ffn_b2']
_OUTS = [((1, 1024, 128), 'float32')]


def kernel(**inputs):
    import numpy as _np
    import concourse.bacc as _bacc
    from concourse import mybir as _mybir
    from concourse.bass_utils import run_bass_kernel_spmd as _run

    nc = _bacc.Bacc("TRN2", target_bir_lowering=False, num_devices=1)
    arrays, args = {}, []
    given = {name: _np.ascontiguousarray(inputs[name]) for name in _INS}
    rot, mask, mats = shape_constants(1024, 64, 64)
    given.update(rot_tab=rot, mask_tab=mask, mats=mats)
    for name, a in given.items():
        arrays[f"in_{name}_dram"] = a
        args.append(nc.dram_tensor(f"in_{name}_dram", a.shape, _mybir.dt.from_np(a.dtype), kind="ExternalInput").ap())
    for i, (shape, dtype) in enumerate(_OUTS):
        dt = _mybir.dt.from_np(_np.dtype(dtype))
        args.append(nc.dram_tensor(f"out_{i}_dram", shape, dt, kind="ExternalOutput").ap())
    xattn_ffn_kernel(nc, *args)
    r = _run(nc, [arrays], core_ids=[0])
    got = tuple(r.results[0][f"out_{i}_dram"] for i in range(len(_OUTS)))
    return got[0]
```

```python
from contextlib import ExitStack

import numpy as np

import concourse.bass as bass
from concourse import mybir

ALU = mybir.AluOpType
ACT = mybir.ActivationFunctionType
AX_X = mybir.AxisListType.X
F32 = mybir.dt.float32
F32R = mybir.dt.float32r

P = 128
MASKED = -1e30


class Shapes:

    def __init__(self, x, ctx, w1):
        _, self.n, self.d = x.shape
        _, self.keys, _ = ctx.shape
        self.tiles = self.n // P
        self.ktiles = self.keys // P
        self.tail = self.keys - self.ktiles * P
        self.hid = w1.shape[2] // 2


def shape_constants(n, heads_dim, window):
    half = np.arange(0, heads_dim, 2, dtype=np.float32)
    inv_freq = (1.0 / 10000.0 ** (half / np.float32(heads_dim))).astype(np.float32)
    t = np.arange(n, dtype=np.float32)
    freqs = t[:, None] * inv_freq[None, :]
    freqs = np.concatenate([freqs, freqs], axis=-1)
    base = ((half + np.float32(0.4 * heads_dim)) / np.float32(1.4 * heads_dim)).astype(np.float32)
    power = ((t - n // 2) / np.float32(window // 2)).astype(np.float32)
    scale = base[None, :] ** power[:, None]
    scale = np.concatenate([scale, scale], axis=-1)
    cos, sin = np.cos(freqs), np.sin(freqs)
    sign = np.where(np.arange(heads_dim) < heads_dim // 2, -1.0, 1.0).astype(np.float32)
    rot = np.stack([np.stack([cos * scale, cos / scale], 1),
                    np.stack([sin * scale * sign, sin / scale * sign], 1)], 1)
    rot = rot.reshape(n // P, P, 2 * 2 * heads_dim).transpose(1, 0, 2)
    i = np.arange(P)[:, None]
    j = np.arange(-window, P)[None, :]
    ok = (j <= i) & (i <= j + window) & (j // window >= i // window - 1)
    mask = np.stack([np.where(ok & (j >= 0), 0.0, MASKED), np.where(ok, 0.0, MASKED)], 1)
    ident = np.eye(P)
    down = np.eye(P, k=1)
    edge = np.zeros((P, P))
    edge[P - 1, 0] = 1.0
    mats = np.stack([ident, down, edge], 1)
    return (np.ascontiguousarray(rot, np.float32), np.ascontiguousarray(mask, np.float32),
            np.ascontiguousarray(mats, np.float32))


def xattn_ffn_kernel(nc, x, ctx_1024, Wk, Wv, bv, Wq, bq, Wo, bo,
                     wqkv, q_scale, k_scale, wo, ln_g, ln_b, w1, b1, w2, b2,
                     rot_tab, mask_tab, mats, out):
    sh = Shapes(x, ctx_1024, w1)
    D = sh.d
    NT, KT, TAIL, NKEYS = sh.tiles, sh.ktiles, sh.tail, sh.keys
    DEPTH = wqkv.shape[0]
    INNER = wqkv.shape[2] // 3
    HD = q_scale.shape[1]
    H = INNER // HD
    HID = sh.hid
    WIN = HD
    SCALE = float(1.0 / np.sqrt(np.float32(D)))
    QK_SCALE = 8.0
    EPS = 1e-5

    PAIRS = NT // 2
    HALVES = 2
    UNITS = PAIRS * HALVES
    HK = KT // HALVES
    half0 = [h * HK * P for h in range(HALVES)]
    hkeys = [HK * P, HK * P + TAIL]
    CH = 4
    CB = HK * P // (2 * CH)
    chunks = [[(c * 2 * CB, CB, CB + (TAIL if h == HALVES - 1 and c == CH - 1 else 0)) for c in range(CH)]
              for h in range(HALVES)]
    G = 2
    NG = (HK + G) // G
    SC_STEP = {g: g for g in range(2 * CH)}

    def group(h, g):
        tiles = [(i * P, P, h * HK + i) for i in range(HK)]
        if h == HALVES - 1:
            tiles.append((HK * P, TAIL, KT))
        return tiles[G * g:G * g + G]

    ring = []
    for u in range(UNITS):
        for g in range(NG):
            ring.append(("T", u, g))
            if u and g == 3:
                ring.append(("O", u - 1, 0))
    at = {e: i for i, e in enumerate(ring)}
    def merges_at(u):
        if u == UNITS - 1:
            return PAIRS - 1
        return u // HALVES - 1 if u and u % HALVES == 0 else None

    T_CT = 4
    N_CT = (KT + T_CT) // T_CT
    parts_at = [-(-(c0 + wa + wb) // (T_CT * P)) for c0, wa, wb in chunks[0]]
    parts_at += [min(parts_at[-1] + 1 + c, N_CT) for c in range(CH)]
    parts_at += [parts_at[-1]]
    exp_steps = {4: (0, 0), 5: (0, 1), 6: (0, 2), 7: (0, 3), 9: (1, 0)}
    exp_late = {0: (1, 1), 1: (1, 2), 2: (1, 3)}
    exps = [(0, j, c) for (j, c) in exp_steps.values()]
    for u in range(UNITS):
        for g in range(NG):
            if g in exp_late:
                exps.append((u, *exp_late[g]))
            if g in exp_steps and u + 1 < UNITS:
                exps.append((u + 1, *exp_steps[g]))
    exp_at = {e: i for i, e in enumerate(exps)}
    RING = 4

    N_UNITS = DEPTH * NT
    GT = 4
    NG_F = NT // GT
    NBLK = (HID + P - 1) // P
    VS = 4
    blk = [(b * P, min(P, HID - b * P)) for b in range(NBLK)]
    HID_PAD = blk[-1][1] // 32 * 32
    B2_ROW = -(-blk[-1][1] // 32) * 32
    assert B2_ROW < P

    with ExitStack() as ctx:
        def sem(name):
            return ctx.enter_context(nc.semaphore(name))

        def sb(name, shape, dt=F32, stack=ctx):
            return stack.enter_context(nc.sbuf_tensor(name, shape, dt))

        psum = ctx.enter_context(nc.psum_tensor("psum", [P, 8, 512], F32))

        x_sb = sb("x_sb", [P, NT, D])
        y_sb = [sb(f"y{l}", [P, NT, D]) for l in range(DEPTH)]
        mat = sb("mat", [P, 3, P])
        ident, down, edge = mat[:, 0, :], mat[:, 1, :], mat[:, 2, :]
        stats = sb("stats", [P, NT, 6])
        mv = sb("mv", [P, NT, 2])
        rstd = sb("rstd", [P, NT, 1])
        minus_half = sb("minus_half", [P, 2 * H])
        warm = sb("warm", [1, 1])

        first = ExitStack()
        with first:
            a = lambda name, shape, dt=F32: sb(name, shape, dt, first)
            keyT = a("keyT", [P, 2, NKEYS], F32R)
            qh = a("qh", [P, 2, NT * P], F32R)
            qT = a("qT", [P, NT * P])
            w4 = a("w4", [P, 4, D])
            S0 = a("S0", [P, 2, hkeys[-1]])
            EARLY = 4 * (2 * NKEYS + 3 * NT * P + 4 * D + 2 * hkeys[-1])
            vals = a("vals", [P, 2, KT + 1, D], F32R)
            S1 = a("S1", [P, 2, hkeys[-1]])
            turned = a("turned", [P, RING, G, 2, 2 * P], F32R)
            LATE = EARLY + 4 * (2 * (KT + 1) * D + 2 * hkeys[-1] + RING * G * 4 * P)
            Sh = [S0, S1]
            pre = a("pre", [P, 2 * D + 1])
            woT, wqk, bqk = pre[:, 0:D], pre[:, D:2 * D], pre[:, 2 * D:2 * D + 1]
            wvo = a("wvo", [P, D])
            bqc = a("bqc", [P, 1])
            bvc = a("bvc", [P, 1])
            bvr = a("bvr", [P, P])
            bob = a("bob", [P, D])
            cmax = a("cmax", [P, UNITS, 2, CH])
            nmax = a("nmax", [P, UNITS, 2])
            zpart = a("zpart", [P, UNITS, 2, CH])
            accb = a("accb", [P, 2 * P])
            uT = a("uT", [P, 2 * P])
            oh = a("oh", [P, HALVES, 2, D])
            mmin = a("mmin", [P, 2])
            al = a("al", [P, HALVES, 2])
            zs = a("zs", [P, HALVES, 2])
            zt = a("zt", [P, 2])
            raw = S1[:, :, :].rearrange("p j k -> p (j k)")[:, 0:KT * D].rearrange("p (t d) -> p t d", d=D)
            rawt = a("rawt", [P, D])

        second = ExitStack()
        ctx.enter_context(second)
        taken_bytes = [0]

        def f(name, shape, dt=F32):
            taken_bytes[0] += 4 * int(np.prod(shape[1:]))
            return sb(name, shape, dt, second)

        wqkv_sb = f("wqkv_sb", [P, DEPTH, 3 * INNER])
        rotl = f("rotl", [P, DEPTH, NT, 2, 2, HD])
        sc_b = f("sc_b", [P, 2, DEPTH, HD])
        mask = f("mask", [P, 2, WIN + P])
        mask_r = f("mask_r", [P, 2, WIN + P], F32R)
        ident_r = f("ident_r", [P, P], F32R)
        assert taken_bytes[0] <= 4 * 2 * NKEYS
        kTh = f("kTh", [P, H // 2, WIN + NT * P])
        hT0 = f("hT0", [P, WIN + NT * P + 4])
        qk = f("qk", [P, 2, H, HD])
        sq = f("sq", [P, 2 * H, HD])
        ra = f("ra", [P, 2, 2, H, HD])
        rb = f("rb", [P, 2, H, HD])
        ss = f("ss", [P, 2 * H])
        rinv = f("rinv", [P, 3, 2 * H])
        qTh = f("qTh", [P, 2, H // 2, P])
        v_sb = f("v_sb", [P, VS, INNER])
        assert taken_bytes[0] <= EARLY, (taken_bytes[0], EARLY)
        hT = [hT0, f("hT1", [P, WIN + NT * P + 4])]
        wo_sb = f("wo_sb", [P, DEPTH, INNER // P, D])
        w1_sb = f("w1_sb", [P, DEPTH, 2 * HID])
        w2_sb = f("w2_sb", [P, DEPTH, NBLK, D])
        b1c = f("b1c", [P, DEPTH, 2, NBLK])
        lnc = f("lnc", [P, 2, DEPTH])
        v_prev = f("v_prev", [WIN, VS, INNER])
        mx = f("mx", [P, H])
        nb = f("nb", [P, 2, H])
        z = f("z", [P, 2, H])
        rz = f("rz", [P, H])
        prob = f("prob", [P, 2, H // 2, WIN + P])
        ptA = f("ptA", [P, 2, H // 2, P])
        ptB = f("ptB", [WIN, 2, H // 2, WIN])
        oT = f("oT", [P, INNER // P, P])
        y1 = [f(f"yatt{l}", [P, NT, D]) for l in range(DEPTH)]
        h2 = f("h2", [P, GT, D])
        hn = f("hn", [P, GT, D])
        fstats = f("fstats", [P, GT, 6])
        fmv = f("fmv", [P, GT, 2])
        fve = f("fve", [P, GT])
        frs = f("frs", [P, GT])
        last = f("last", [P, GT, D])
        h2T = f("h2T", [P, GT * P])
        gl = f("gl", [P, NBLK, GT * P])
        mid = f("mid", [P, NBLK, GT * P])
        assert taken_bytes[0] <= LATE

        ld_x, ld_w, ld_t, ld_m, ld_b = (sem(s) for s in ("ld_x", "ld_w", "ld_t", "ld_m", "ld_b"))
        LOADS = 5
        ld_c = [sem(f"ld_c{i}") for i in range(LOADS)]
        ld_s, ld_bq = sem("ld_s"), sem("ld_bq")
        stored = sem("stored")
        norm_parts = [slice(0, NT // 2), slice(NT // 2, NT), slice(0, NT - 2), slice(NT - 2, NT)]
        ld_qkv, ld_g, ld_k, ld_wo, ld_f = (sem(s) for s in ("ld_qkv", "ld_g", "ld_k", "ld_wo", "ld_f"))
        half_set = sem("half_set")
        dve_link, act_link, pool_link = sem("dve_link"), sem("act_link"), sem("pool_link")
        var_ready, rstd_ready, xn_ready = sem("var_ready"), sem("rstd_ready"), sem("xn_ready")
        pre_pe, pre_act = sem("pre_pe"), sem("pre_act")
        q_low, bvr_ready, bias_made = sem("q_low"), sem("bvr_ready"), sem("bias_made")
        x_turned, x_moved, q_made, q_high = sem("x_turned"), sem("x_moved"), sem("q_made"), sem("q_high")
        ct_ready, ct_high, ct_low = sem("ct_ready"), sem("ct_high"), sem("ct_low")
        vh_ready, vl_ready = sem("vh_ready"), sem("vl_ready")
        scores_ready, scores_moved = sem("scores_ready"), sem("scores_moved")
        max_ready, prob_ready = sem("max_ready"), sem("prob_ready")
        ring_ready, high_ready, ring_done = sem("ring_ready"), sem("high_ready"), sem("ring_done")
        pv_done, accb_ready, acc_read = sem("pv_done"), sem("accb_ready"), sem("acc_read")
        alpha_in, alpha_ready = sem("alpha_in"), sem("alpha_ready")
        last_made, last_read = sem("last_made"), sem("last_read")
        y0_ready = sem("y0_ready")
        x_out = sem("x_out")
        pads_set = sem("pads_set")
        rot_ready, ends_set, const_ready = sem("rot_ready"), sem("ends_set"), sem("const_ready")
        f_yT, f_hT, f_q, f_k, f_v, f_q_moved, f_k_moved, f_v_moved = (
            sem(s) for s in ("f_yT", "f_hT", "f_q", "f_k", "f_v", "f_q_moved", "f_k_moved", "f_v_moved"))
        f_vp = [sem(f"f_vp{i}") for i in range(VS)]
        f_sq, f_ss, f_rk, f_rinv, f_ra, f_rb, f_rsum, f_kn = (
            sem(s) for s in ("f_sq", "f_ss", "f_rk", "f_rinv", "f_ra", "f_rb", "f_rsum", "f_kn"))
        f_qT, f_kT, f_qT_moved, f_kT_moved = (sem(s) for s in ("f_qT", "f_kT", "f_qT_moved", "f_kT_moved"))
        a_s, a_nb, a_p, a_t, a_tb, a_tA, a_tB, a_o, a_pn, a_oTm, a_wo, a_y1 = (
            sem(s) for s in ("a_s", "a_nb", "a_p", "a_t", "a_tb", "a_tA", "a_tB", "a_o", "a_pn", "a_oTm",
                             "a_wo", "a_y1"))
        m_left = sem("m_left")
        m_sh, m_h2, m_var, m_rs, m_hn, m_hT, m_h2T, m_w1, m_gelu, m_mid, m_w2, m_y = (
            sem(s) for s in ("m_sh", "m_h2", "m_var", "m_rs", "m_hn", "m_hT", "m_h2T", "m_w1", "m_gelu",
                             "m_mid", "m_w2", "m_y"))
        block = ctx.enter_context(nc.Block())

        x_tok = x.rearrange("a (t p) d -> p (a t) d", p=P)
        out_tok = out.rearrange("a (t p) d -> p (a t) d", p=P)
        ctx_whole = ctx_1024[0, 0:KT * P, :].rearrange("(p t) d -> p t d", p=P)
        piece = KT // LOADS

        FFN_LOADS = 2 + DEPTH * (3 * NBLK + 2)
        G_LOADS = 3 * DEPTH

        @block.sync
        def _(sp):
            sp.dma_start(x_sb[:, :, :], x_tok).then_inc(ld_x, 16)
            sp.dma_start(ident, mats[:, 0, :]).then_inc(ld_m, 16)

            def load_context(i):
                sp.dma_start(raw[:, i * piece:(i + 1) * piece, :],
                             ctx_whole[:, i * piece:(i + 1) * piece, :]).then_inc(ld_c[i], 16)

            def load_weight(i, w):
                sp.dma_start(w4[:, i, :], w).then_inc(ld_w, 16)

            load_context(0)
            load_weight(3, Wo)
            load_weight(0, Wq)
            load_weight(1, Wk)
            sp.dma_start(bqc[:, :], bq.rearrange("(p a) -> p a", a=1)).then_inc(ld_bq, 16)
            load_weight(2, Wv)
            load_context(1)
            sp.dma_start(bvc[:, :], bv.rearrange("(p a) -> p a", a=1)).then_inc(ld_b, 16)
            sp.dma_start(bob[:, :], bo.rearrange("(a d) -> a d", a=1).broadcast_to([P, D])).then_inc(ld_b, 16)
            for i in range(2, LOADS):
                load_context(i)
            sp.dma_start(rawt[0:TAIL, :], ctx_1024[0, KT * P:NKEYS, :]).then_inc(ld_t, 16)
            sp.dma_start(mat[:, 1:3, :], mats[:, 1:3, :]).then_inc(ld_s, 16)

            sp.wait_ge(scores_ready, UNITS * 2 * CH)
            sp.dma_start(wqkv_sb[:, :, :], wqkv.rearrange("l p n -> p l n")).then_inc(ld_qkv, 16)
            for l in range(DEPTH):
                sp.dma_start(rotl[:, l, :, :, :, :],
                             rot_tab.rearrange("p t (c k d) -> p t c k d", c=2, k=2)).then_inc(ld_g, 16)
                for i, s in enumerate((q_scale, k_scale)):
                    sp.dma_start(sc_b[:, i, l, :], s[l:l + 1, :].broadcast_to([P, HD])).then_inc(ld_g, 16)
            sp.dma_start(mask[:, :, :], mask_tab).then_inc(ld_k, 16)
            sp.wait_ge(pv_done, UNITS * NG)
            sp.dma_start(wo_sb[:, :, :, :], wo.rearrange("l (c p) n -> p l c n", p=P)).then_inc(ld_wo, 16)
            sp.dma_start(w1_sb[:, :, :], w1.rearrange("l p n -> p l n")).then_inc(ld_f, 16)
            for l in range(DEPTH):
                for b, (c0, w) in enumerate(blk):
                    if b == NBLK - 1:
                        sp.wait_ge(pads_set, 1)
                    sp.dma_start(w2_sb[0:w, l, b, :], w2[l, c0:c0 + w, :]).then_inc(ld_f, 16)
                    for k in range(2):
                        sp.dma_start(b1c[0:w, l, k, b:b + 1],
                                     b1[l, k * HID + c0:k * HID + c0 + w].rearrange("(p a) -> p a", a=1)).then_inc(ld_f, 16)
                sp.dma_start(lnc[:, 0, l:l + 1], ln_g[l, :].rearrange("(p a) -> p a", a=1)).then_inc(ld_f, 16)
                sp.dma_start(lnc[:, 1, l:l + 1], ln_b[l, :].rearrange("(p a) -> p a", a=1)).then_inc(ld_f, 16)
            sp.dma_start(w2_sb[B2_ROW:B2_ROW + 1, :, NBLK - 1, :], b2.rearrange("(a l) d -> a l d", a=1)).then_inc(ld_f, 16)

            for n in range(N_UNITS):
                sp.wait_ge(f_v_moved, n + 1)
                if n >= VS:
                    sp.wait_ge(a_o, 2 * (n - VS + 2))
                sp.dma_start(v_prev[:, n % VS, :], v_sb[WIN:2 * WIN, n % VS, :]).then_inc(f_vp[n % VS], 16)
            for g in range(NT // GT):
                sp.wait_ge(x_out, g + 1)
                sp.dma_start(out_tok[:, g * GT:(g + 1) * GT, :], x_sb[:, g * GT:(g + 1) * GT, :]).then_inc(stored, 16)
            sp.wait_ge(stored, 16 * (NT // GT))


        def three(pe, o, lh, ll, rh, rl):
            pe.matmul(o, lh, rh, start=True, stop=False)
            pe.matmul(o, lh, rl, start=False, stop=False)
            return pe.matmul(o, ll, rh, start=False, stop=True)

        def keep_busy(pe, bank, times):
            for _ in range(times):
                pe.matmul(psum[:, bank, 0:3 * P], ident, mat[:, :, :].rearrange("p a b -> p (a b)"), start=True, stop=True)

        x_bank, q_bank = [2, 6], [0, 7]

        def cross_tensor(pe):
            def turn_context(i):
                if i >= 4:
                    pe.wait_ge(ct_low, i - 3)
                for s_, t in enumerate(range(T_CT * i, min(T_CT * i + T_CT, KT + 1))):
                    b = psum[:, 4 + i % 4, s_ * P:(s_ + 1) * P]
                    if t < KT:
                        pe.wait_ge(ld_c[t // piece], 16)
                        m = pe.transpose(b, raw[:, t, :], ident)
                    else:
                        pe.wait_ge(ld_t, 16)
                        m = pe.transpose(b[:, 0:TAIL], rawt[0:TAIL, :], ident[0:TAIL, 0:TAIL])
                m.then_inc(ct_ready, 1)

            def turn_x(b):
                pe.wait_ge(xn_ready, b + 1)
                for t in range(4):
                    m = pe.transpose(psum[:, x_bank[b], t * P:(t + 1) * P], y_sb[0][:, 4 * b + t, :], ident)
                m.then_inc(x_turned, 1)

            def query(b):
                pe.wait_ge(x_moved, b + 1)
                pe.wait_ge(pre_act, 2)
                pe.matmul(psum[:, q_bank[b], :], wqk, qT[:, b * 512:(b + 1) * 512], start=True, stop=True).then_inc(q_made, 1)

            pe.wait_ge(ld_m, 16)
            turn_context(0)
            pe.wait_ge(ld_w, 64)
            pe.wait_ge(ld_bq, 16)
            pe.transpose(psum[:, 0, 0:D], w4[:, 3, :], ident)
            pe.matmul(psum[:, 0, D:2 * D], w4[:, 0, :], w4[:, 1, :], start=True, stop=True)
            pe.matmul(psum[:, 0, 2 * D:2 * D + 1], w4[:, 1, :], bqc[:, :], start=True, stop=True).then_inc(pre_pe, 1)
            turn_x(0)
            pe.wait_ge(pre_act, 1)
            pe.wait_ge(bvr_ready, 1)
            pe.matmul(psum[:, 1, 0:D], w4[:, 2, :], woT, start=True, stop=True)
            pe.matmul(psum[:, 1, D:2 * D], bvr[:, :], woT, start=True, stop=True).then_inc(pre_pe, 1)
            turn_context(1)
            query(0)
            for i in range(2, parts_at[0]):
                turn_context(i)

            def scores(u, j, c):
                p, h = divmod(u, HALVES)
                k = (u * 2 + j) * CH + c
                c0, *widths = chunks[h][c]
                if k >= 2:
                    pe.wait_ge(scores_moved, k - 1)
                rows = slice((2 * p + j) * P, (2 * p + j + 1) * P)
                for b, w in enumerate(widths):
                    cols = slice(half0[h] + c0 + b * CB, half0[h] + c0 + b * CB + w)
                    m = three(pe, psum[:, 2 * (k % 2) + b, 0:w], qh[:, 0, rows], qh[:, 1, rows],
                              keyT[:, 0, cols], keyT[:, 1, cols])
                m.then_inc(scores_ready, 1)

            def enter(e):
                i = at[e]
                if i >= 2:
                    pe.wait_ge(ring_done, i - 1)
                return psum[:, 4 + i % 2, :]

            def turn(u, g):
                h = u % HALVES
                last = group(h, g)[-1]
                c = min((last[0] + last[1] - 1) // (2 * CB), CH - 1)
                pe.wait_ge(prob_ready, max(exp_at[u, 0, c], exp_at[u, 1, c]) + 1)
                b = enter(("T", u, g))
                for s, (c0, rows, _) in enumerate(group(h, g)):
                    for j in range(2):
                        m = pe.transpose(b[0:rows, s * 256 + j * P:s * 256 + (j + 1) * P],
                                         Sh[h][:, j, c0:c0 + rows], ident)
                m.then_inc(ring_ready, 1)

            def weigh(u, g):
                h = u % HALVES
                if g == 0 and u:
                    pe.wait_ge(acc_read, u)
                i = at["T", u, g]
                pe.wait_ge(ring_done, i + 1)
                slot = (u * NG + g) % RING
                for s, (c0, rows, t) in enumerate(group(h, g)):
                    if u < HALVES:
                        pe.wait_ge(vl_ready, t // piece + 1)
                    start, stop = g == 0 and s == 0, g == NG - 1 and s == len(group(h, g)) - 1
                    pe.matmul(psum[:, 6, :], vals[0:rows, 0, t, :],
                              turned[0:rows, slot, s, :, :].rearrange("p a b -> p (a b)"), start=start, stop=stop)
                    m = pe.matmul(psum[:, 7, 0:256], vals[0:rows, 1, t, :], turned[0:rows, slot, s, 0, :],
                                  start=start, stop=stop)
                m.then_inc(pv_done, 1)

            def output(u):
                b = enter(("O", u, 0))
                pe.wait_ge(acc_read, u + 1)
                for j in range(2):
                    m = pe.matmul(b[:, j * P:(j + 1) * P], uT[:, j * P:(j + 1) * P], wvo[:, :], start=True, stop=True)
                m.then_inc(ring_ready, 1)

            for k in range(2 * CH):
                for i in range(parts_at[k], parts_at[k + 1]):
                    turn_context(i)
                if k == 2 * CH - 1:
                    turn_context(parts_at[-1])
                if k == 0:
                    pe.wait_ge(q_low, 1)
                    pe.wait_ge(bias_made, 1)
                pe.wait_ge(ct_low, parts_at[k])
                scores(0, *divmod(k, CH))
            for i in range(parts_at[-1] + 1, N_CT):
                turn_context(i)
            pe.wait_ge(ld_s, 16)
            keep_busy(pe, 5, 2)
            pe.wait_ge(ct_low, N_CT)
            turn_x(1)
            for u in range(UNITS):
                for g in range(NG):
                    turn(u, g)
                    if u == 0 and g == 0:
                        query(1)
                    if u == 0 and g == 2:
                        pe.wait_ge(q_low, 2)
                    if u and g == 3:
                        output(u - 1)
                    if g in SC_STEP and u + 1 < UNITS:
                        scores(u + 1, *divmod(SC_STEP[g], CH))
                    if u == UNITS - 1:
                        if g == 2:
                            pe.wait_ge(scores_moved, UNITS * 2 * CH)
                            turn_y(pe, 0)
                        if g == 4:
                            project(pe, 0)
                        if g == 5:
                            turn_y(pe, 1)
                        if g == 9:
                            project(pe, 1)
                    if g >= 2:
                        weigh(u, g - 2)
                weigh(u, NG - 2)
                if u == UNITS - 1:
                    turn_q(pe, 0)
                    turn_k(pe, 0)
                weigh(u, NG - 1)

        def last_output(pe):
            pe.wait_ge(acc_read, UNITS)
            for j in range(2):
                m = pe.matmul(psum[:, 6, j * P:(j + 1) * P], uT[:, j * P:(j + 1) * P], wvo[:, :], start=True, stop=True)
            m.then_inc(last_made, 1)

        def place(n):
            return divmod(n, NT)

        def is_unit(n):
            return 0 <= n < N_UNITS

        def group_from(n, lag):
            m = n - lag
            return m // GT - 1 if m > 0 and m % GT == 0 and m // GT - 1 < DEPTH * NG_F else None

        LAST_STEP = N_UNITS + 3
        front = []
        for n in range(-2, LAST_STEP):
            own = [(kind, n + 2) for kind in ("yT", "q", "k", "v")] if is_unit(n + 2) else []
            following = [(kind, n + 1) for kind in ("qT", "kT")] if is_unit(n + 1) else []
            if group_from(n, 2) is not None:
                front += [("hn", group_from(n, 2)), ("w2", group_from(n, 2))] + following + own
            else:
                front += own + following
            if group_from(n, 0) is not None:
                front.append(("shift", group_from(n, 0)))
        fat = {e: i for i, e in enumerate(front)}
        taken = {"yT": f_hT, "q": f_q_moved, "k": f_k_moved, "v": f_v_moved, "qT": f_qT_moved, "kT": f_kT_moved,
                 "w2": m_y, "hn": m_h2T, "shift": m_h2}

        def front_bank(kind, n):
            return fat[kind, n] % 2

        def enter_front(pe, kind, n):
            i = fat[kind, n]
            if i >= 2:
                before, m = front[i - 2]
                pe.wait_ge(taken[before], m + 1)
            return psum[:, i % 2, :]

        def turn_y(pe, n):
            l, t = place(n)
            if l == 0:
                pe.wait_ge(y0_ready, t // 2 + 1)
            else:
                pe.wait_ge(m_y, (l - 1) * NG_F + t // GT + 1)
            b = enter_front(pe, "yT", n)
            pe.transpose(b[:, 0:P], y_sb[l][:, t, :], ident).then_inc(f_yT, 1)

        def project(pe, n, kinds="qkv"):
            l, t = place(n)
            if n == 0:
                pe.wait_ge(ld_qkv, 16)
            pe.wait_ge(f_hT, n + 1)
            h = hT[l][:, WIN + t * P:WIN + (t + 1) * P]
            for i, (kind, made) in enumerate((("q", f_q), ("k", f_k), ("v", f_v))):
                if kind not in kinds:
                    continue
                b = enter_front(pe, kind, n)
                pe.matmul(b[:, 0:INNER], h, wqkv_sb[:, l, i * INNER:(i + 1) * INNER], start=True, stop=True)\
                  .then_inc(made, 1)

        def turn_q(pe, n):
            pe.wait_ge(f_rsum, n + 1)
            b = enter_front(pe, "qT", n)
            for a_ in range(H // 2):
                m = pe.transpose(b[:, a_ * P:(a_ + 1) * P],
                                 ra[:, n % 2, 0, 2 * a_:2 * a_ + 2, :].rearrange("p h d -> p (h d)"), ident)
            m.then_inc(f_qT, 1)

        def turn_k(pe, n):
            pe.wait_ge(f_kn, n + 1)
            b = enter_front(pe, "kT", n)
            for a_ in range(H // 2):
                m = pe.transpose(b[:, a_ * P:(a_ + 1) * P],
                                 ra[:, n % 2, 1, 2 * a_:2 * a_ + 2, :].rearrange("p h d -> p (h d)"), ident)
            m.then_inc(f_kT, 1)

        def moved_b(i):
            return sum(k // 2 % NT > 0 for k in range(i + 1))

        def att_scores(pe, n, hg):
            l, t = place(n)
            pe.wait_ge(f_qT_moved, n + 1)
            pe.wait_ge(f_kT_moved, n + 1)
            if n == 0 and hg == 0:
                pe.wait_ge(const_ready, 2)
                pe.wait_ge(ends_set, 1)
            if n:
                pe.wait_ge(a_tA, 2 * (n - 1) + hg + 1)
                if moved_b(2 * (n - 1) + hg):
                    pe.wait_ge(a_tB, moved_b(2 * (n - 1) + hg))
            for b in range(2):
                pe.matmul(psum[:, 2 + 2 * hg + b, 0:2 * (WIN + P)].rearrange("p (h k) -> p h k", h=2), ident_r[:, :],
                          mask_r[:, min(t, 1), :].unsqueeze(1).broadcast_to([P, 2, WIN + P]), start=True, stop=False)
            for e in range(2):
                pr = 2 * hg + e
                for b in range(2):
                    rows = slice(b * HD, (b + 1) * HD)
                    m = pe.matmul(psum[:, 2 + 2 * hg + b, e * (WIN + P):(e + 1) * (WIN + P)], qTh[rows, n % 2, pr, :],
                                  kTh[rows, pr, t * P:t * P + WIN + P], start=False, stop=(e == 1))
            m.then_inc(a_s, 1)

        def att_turn(pe, n, hg):
            l, t = place(n)
            pe.wait_ge(a_pn, 2 * n + hg + 1)
            for e in range(H // 2):
                m = pe.transpose(psum[:, 2 + 2 * hg, e * P:(e + 1) * P], prob[:, hg, e, WIN:WIN + P], ident)
            m.then_inc(a_t, 1)
            if t:
                for e in range(H // 2):
                    m = pe.transpose(psum[0:WIN, 3 + 2 * hg, e * WIN:(e + 1) * WIN], prob[0:WIN, hg, e, 0:WIN],
                                     ident[0:WIN, 0:WIN])
                m.then_inc(a_tb, 1)

        def att_weigh(pe, n, hg):
            l, t = place(n)
            i = 2 * n + hg
            pe.wait_ge(a_tA, i + 1)
            pe.wait_ge(f_v_moved, n + 1)
            if t:
                pe.wait_ge(a_tB, moved_b(i))
                pe.wait_ge(f_vp[(n - 1) % VS], 16 * ((n - 1) // VS + 1))
            if hg == 0 and n:
                pe.wait_ge(a_oTm, n)
            elif hg == 0:
                pe.wait_ge(accb_ready, UNITS)
            for pr in range(H // 4 * hg, H // 4 * (hg + 1)):
                heads = [(2 * pr + c, slice(c * HD, (c + 1) * HD)) for c in range(2)]
                for hd, rows in heads:
                    m = pe.matmul(psum[rows, 7, pr * P:(pr + 1) * P], v_sb[:, n % VS, hd * HD:(hd + 1) * HD],
                                  ptA[:, hg, hd % (H // 2), :], start=True, stop=not t, skip_group_check=True)
                if t:
                    for hd, rows in heads:
                        m = pe.matmul(psum[rows, 7, pr * P:pr * P + WIN], v_prev[:, (n - 1) % VS, hd * HD:(hd + 1) * HD],
                                      ptB[:, hg, hd % (H // 2), :], start=False, stop=True, skip_group_check=True)
            m.then_inc(a_o, 1)

        def out_proj(pe, n):
            l, t = place(n)
            if n == 0:
                pe.wait_ge(ld_wo, 16)
                pe.wait_ge(last_read, 1)
            else:
                pe.wait_ge(a_y1, n)
            pe.wait_ge(a_oTm, n + 1)
            for a_ in range(INNER // P):
                m = pe.matmul(psum[:, 6, 0:D], oT[:, a_, :], wo_sb[:, l, a_, :], start=(a_ == 0),
                              stop=(a_ == INNER // P - 1))
            m.then_inc(a_wo, 1)

        w1_order = [(kind, b) for b in range(NBLK) for kind in (1, 0)]

        def shift(pe, k):
            l, g = divmod(k, NG_F)
            if k == 0:
                pe.wait_ge(ld_f, 16 * FFN_LOADS)
                pe.wait_ge(ld_s, 16)
            pe.wait_ge(a_y1, (k + 1) * GT)
            bank = enter_front(pe, "shift", k)
            for s in range(GT):
                t = g * GT + s
                o = bank[:, s * HD:(s + 1) * HD]
                m = pe.matmul(o, down, y1[l][:, t, HD:D], start=True, stop=(t == 0), skip_group_check=True)
                if t:
                    m = pe.matmul(o, edge, y1[l][:, t - 1, HD:D], start=False, stop=True, skip_group_check=True)
            m.then_inc(m_sh, 1)

        def turn_hn(pe, k):
            pe.wait_ge(m_hn, k + 1)
            bank = enter_front(pe, "hn", k)
            for s in range(GT):
                m = pe.transpose(bank[:, s * P:(s + 1) * P], hn[:, s, :], ident)
            m.then_inc(m_hT, 1)

        def hidden(pe, k, blocks):
            l = k // NG_F
            pe.wait_ge(m_h2T, k + 1)
            done = min((k + 1) * GT + 2, N_UNITS)
            pe.wait_ge(a_y1, min(done, (k + 1) * GT + 1))
            for i in blocks:
                kind, b = w1_order[i]
                if i == 1:
                    pe.wait_ge(a_oTm, done)
                if i >= 2:
                    pe.wait_ge(m_gelu if kind else m_mid, k * NBLK + b)
                c0, w = blk[b]
                pe.matmul(psum[0:w, 6 + i % 2, :], w1_sb[:, l, kind * HID + c0:kind * HID + c0 + w],
                          h2T[:, :], start=True, stop=True).then_inc(m_w1, 1)

        def feed_out(pe, k, b):
            l = k // NG_F
            bank = enter_front(pe, "w2", k) if b == 0 else psum[:, front_bank("w2", k), :]
            pe.wait_ge(m_mid, k * NBLK + b + 1)
            rows = blk[b][1] if b < NBLK - 1 else B2_ROW + 1
            for s in range(GT):
                m = pe.matmul(bank[:, s * D:(s + 1) * D], mid[0:rows, b, s * P:(s + 1) * P], w2_sb[0:rows, l, b, :],
                              start=(b == 0 and s == 0), stop=(b == NBLK - 1), skip_group_check=True)
            if b == NBLK - 1:
                m.then_inc(m_w2, 1)

        @block.tensor
        def _(pe):
            cross_tensor(pe)
            for n in range(0, LAST_STEP):
                feed = group_from(n, 2) is not None
                if is_unit(n + 2) and not feed:
                    turn_y(pe, n + 2)
                if is_unit(n):
                    att_scores(pe, n, 0)
                if n == N_UNITS + 2:
                    keep_busy(pe, 2, 6)
                if feed:
                    turn_hn(pe, group_from(n, 2))
                if n == N_UNITS + 2:
                    keep_busy(pe, 2, 1)
                if n == N_UNITS:
                    keep_busy(pe, 2, 2)
                if is_unit(n - 1):
                    att_turn(pe, n - 1, 1)
                if is_unit(n + 2) and not feed:
                    project(pe, n + 2, "qk")
                if feed:
                    hidden(pe, group_from(n, 2), range(1))
                if n == N_UNITS - 1:
                    enter_front(pe, "shift", DEPTH * NG_F - 1)
                    keep_busy(pe, front_bank("shift", DEPTH * NG_F - 1), 2)
                if n == N_UNITS:
                    keep_busy(pe, 2, 1)
                if is_unit(n - 1):
                    att_weigh(pe, n - 1, 1)
                if is_unit(n):
                    att_scores(pe, n, 1)
                if is_unit(n + 2) and not feed:
                    project(pe, n + 2, "v")
                if n == 0:
                    last_output(pe)
                if feed:
                    hidden(pe, group_from(n, 2), range(1, 2 * NBLK))
                    if n > N_UNITS:
                        keep_busy(pe, 2, 1)
                    for b in range(NBLK - 1):
                        feed_out(pe, group_from(n, 2), b)
                if is_unit(n + 1):
                    turn_q(pe, n + 1)
                if feed:
                    feed_out(pe, group_from(n, 2), NBLK - 1)
                if is_unit(n) and not feed:
                    att_turn(pe, n, 0)
                if is_unit(n - 1) and feed:
                    out_proj(pe, n - 1)
                if is_unit(n + 1):
                    turn_k(pe, n + 1)
                if n == N_UNITS - 1:
                    keep_busy(pe, front_bank("shift", DEPTH * NG_F - 1), 2)
                if n == N_UNITS:
                    keep_busy(pe, 2, 1)
                if is_unit(n) and feed:
                    att_turn(pe, n, 0)
                if is_unit(n + 2) and feed:
                    turn_y(pe, n + 2)
                if is_unit(n - 1) and not feed:
                    out_proj(pe, n - 1)
                if is_unit(n + 2) and feed:
                    project(pe, n + 2)
                if n == N_UNITS - 2:
                    enter_front(pe, "shift", DEPTH * NG_F - 1)
                    keep_busy(pe, front_bank("shift", DEPTH * NG_F - 1), 1)
                if is_unit(n):
                    att_weigh(pe, n, 0)
                if group_from(n, 0) is not None:
                    shift(pe, group_from(n, 0))

        @block.scalar
        def _(act):
            def context_high(i):
                c0, w = 512 * i, min(512, NKEYS - 512 * i)
                act.wait_ge(ct_ready, i + 1)
                act.copy(keyT[:, 0, c0:c0 + w], psum[:, 4 + i % 4, 0:w]).then_inc(ct_high, 1)

            def move_x(b):
                act.wait_ge(x_turned, b + 1)
                act.copy(qT[:, b * 512:(b + 1) * 512], psum[:, x_bank[b], :]).then_inc(x_moved, 1)

            def query_high(b):
                act.wait_ge(q_made, b + 1)
                act.activation(qh[:, 0, b * 512:(b + 1) * 512], psum[:, q_bank[b], :], ACT.Identity, bias=bqk).then_inc(q_high, 1)

            def values_high(i):
                if i < LOADS:
                    act.wait_ge(ld_c[i], 16)
                    ts = slice(i * piece, (i + 1) * piece)
                    act.copy(vals[:, 0, ts, :], raw[:, ts, :]).then_inc(vh_ready, 1)
                else:
                    act.wait_ge(ld_t, 16)
                    act.copy(vals[0:TAIL, 0, KT, :], rawt[0:TAIL, :]).then_inc(vh_ready, 1)

            def expo(u, j, c):
                h = u % HALVES
                act.wait_ge(max_ready, 2 * u + j + 1)
                c0, *widths = chunks[h][c]
                s = Sh[h][:, j, c0:c0 + sum(widths)]
                act.activation(s, s, ACT.Exp, bias=nmax[:, u, j:j + 1],
                               accum_out=zpart[:, u, j, c:c + 1]).then_inc(prob_ready, 1)

            context_high(0)
            act.wait_ge(pre_pe, 1)
            act.copy(pre[:, :], psum[:, 0, 0:2 * D + 1]).then_inc(pre_act, 1)
            move_x(0)
            act.wait_ge(pre_pe, 2)
            act.copy(wvo[:, :], psum[:, 1, 0:D]).then_inc(pre_act, 1)
            context_high(1)
            query_high(0)
            values_high(0)
            values_after = (3, 4, 6, 8, 12)
            exps_after = (8, 9, 10, 11)
            for i in range(2, N_CT):
                context_high(i)
                if i in values_after:
                    values_high(values_after.index(i) + 1)
                if i in exps_after:
                    expo(0, 0, exps_after.index(i))

            def high(u, g):
                act.wait_ge(ring_ready, at["T", u, g] + 1)
                k = u * NG + g
                if k >= RING:
                    act.wait_ge(pv_done, k - RING + 1)
                tiles = group(u % HALVES, g)
                rows = tiles[0][1]
                if all(r == P for _, r, _ in tiles):
                    w = len(tiles)
                    act.copy(turned[:, k % RING, 0:w, 0, :],
                             psum[:, 4 + at["T", u, g] % 2, 0:256 * w].rearrange("p (a b) -> p a b", b=256))\
                       .then_inc(high_ready, 1)
                else:
                    for s, (_, r, _) in enumerate(tiles):
                        m = act.copy(turned[0:r, k % RING, s, 0, :],
                                     psum[0:r, 4 + at["T", u, g] % 2, 256 * s:256 * (s + 1)])
                    m.then_inc(high_ready, 1)

            def acc_b(u):
                act.wait_ge(pv_done, (u + 1) * NG)
                if u:
                    act.wait_ge(acc_read, u)
                act.copy(accb[:, :], psum[:, 7, 0:256]).then_inc(accb_ready, 1)

            def alphas(p):
                act.wait_ge(alpha_in, p + 1)
                act.activation(al[:, :, :], al[:, :, :], ACT.Exp).then_inc(alpha_ready, 1)

            def query_move(n):
                act.wait_ge(f_q, n + 1)
                if n:
                    act.wait_ge(f_sq, n)
                    act.wait_ge(f_ra, n)
                    act.wait_ge(f_rb, n)
                act.copy(qk[:, 0, :, :], psum[:, front_bank("q", n), :].rearrange("p (h d) -> p h d", h=H))\
                   .then_inc(f_q_moved, 1)

            def key_move(n):
                act.wait_ge(f_k, n + 1)
                if n:
                    act.wait_ge(f_ra, n)
                    act.wait_ge(f_rb, n)
                act.copy(qk[:, 1, :, :], psum[:, front_bank("k", n), :].rearrange("p (h d) -> p h d", h=H))\
                   .then_inc(f_k_moved, 1)

            def value_move(n):
                act.wait_ge(f_v, n + 1)
                if n >= VS:
                    act.wait_ge(a_o, 2 * (n - VS + 1))
                    act.wait_ge(f_vp[n % VS], 16 * (n // VS))
                act.copy(v_sb[:, n % VS, :], psum[:, front_bank("v", n), :]).then_inc(f_v_moved, 1)

            def squares(n):
                act.wait_ge(f_q_moved, n + 1)
                act.wait_ge(f_k_moved, n + 1)
                if n:
                    act.wait_ge(f_ss, n)
                act.activation(sq[:, :, :], qk[:, :, :, :].rearrange("p k h d -> p (k h) d"), ACT.Square).then_inc(f_sq, 1)

            def probs(n, hg):
                i = 2 * n + hg
                act.wait_ge(a_nb, i + 1)
                if i >= 2:
                    act.wait_ge(a_t, i - 1)
                    if moved_b(i - 2):
                        act.wait_ge(a_tb, moved_b(i - 2))
                if n >= 2 and hg == 0:
                    act.wait_ge(a_pn, 2 * (n - 1))
                for e in range(H // 2):
                    hd = hg * (H // 2) + e
                    m = act.activation(prob[:, hg, e, :],
                                       psum[:, 2 + 2 * hg + e % 2, (e // 2) * (WIN + P):(e // 2 + 1) * (WIN + P)],
                                       ACT.Exp, bias=nb[:, n % 2, hd:hd + 1], scale=rinv[:, n % 3, hd:hd + 1],
                                       accum_out=z[:, n % 2, hd:hd + 1])
                m.then_inc(a_p, 1)

            def turned_a(n, hg):
                i = 2 * n + hg
                act.wait_ge(a_t, i + 1)
                if i >= 2:
                    act.wait_ge(a_o, i - 1)
                act.copy(ptA[:, hg, :, :], psum[:, 2 + 2 * hg, :].rearrange("p (a t) -> p a t", t=P)).then_inc(a_tA, 1)

            def o_turned(n):
                act.wait_ge(a_o, 2 * n + 2)
                if n:
                    act.wait_ge(a_wo, n)
                act.copy(oT[:, :, :], psum[:, 7, :].rearrange("p (a t) -> p a t", t=P)).then_inc(a_oTm, 1)

            def shifted(k):
                act.wait_ge(m_sh, k + 1)
                if k:
                    act.wait_ge(m_hn, k)
                act.copy(h2[:, :, HD:D], psum[:, front_bank("shift", k), 0:GT * HD].rearrange("p (s d) -> p s d", d=HD))\
                   .then_inc(m_h2, 1)

            def hn_turned(k):
                l = k // NG_F
                act.wait_ge(m_hT, k + 1)
                if k:
                    act.wait_ge(m_w1, 2 * NBLK * k)
                act.activation(h2T[:, :], psum[:, front_bank("hn", k), :], ACT.Identity, bias=lnc[:, 1, l:l + 1],
                               scale=lnc[:, 0, l:l + 1]).then_inc(m_h2T, 1)

            def gates(k):
                l = k // NG_F
                act.activation(warm[:, :], minus_half[0:1, 0:1], ACT.Gelu)
                if k:
                    act.wait_ge(m_mid, k * NBLK)
                for b, (c0, w) in enumerate(blk):
                    act.wait_ge(m_w1, 2 * NBLK * k + 2 * b + 1)
                    act.activation(gl[0:w, b, :], psum[0:w, 6, :], ACT.Gelu,
                                   bias=b1c[0:w, l, 1, b:b + 1]).then_inc(m_gelu, 1)

            expo(0, 1, 0)
            move_x(1)
            for u in range(UNITS):
                for g in range(NG):
                    high(u, g)
                    if u == 0 and g == 0:
                        query_high(1)
                    if g in exp_late:
                        expo(u, *exp_late[g])
                    if g in exp_steps and u + 1 < UNITS:
                        expo(u + 1, *exp_steps[g])
                    if g == 4 and merges_at(u) is not None:
                        alphas(merges_at(u))
                    if u == UNITS - 1:
                        if g == 4:
                            query_move(0)
                            key_move(0)
                            value_move(0)
                        if g == 5:
                            squares(0)
                        if g == 9:
                            query_move(1)
                            key_move(1)
                            value_move(1)
                        if g == 10:
                            squares(1)
                acc_b(u)

            for n in range(0, LAST_STEP):
                feed = group_from(n, 2) is not None
                if feed:
                    hn_turned(group_from(n, 2))
                if is_unit(n - 1):
                    turned_a(n - 1, 1)
                if feed:
                    if is_unit(n - 1):
                        o_turned(n - 1)
                    gates(group_from(n, 2))
                if is_unit(n):
                    probs(n, 0)
                if is_unit(n - 1) and not feed:
                    o_turned(n - 1)
                if is_unit(n + 2) and not feed:
                    query_move(n + 2)
                    key_move(n + 2)
                    value_move(n + 2)
                if is_unit(n) and not feed:
                    turned_a(n, 0)
                if is_unit(n):
                    probs(n, 1)
                if n == N_UNITS - 1:
                    act.activation(warm[:, :], minus_half[0:1, 0:1], ACT.Gelu)
                if is_unit(n + 2) and not feed:
                    squares(n + 2)
                if is_unit(n) and feed:
                    turned_a(n, 0)
                if is_unit(n + 2) and feed:
                    query_move(n + 2)
                    key_move(n + 2)
                    value_move(n + 2)
                    squares(n + 2)
                if group_from(n, 0) is not None:
                    shifted(group_from(n, 0))

        @block.gpsimd
        def _(pool):
            pool.memset(minus_half[:, :], -0.5).then_inc(half_set, 1)
            pool.wait_ge(half_set, 1)

            def powers(i, tiles):
                pool.wait_ge(var_ready, i + 1)
                pool.tensor_tensor(rstd[:, tiles, 0], rstd[:, tiles, 0], minus_half[:, tiles], ALU.pow).then_inc(rstd_ready, 1)

            powers(0, norm_parts[0])
            powers(1, norm_parts[1])
            for i in range(LOADS):
                ts = slice(i * piece, (i + 1) * piece)
                pool.wait_ge(vh_ready, i + 1)
                pool.tensor_tensor(vals[:, 1, ts, :], raw[:, ts, :], vals[:, 0, ts, :].bitcast(F32), ALU.subtract)\
                    .then_inc(vl_ready, 1)
            pool.wait_ge(vh_ready, LOADS + 1)
            pool.tensor_tensor(vals[0:TAIL, 1, KT, :], rawt[0:TAIL, :], vals[0:TAIL, 0, KT, :].bitcast(F32),
                               ALU.subtract).then_inc(vl_ready, 1)
            powers(2, norm_parts[2])

            pool.wait_ge(ld_k, 16)
            pool.tensor_copy(mask_r[:, :, :], mask[:, :, :]).then_inc(const_ready, 1)
            pool.tensor_copy(ident_r[:, :], ident).then_inc(const_ready, 1)
            pool.wait_ge(ld_g, 16 * G_LOADS)
            pool.tensor_scalar(sc_b[:, 0, :, :], sc_b[:, 0, :, :], QK_SCALE, None, ALU.mult).then_inc(pool_link, 1)
            pool.wait_ge(pool_link, 1)
            hh = HD // 2

            def scale_table(l, k):
                r = rotl[:, l, :, 0, k, :]
                pool.tensor_tensor(r, r, sc_b[:, k, l, :].unsqueeze(1).broadcast_to([P, NT, HD]), ALU.mult)
                for e in range(2):
                    r = rotl[:, l, :, 1, k, e * hh:(e + 1) * hh]
                    m = pool.tensor_tensor(r, r, sc_b[:, k, l, (1 - e) * hh:(2 - e) * hh].unsqueeze(1)
                                           .broadcast_to([P, NT, hh]), ALU.mult)
                m.then_inc(rot_ready, 1)

            for k in range(2):
                scale_table(0, k)

            def rotate(n):
                l, t = place(n)
                if t == 0:
                    pool.wait_ge(rot_ready, 2 * (l + 1))
                pool.wait_ge(f_q_moved, n + 1)
                pool.wait_ge(f_k_moved, n + 1)
                if n:
                    pool.wait_ge(f_rsum, n)
                for e in range(2):
                    m = pool.tensor_tensor(rb[:, :, :, e * hh:(e + 1) * hh], qk[:, :, :, (1 - e) * hh:(2 - e) * hh],
                                           rotl[:, l, t, 1, :, e * hh:(e + 1) * hh].unsqueeze(2).broadcast_to([P, 2, H, hh]),
                                           ALU.mult)
                m.then_inc(f_rb, 1)
                pool.wait_ge(f_rb, n + 1)
                pool.wait_ge(f_ra, n + 1)
                pool.tensor_tensor(ra[:, n % 2, :, :, :], ra[:, n % 2, :, :, :], rb[:, :, :, :], ALU.add).then_inc(f_rsum, 1)

            def norms(n):
                pool.wait_ge(f_ss, n + 1)
                if n >= 3:
                    pool.wait_ge(a_p, 2 * (n - 2))
                pool.tensor_tensor(rinv[:, n % 3, H:2 * H], ss[:, H:2 * H], minus_half[:, 0:H], ALU.pow).then_inc(f_rk, 1)
                pool.wait_ge(f_rsum, n + 1)
                pool.wait_ge(f_rk, n + 1)
                pool.tensor_tensor(ra[:, n % 2, 1, :, :], ra[:, n % 2, 1, :, :],
                                   rinv[:, n % 3, H:2 * H].unsqueeze(2).broadcast_to([P, H, HD]), ALU.mult).then_inc(f_kn, 1)
                pool.tensor_tensor(rinv[:, n % 3, 0:H], ss[:, 0:H], minus_half[:, 0:H], ALU.pow).then_inc(f_rinv, 1)

            def left_half(k):
                l, g = divmod(k, NG_F)
                pool.wait_ge(a_y1, (k + 1) * GT)
                if k:
                    pool.wait_ge(m_hn, k)
                pool.tensor_copy(h2[:, :, 0:HD], y1[l][:, g * GT:(g + 1) * GT, 0:HD]).then_inc(m_left, 1)

            def group_powers(k):
                pool.wait_ge(m_var, k + 1)
                pool.tensor_tensor(frs[:, :], fve[:, :], minus_half[:, 0:GT], ALU.pow).then_inc(m_rs, 1)

            for n in range(-2, LAST_STEP):
                if is_unit(n + 1):
                    norms(n + 1)
                if group_from(n, 1) is not None:
                    group_powers(group_from(n, 1))
                if is_unit(n + 2):
                    rotate(n + 2)
                if n in (1, 4):
                    scale_table(1, n // 4)
                if n == 2:
                    powers(3, norm_parts[3])
                if group_from(n, 0) is not None:
                    left_half(group_from(n, 0))

        @block.vector
        def _(dve):
            links = [0]

            def link(ins):
                links[0] += 1
                ins.then_inc(dve_link, 1)
                dve.wait_ge(dve_link, links[0])

            def channel_sums(ts):
                for t in ts:
                    m = dve.bn_stats(stats[:, t, :], x_sb[:, t, :])
                return m

            def norm_stats(i, sums=True):
                ts = range(NT)[norm_parts[i]]
                if sums:
                    link(channel_sums(ts))
                for t in ts:
                    m = dve.bn_aggr(mv[:, t, :], stats[:, t, :])
                link(m)
                dve.tensor_scalar(rstd[:, norm_parts[i], :], mv[:, norm_parts[i], 1:2], EPS, None, ALU.add)\
                   .then_inc(var_ready, 1)

            def normalise(i, ts=None):
                dve.wait_ge(rstd_ready, i + 1)
                for t in range(NT)[norm_parts[i]] if ts is None else ts:
                    m = dve.tensor_scalar(y_sb[0][:, t, :], x_sb[:, t, :], mv[:, t, 0:1], rstd[:, t, 0:1],
                                          ALU.subtract, ALU.mult)
                return m

            def context_low(i):
                c0, w = 512 * i, min(512, NKEYS - 512 * i)
                dve.wait_ge(ct_high, i + 1)
                dve.tensor_tensor(keyT[:, 1, c0:c0 + w], psum[:, 4 + i % 4, 0:w], keyT[:, 0, c0:c0 + w].bitcast(F32),
                                  ALU.subtract).then_inc(ct_low, 1)

            def query_low(b):
                cols = slice(b * 512, (b + 1) * 512)
                dve.wait_ge(q_high, b + 1)
                dve.scalar_tensor_tensor(qh[:, 1, cols], psum[:, q_bank[b], :], bqk, qh[:, 0, cols].bitcast(F32),
                                         ALU.add, ALU.subtract).then_inc(q_low, 1)

            dve.wait_ge(ld_x, 16)
            norm_stats(0)
            norm_stats(1)
            normalise(0).then_inc(xn_ready, 1)
            dve.wait_ge(ld_b, 32)
            dve.tensor_copy(bvr[:, :], bvc[:, 0:1].broadcast_to([P, P])).then_inc(bvr_ready, 1)
            context_low(0)
            normalise(1).then_inc(xn_ready, 1)
            dve.wait_ge(pre_act, 2)
            dve.tensor_tensor(bob[:, :], psum[:, 1, D:2 * D], bob[:, :], ALU.add).then_inc(bias_made, 1)
            context_low(1)
            query_low(0)

            def move_scores(u, j, c):
                h = u % HALVES
                k = (u * 2 + j) * CH + c
                c0, wa, wb = chunks[h][c]
                S = Sh[h]
                dve.wait_ge(scores_ready, k + 1)
                if u == 1:
                    dve.wait_ge(vl_ready, LOADS)
                if u >= HALVES:
                    dve.wait_ge(ring_done, at["T", u - HALVES, NG - 1] + 1)
                if wa == wb:
                    dve.tensor_scalar(S[:, j, c0:c0 + 2 * wa].rearrange("p (a b) -> p a b", a=2),
                                      psum[:, 2 * (k % 2):2 * (k % 2) + 2, 0:wa], SCALE, None, ALU.mult, ALU.max,
                                      accum_out=cmax[:, u, j, c:c + 1]).then_inc(scores_moved, 1)
                    dve.wait_ge(scores_moved, k + 1)
                else:
                    link(dve.tensor_scalar(S[:, j, c0:c0 + wa], psum[:, 2 * (k % 2), 0:wa], SCALE, None, ALU.mult,
                                           ALU.max, accum_out=cmax[:, u, j, c:c + 1]))
                    dve.tensor_scalar(S[:, j, c0 + wa:c0 + wa + wb], psum[:, 2 * (k % 2) + 1, 0:wb], SCALE,
                                      cmax[:, u, j, c:c + 1], ALU.mult, ALU.max,
                                      accum_out=cmax[:, u, j, c:c + 1]).then_inc(scores_moved, 1)
                    dve.wait_ge(scores_moved, k + 1)
                if c == CH - 1:
                    link(dve.tensor_reduce(nmax[:, u, j:j + 1], cmax[:, u, j, :], AX_X, ALU.max))
                    dve.tensor_scalar(nmax[:, u, j:j + 1], nmax[:, u, j:j + 1], -1.0, None, ALU.mult).then_inc(max_ready, 1)

            def low(u, g):
                i = at["T", u, g]
                k = u * NG + g
                dve.wait_ge(high_ready, k + 1)
                tiles = group(u % HALVES, g)
                if all(r == P for _, r, _ in tiles):
                    w = len(tiles)
                    dve.tensor_tensor(turned[:, k % RING, 0:w, 1, :],
                                      psum[:, 4 + i % 2, 0:256 * w].rearrange("p (a b) -> p a b", b=256),
                                      turned[:, k % RING, 0:w, 0, :].bitcast(F32), ALU.subtract).then_inc(ring_done, 1)
                else:
                    for s, (_, r, _) in enumerate(tiles):
                        m = dve.tensor_tensor(turned[0:r, k % RING, s, 1, :], psum[0:r, 4 + i % 2, 256 * s:256 * (s + 1)],
                                              turned[0:r, k % RING, s, 0, :].bitcast(F32), ALU.subtract)
                    m.then_inc(ring_done, 1)

            def acc_a(u):
                dve.wait_ge(accb_ready, u + 1)
                if u:
                    dve.wait_ge(ring_ready, at["O", u - 1, 0] + 1)
                link(dve.tensor_tensor(uT[:, :], psum[:, 6, 0:256], accb[:, :], ALU.add))
                dve.tensor_tensor(uT[:, :], psum[:, 6, 256:512], uT[:, :], ALU.add).then_inc(acc_read, 1)

            def move_output(u):
                if u < UNITS - 1:
                    dve.wait_ge(ring_ready, at["O", u, 0] + 1)
                    bank, moved = 4 + at["O", u, 0] % 2, ring_done
                else:
                    dve.wait_ge(last_made, 1)
                    bank, moved = 6, last_read
                dve.tensor_copy(oh[:, u % HALVES, :, :],
                                psum[:, bank, 0:256].rearrange("p (j d) -> p j d", d=D)).then_inc(moved, 1)
                dve.wait_ge(moved, at["O", u, 0] + 1 if u < UNITS - 1 else 1)

            def merge_in(p):
                u0, u1 = HALVES * p, HALVES * p + 1
                if p:
                    dve.wait_ge(alpha_ready, p)
                link(dve.tensor_tensor(mmin[:, :], nmax[:, u0, :], nmax[:, u1, :], ALU.min))
                for h, u in ((0, u0), (1, u1)):
                    m = dve.tensor_tensor(al[:, h, :], mmin[:, :], nmax[:, u, :], ALU.subtract)
                m.then_inc(alpha_in, 1)

            def merge_weights(p):
                u0, u1 = HALVES * p, HALVES * p + 1
                dve.wait_ge(alpha_ready, p + 1)
                for h, u in ((0, u0), (1, u1)):
                    dve.wait_ge(prob_ready, exp_at[u, 1, CH - 1] + 1)
                    m = dve.tensor_reduce(zs[:, h, :], zpart[:, u, :, :], AX_X, ALU.add)
                link(m)
                link(dve.tensor_tensor(zs[:, :, :], zs[:, :, :], al[:, :, :], ALU.mult))
                link(dve.tensor_tensor(zt[:, :], zs[:, 0, :], zs[:, 1, :], ALU.add))
                link(dve.reciprocal(zt[:, :], zt[:, :]))
                for j in range(2):
                    m = dve.tensor_scalar(al[:, :, j], al[:, :, j], zt[:, j:j + 1], None, ALU.mult)
                link(m)

            def merge(p, h):
                for j in range(2):
                    m = dve.scalar_tensor_tensor(x_sb[:, 2 * p + j, :], oh[:, h, j, :], al[:, h, j:j + 1],
                                                 x_sb[:, 2 * p + j, :], ALU.mult, ALU.add)
                link(m)

            hh = HD // 2

            def h_turn(n):
                l, t = place(n)
                dve.wait_ge(f_yT, n + 1)
                c = WIN + t * P
                dve.tensor_copy(hT[l][0:HD, c:c + P], psum[0:HD, front_bank("yT", n), 0:P])
                dve.tensor_copy(hT[l][HD:D, c + 1:c + 1 + P], psum[HD:D, front_bank("yT", n), 0:P]).then_inc(f_hT, 1)

            def qk_turned(n):
                l, t = place(n)
                dve.wait_ge(f_qT, n + 1)
                if n >= 2:
                    dve.wait_ge(a_s, 2 * (n - 1))
                dve.tensor_copy(qTh[:, n % 2, :, :], psum[:, front_bank("qT", n), :].rearrange("p (a t) -> p a t", t=P))\
                   .then_inc(f_qT_moved, 1)
                dve.wait_ge(f_kT, n + 1)
                if n >= NT:
                    dve.wait_ge(a_s, 2 * min(n - NT + 2, NT))
                c = WIN + t * P
                dve.tensor_copy(kTh[:, :, c:c + P], psum[:, front_bank("kT", n), :].rearrange("p (a t) -> p a t", t=P))\
                   .then_inc(f_kT_moved, 1)

            def rotate(n):
                l, t = place(n)
                if t == 0:
                    dve.wait_ge(rot_ready, 2 * (l + 1))
                dve.wait_ge(f_q_moved, n + 1)
                dve.wait_ge(f_k_moved, n + 1)
                if n >= 2:
                    dve.wait_ge(f_qT, n - 1)
                    dve.wait_ge(f_kT, n - 1)
                dve.tensor_tensor(ra[:, n % 2, :, :, :], qk[:, :, :, :],
                                  rotl[:, l, t, 0, :, :].unsqueeze(2).broadcast_to([P, 2, H, HD]), ALU.mult).then_inc(f_ra, 1)

            def square_sums(n):
                dve.wait_ge(f_sq, n + 1)
                if n:
                    dve.wait_ge(f_rinv, n)
                link(dve.tensor_reduce(ss[:, :], sq[:, :, :], AX_X, ALU.add))
                dve.tensor_scalar(ss[:, :], ss[:, :], 1e-24, None, ALU.max).then_inc(f_ss, 1)

            def maxima(n, hg):
                i = 2 * n + hg
                dve.wait_ge(a_s, i + 1)
                q = H // 2
                if i >= 4:
                    dve.wait_ge(a_p, i - 3)
                link(dve.tensor_reduce(mx[:, hg * q:(hg + 1) * q].rearrange("p (e b) -> p b e", b=2),
                                       psum[:, 2 + 2 * hg:4 + 2 * hg, 0:2 * (WIN + P)].rearrange("p a (h k) -> p a h k", h=2),
                                       AX_X, ALU.max))
                dve.wait_ge(f_rinv, n + 1)
                dve.scalar_tensor_tensor(nb[:, n % 2, hg * q:(hg + 1) * q], mx[:, hg * q:(hg + 1) * q], -1.0,
                                         rinv[:, n % 3, hg * q:(hg + 1) * q], ALU.mult, ALU.mult).then_inc(a_nb, 1)
                dve.wait_ge(a_nb, i + 1)

            def turned_b(n, hg):
                l, t = place(n)
                if t:
                    dve.wait_ge(a_tb, moved_b(2 * n + hg))
                    if n >= 2:
                        dve.wait_ge(a_o, 2 * (n - 1) + hg + 1)
                    dve.tensor_copy(ptB[:, hg, :, :], psum[0:WIN, 3 + 2 * hg, 0:H // 2 * WIN].rearrange("p (a t) -> p a t", t=WIN))\
                       .then_inc(a_tB, 1)

            def p_norm(n, hg):
                q = H // 2
                heads = slice(hg * q, (hg + 1) * q)
                dve.wait_ge(a_p, 2 * n + hg + 1)
                link(dve.reciprocal(rz[:, heads], z[:, n % 2, heads]))
                for e in range(q):
                    m = dve.tensor_scalar(prob[:, hg, e, :], prob[:, hg, e, :], rz[:, hg * q + e:hg * q + e + 1], None,
                                          ALU.mult)
                m.then_inc(a_pn, 1)

            def add_att(n):
                l, t = place(n)
                dve.wait_ge(a_wo, n + 1)
                dve.tensor_tensor(y1[l][:, t, :], psum[:, 6, 0:D], y_sb[l][:, t, :], ALU.add).then_inc(a_y1, 1)

            def group_stats(k):
                dve.wait_ge(m_h2, k + 1)
                dve.wait_ge(m_left, k + 1)
                if k:
                    dve.wait_ge(m_rs, k)
                for s in range(GT):
                    m = dve.bn_stats(fstats[:, s, :], h2[:, s, :])
                link(m)
                for s in range(GT):
                    m = dve.bn_aggr(fmv[:, s, :], fstats[:, s, :])
                link(m)
                dve.tensor_scalar(fve[:, :], fmv[:, :, 1], EPS, None, ALU.add).then_inc(m_var, 1)

            def group_norm(k):
                dve.wait_ge(m_rs, k + 1)
                if k:
                    dve.wait_ge(m_hT, k)
                for s in range(GT):
                    m = dve.tensor_scalar(hn[:, s, :], h2[:, s, :], fmv[:, s, 0:1], frs[:, s:s + 1],
                                          ALU.subtract, ALU.mult)
                m.then_inc(m_hn, 1)
                dve.wait_ge(m_hn, k + 1)

            def gated(k):
                l = k // NG_F
                if k:
                    dve.wait_ge(m_w2, k)
                for b, (c0, w) in enumerate(blk):
                    dve.wait_ge(m_gelu, k * NBLK + b + 1)
                    dve.wait_ge(m_w1, 2 * NBLK * k + 2 * b + 2)
                    dve.scalar_tensor_tensor(mid[0:w, b, :], psum[0:w, 7, :],
                                             b1c[0:w, l, 0, b:b + 1], gl[0:w, b, :], ALU.add, ALU.mult).then_inc(m_mid, 1)

            def add_feed(k):
                l, g = divmod(k, NG_F)
                ts = slice(g * GT, (g + 1) * GT)
                fed = psum[:, front_bank("w2", k), :].rearrange("p (s d) -> p s d", d=D)
                dve.wait_ge(m_w2, k + 1)
                if l + 1 < DEPTH:
                    dve.tensor_tensor(y_sb[l + 1][:, ts, :], fed, y1[l][:, ts, :], ALU.add).then_inc(m_y, 1)
                else:
                    dve.tensor_tensor(last[:, :, :], fed, y1[l][:, ts, :], ALU.add).then_inc(m_y, 1)
                    dve.wait_ge(m_y, k + 1)
                    dve.tensor_tensor(x_sb[:, ts, :], x_sb[:, ts, :], last[:, :, :], ALU.add).then_inc(x_out, 1)
                    dve.wait_ge(x_out, g + 1)

            for k in range(2 * CH):
                for i in range(parts_at[k], parts_at[k + 1]):
                    context_low(i)
                move_scores(0, *divmod(k, CH))
            for i in range(parts_at[-1], N_CT):
                context_low(i)
            for u in range(UNITS):
                for g in range(NG):
                    low(u, g)
                    if u == 0 and g == 0:
                        query_low(1)
                    if u == 0 and g == 9:
                        link(dve.tensor_tensor(x_sb[:, :, :], x_sb[:, :, :],
                                               bob[:, :].unsqueeze(1).broadcast_to([P, NT, D]), ALU.add))
                    if u and g == 3:
                        move_output(u - 1)
                        if merges_at(u) is not None:
                            merge_in(merges_at(u))
                    if merges_at(u) is not None and u < UNITS - 1:
                        if g == 8:
                            merge_weights(merges_at(u))
                        if g in (9, 10):
                            merge(merges_at(u), g - 9)
                    if g in SC_STEP and u + 1 < UNITS:
                        move_scores(u + 1, *divmod(SC_STEP[g], CH))
                    if u == UNITS - 2:
                        if g in (7, 11):
                            link(channel_sums(range(0, 3) if g == 7 else range(3, NT - 2)))
                        if g == 12:
                            norm_stats(2, sums=False)
                    if u == UNITS - 1:
                        if g == 0:
                            link(dve.memset(hT[0][:, 0:WIN + 1], 0.0))
                        if g == 1:
                            dve.memset(kTh[:, :, 0:WIN], 0.0).then_inc(ends_set, 1)
                        if g < PAIRS - 1:
                            normalise(2, (2 * g, 2 * g + 1)).then_inc(y0_ready, 1)
                        if g == 2:
                            h_turn(0)
                        if g == 5:
                            h_turn(1)
                        if g == 6:
                            rotate(0)
                        if g == 8:
                            square_sums(0)
                        if g == 10:
                            merge_weights(PAIRS - 1)
                        if g == 11:
                            rotate(1)
                        if g == 12:
                            qk_turned(0)
                acc_a(u)
            for n in range(0, LAST_STEP):
                feed = group_from(n, 2) is not None
                if is_unit(n - 1):
                    p_norm(n - 1, 1)
                if is_unit(n + 2) and not feed:
                    h_turn(n + 2)
                if n == 0:
                    dve.memset(w2_sb[HID_PAD:P, :, NBLK - 1, :], 0.0).then_inc(pads_set, 1)
                if is_unit(n):
                    maxima(n, 0)
                if is_unit(n - 1):
                    turned_b(n - 1, 1)
                if is_unit(n + 1):
                    square_sums(n + 1)
                if is_unit(n) and feed:
                    maxima(n, 1)
                if feed:
                    gated(group_from(n, 2))
                    add_feed(group_from(n, 2))
                if group_from(n, 1) is not None:
                    group_stats(group_from(n, 1))
                if is_unit(n):
                    p_norm(n, 0)
                if is_unit(n + 1) and feed:
                    qk_turned(n + 1)
                if is_unit(n + 2) and feed:
                    h_turn(n + 2)
                if n == 3:
                    normalise(3).then_inc(y0_ready, 1)
                if is_unit(n + 2) and not feed:
                    rotate(n + 2)
                if is_unit(n) and not feed:
                    maxima(n, 1)
                if is_unit(n):
                    turned_b(n, 0)
                if is_unit(n + 1) and not feed:
                    qk_turned(n + 1)
                if is_unit(n - 1):
                    add_att(n - 1)
                if group_from(n, 1) is not None:
                    group_norm(group_from(n, 1))
                if is_unit(n + 2) and feed:
                    rotate(n + 2)
                if n == 4:
                    link(dve.memset(hT[1][:, 0:WIN + 1], 0.0))
                    link(dve.memset(mid[HID_PAD:P, NBLK - 1, :], 0.0))
                    link(dve.memset(mid[B2_ROW:B2_ROW + 1, NBLK - 1, :], 1.0))
                if n == 0:
                    move_output(UNITS - 1)
                    merge(PAIRS - 1, 0)
                if n == 1:
                    merge(PAIRS - 1, 1)
                if n == 2:
                    norm_stats(3)



_INS = ['x', 'ctx_1024', 'L0_xattn_Wk', 'L0_xattn_Wv', 'L0_xattn_bv', 'L0_xattn_Wq', 'L0_xattn_bq', 'L0_xattn_Wo',
        'L0_xattn_bo', 'L0_ffn_wqkv', 'L0_ffn_q_scale', 'L0_ffn_k_scale', 'L0_ffn_wo', 'L0_ffn_ln_g', 'L0_ffn_ln_b',
        'L0_ffn_w1', 'L0_ffn_b1', 'L0_ffn_w2', 'L0_ffn_b2']
_OUTS = [((1, 1024, 128), 'float32')]


def kernel(**inputs):
    import numpy as _np
    import concourse.bacc as _bacc
    from concourse import mybir as _mybir
    from concourse.bass_utils import run_bass_kernel_spmd as _run

    nc = _bacc.Bacc("TRN2", target_bir_lowering=False, num_devices=1)
    arrays, args = {}, []
    given = {name: _np.ascontiguousarray(inputs[name]) for name in _INS}
    rot, mask, mats = shape_constants(1024, 64, 64)
    given.update(rot_tab=rot, mask_tab=mask, mats=mats)
    for name, a in given.items():
        arrays[f"in_{name}_dram"] = a
        args.append(nc.dram_tensor(f"in_{name}_dram", a.shape, _mybir.dt.from_np(a.dtype), kind="ExternalInput").ap())
    for i, (shape, dtype) in enumerate(_OUTS):
        dt = _mybir.dt.from_np(_np.dtype(dtype))
        args.append(nc.dram_tensor(f"out_{i}_dram", shape, dt, kind="ExternalOutput").ap())
    xattn_ffn_kernel(nc, *args)
    r = _run(nc, [arrays], core_ids=[0])
    got = tuple(r.results[0][f"out_{i}_dram"] for i in range(len(_OUTS)))
    return got[0]
```
